# Optimizing a Trainium2 kernel written in Bass

```python
import numpy as np
import jax
import jax.numpy as jnp

def _softmax(x, axis=-1):
    return jax.nn.softmax(x, axis=axis)

def _gelu(x):
    return jax.nn.gelu(x, approximate=True)

def _silu(x):
    return jax.nn.silu(x)

def _sigmoid(x):
    return jax.nn.sigmoid(x)

def _layernorm(x, axis=-1, eps=1e-05):
    m = jnp.mean(x, axis=axis, keepdims=True)
    v = jnp.var(x, axis=axis, keepdims=True)
    return (x - m) / jnp.sqrt(v + eps)

def _scatter_add(tgt, idx, src, axis=0):
    return tgt.at[idx].add(src)

def _segment_sum(src, seg, n):
    return jax.ops.segment_sum(src, seg, n)
kernel_name = 'mk_gnn_ffn_d2_gnn_r32_df9896'

def setup_inputs(seed: int=0):
    np.random.seed(seed)
    _w = jnp.asarray

    def _rec_inputs():
        import jax
        import jax.numpy as jnp
        _gk = jax.random.key(seed)
        x = -0.0002117 + 1 * jax.random.normal(jax.random.fold_in(_gk, 1), (3125, 256), jnp.float32)
        src = jax.random.randint(jax.random.fold_in(_gk, 2), (50000,), 0, 3125, jnp.int32)
        dst = jax.random.randint(jax.random.fold_in(_gk, 3), (50000,), 0, 3125, jnp.int32)
        _o = jnp.argsort(dst, stable=True)
        src = src[_o]
        dst = dst[_o]
        edge_weight = jax.random.uniform(jax.random.fold_in(_gk, 12), (50000,), jnp.float32, 0.0, 1)
        return (x, src, dst, edge_weight)
    x, src, dst, edge_weight = _rec_inputs()

    def _L0_gnn_setup():
        import jax, jax.numpy as jnp
        import numpy as np
        N_NODES = 3125
        N_EDGES = 50000
        IN_F = 256
        HID = 256
        OUT_F = 256
        BN_EPS = 1e-05

        def make_quaternion_mul(kernel):
            dim = kernel.shape[1] // 4
            r, i, j, k = jnp.split(kernel, 4, axis=1)
            r2 = jnp.concatenate([r, -i, -j, -k], axis=0)
            i2 = jnp.concatenate([i, r, -k, j], axis=0)
            j2 = jnp.concatenate([j, k, r, -i], axis=0)
            k2 = jnp.concatenate([k, -j, i, r], axis=0)
            return jnp.concatenate([r2, i2, j2, k2], axis=1)
        key = jax.random.key(seed)
        ks = jax.random.split(key, 6)
        x = jax.random.normal(ks[0], (N_NODES, IN_F), dtype=jnp.float32)
        rows = jax.random.randint(ks[1], (N_EDGES,), 0, N_NODES, dtype=jnp.int32)
        cols = jax.random.randint(ks[2], (N_EDGES,), 0, N_NODES, dtype=jnp.int32)
        edge_vals = jax.random.uniform(ks[3], (N_EDGES,), dtype=jnp.float32)
        stdv1 = np.sqrt(6.0 / (IN_F // 4 + HID))
        weight1 = jax.random.uniform(ks[4], (IN_F // 4, HID), dtype=jnp.float32, minval=-stdv1, maxval=stdv1)
        stdv2 = np.sqrt(6.0 / (HID // 4 + OUT_F))
        weight2 = jax.random.uniform(ks[5], (HID // 4, OUT_F), dtype=jnp.float32, minval=-stdv2, maxval=stdv2)
        gamma = jnp.ones((HID,), dtype=jnp.float32)
        beta = jnp.zeros((HID,), dtype=jnp.float32)
        return {'x': x, 'rows': rows, 'cols': cols, 'edge_vals': edge_vals, 'weight1': weight1, 'weight2': weight2, 'gamma': gamma, 'beta': beta}
    _L0_gnn_all = _L0_gnn_setup()
    _L0_gnn_in = {k: v for k, v in _L0_gnn_all.items() if k in ('weight1', 'weight2', 'gamma', 'beta')}
    del _L0_gnn_all

    def _L0_ffn_setup():
        import jax, jax.numpy as jnp
        import numpy as np
        B, N, D = (16, 128, 256)
        NUM_EXPERTS, TOP_K, HEADS = (4, 2, 4)
        N_EDGES = 32768
        LN_EPS = 1e-05

        def _layernorm(x, g, b):
            mu = x.mean(-1, keepdims=True)
            var = ((x - mu) ** 2).mean(-1, keepdims=True)
            return (x - mu) * jax.lax.rsqrt(var + LN_EPS) * g + b

        def _forward(x, edge_index, W_gat, att_src, att_dst, b_gat, ln_gamma, ln_beta, W1, b1, W2, b2):
            Bc, Nc, Dc = x.shape
            M = Bc * Nc
            x_flat = x.reshape(M, Dc)
            h = (x_flat @ W_gat).reshape(M, HEADS, NUM_EXPERTS)
            loops = jnp.arange(M, dtype=edge_index.dtype)
            src = jnp.concatenate([edge_index[0], loops])
            dst = jnp.concatenate([edge_index[1], loops])
            a_src = (h * att_src).sum(-1)
            a_dst = (h * att_dst).sum(-1)
            e = jax.nn.leaky_relu(a_src[src] + a_dst[dst], negative_slope=0.2)
            e_max = jax.ops.segment_max(e, dst, num_segments=M)
            ee = jnp.exp(e - e_max[dst])
            denom = jax.ops.segment_sum(ee, dst, num_segments=M)
            alpha = ee / (denom[dst] + 1e-16)
            msg = h[src] * alpha[:, :, None]
            agg = jax.ops.segment_sum(msg, dst, num_segments=M).reshape(M, HEADS * NUM_EXPERTS) + b_gat
            scores = _layernorm(agg, ln_gamma, ln_beta).reshape(M, HEADS, NUM_EXPERTS).mean(1)
            scores = scores.reshape(Bc, Nc, NUM_EXPERTS)
            topk_s, topk_i = jax.lax.top_k(scores, TOP_K)
            w = jax.nn.softmax(topk_s, axis=-1)
            out = jnp.zeros_like(x)
            for ei in range(NUM_EXPERTS):
                g = jnp.where(topk_i == ei, w, 0.0).sum(-1)
                hh = jax.nn.gelu(x @ W1[ei] + b1[ei], approximate=False)
                out = out + g[..., None] * (hh @ W2[ei] + b2[ei])
            return out
        key = jax.random.key(seed)
        ks = jax.random.split(key, 8)
        s = 0.05
        return {'x': jax.random.normal(ks[0], (B, N, D), jnp.float32), 'W_gat': jax.random.normal(ks[1], (D, HEADS * NUM_EXPERTS), jnp.float32) * s, 'att_src': jax.random.normal(ks[2], (HEADS, NUM_EXPERTS), jnp.float32) * s, 'att_dst': jax.random.normal(ks[3], (HEADS, NUM_EXPERTS), jnp.float32) * s, 'b_gat': jnp.zeros((HEADS * NUM_EXPERTS,), jnp.float32), 'ln_gamma': jnp.ones((HEADS * NUM_EXPERTS,), jnp.float32), 'ln_beta': jnp.zeros((HEADS * NUM_EXPERTS,), jnp.float32), 'W1': jax.random.normal(ks[4], (NUM_EXPERTS, D, 2 * D), jnp.float32) * s, 'b1': jnp.zeros((NUM_EXPERTS, 2 * D), jnp.float32), 'W2': jax.random.normal(ks[5], (NUM_EXPERTS, 2 * D, D), jnp.float32) * s, 'b2': jnp.zeros((NUM_EXPERTS, D), jnp.float32), 'edge_index': jax.random.randint(ks[6], (2, N_EDGES), 0, B * N, jnp.int32)}
    _L0_ffn_all = _L0_ffn_setup()
    _L0_ffn_in = {k: v for k, v in _L0_ffn_all.items() if k in ('W_gat', 'att_src', 'att_dst', 'b_gat', 'ln_gamma', 'ln_beta', 'W1', 'b1', 'W2', 'b2', 'edge_index')}
    del _L0_ffn_all

    def _L1_gnn_setup():
        import jax, jax.numpy as jnp
        import numpy as np
        N = 50000
        E = 25000
        DIM = 256
        H = 8
        DH = DIM // H
        SCALE = DH ** (-0.5)
        key = jax.random.key(seed)
        ks = jax.random.split(key, 7)
        h = jax.random.normal(ks[0], (N, DIM), dtype=jnp.float32)
        src = jax.random.randint(ks[1], (E,), 0, N, dtype=jnp.int32)
        dst = jax.random.randint(ks[2], (E,), 0, N, dtype=jnp.int32)
        W_qkv = jax.random.normal(ks[3], (DIM, 3 * DIM), dtype=jnp.float32) * DIM ** (-0.5)
        b_qkv = jnp.zeros((3 * DIM,), dtype=jnp.float32)
        W_out = jax.random.normal(ks[4], (DIM, DIM), dtype=jnp.float32) * DIM ** (-0.5)
        b_out = jnp.zeros((DIM,), dtype=jnp.float32)
        return {'h': h, 'src': src, 'dst': dst, 'W_qkv': W_qkv, 'b_qkv': b_qkv, 'W_out': W_out, 'b_out': b_out}
    _L1_gnn_all = _L1_gnn_setup()
    _L1_gnn_in = {k: v for k, v in _L1_gnn_all.items() if k in ('W_qkv', 'b_qkv', 'W_out', 'b_out')}
    del _L1_gnn_all

    def _L1_ffn_setup():
        import jax, jax.numpy as jnp
        import numpy as np
        B, S, H, F, E, K = (8, 128, 256, 512, 16, 2)
        EPS = 1e-05
        key = jax.random.key(seed)
        ks = jax.random.split(key, 9)
        sc = 0.02
        return {'x': jax.random.normal(ks[0], (B, S, H), dtype=jnp.float32), 'gate_w': jax.random.normal(ks[1], (H, E), dtype=jnp.float32) * sc, 'gate_b': jnp.zeros((E,), dtype=jnp.float32), 'w1': jax.random.normal(ks[2], (E, H, F), dtype=jnp.float32) * sc, 'b1': jnp.zeros((E, F), dtype=jnp.float32), 'w2': jax.random.normal(ks[3], (E, F, H), dtype=jnp.float32) * sc, 'b2': jnp.zeros((E, H), dtype=jnp.float32), 'gamma': jnp.ones((H,), dtype=jnp.float32), 'beta': jnp.zeros((H,), dtype=jnp.float32)}
    _L1_ffn_all = _L1_ffn_setup()
    _L1_ffn_in = {k: v for k, v in _L1_ffn_all.items() if k in ('gate_w', 'gate_b', 'w1', 'b1', 'w2', 'b2', 'gamma', 'beta')}
    del _L1_ffn_all
    return {'x': x, 'src': src, 'dst': dst, 'edge_weight': edge_weight, 'L0_gnn_weight1': _L0_gnn_in['weight1'], 'L0_gnn_weight2': _L0_gnn_in['weight2'], 'L0_gnn_gamma': _L0_gnn_in['gamma'], 'L0_gnn_beta': _L0_gnn_in['beta'], 'L0_ffn_W_gat': _L0_ffn_in['W_gat'], 'L0_ffn_att_src': _L0_ffn_in['att_src'], 'L0_ffn_att_dst': _L0_ffn_in['att_dst'], 'L0_ffn_b_gat': _L0_ffn_in['b_gat'], 'L0_ffn_ln_gamma': _L0_ffn_in['ln_gamma'], 'L0_ffn_ln_beta': _L0_ffn_in['ln_beta'], 'L0_ffn_W1': _L0_ffn_in['W1'], 'L0_ffn_b1': _L0_ffn_in['b1'], 'L0_ffn_W2': _L0_ffn_in['W2'], 'L0_ffn_b2': _L0_ffn_in['b2'], 'L0_ffn_edge_index': _L0_ffn_in['edge_index'], 'L1_gnn_W_qkv': _L1_gnn_in['W_qkv'], 'L1_gnn_b_qkv': _L1_gnn_in['b_qkv'], 'L1_gnn_W_out': _L1_gnn_in['W_out'], 'L1_gnn_b_out': _L1_gnn_in['b_out'], 'L1_ffn_gate_w': _L1_ffn_in['gate_w'], 'L1_ffn_gate_b': _L1_ffn_in['gate_b'], 'L1_ffn_w1': _L1_ffn_in['w1'], 'L1_ffn_b1': _L1_ffn_in['b1'], 'L1_ffn_w2': _L1_ffn_in['w2'], 'L1_ffn_b2': _L1_ffn_in['b2'], 'L1_ffn_gamma': _L1_ffn_in['gamma'], 'L1_ffn_beta': _L1_ffn_in['beta']}

def reference(x, src, dst, edge_weight, L0_gnn_weight1, L0_gnn_weight2, L0_gnn_gamma, L0_gnn_beta, L0_ffn_W_gat, L0_ffn_att_src, L0_ffn_att_dst, L0_ffn_b_gat, L0_ffn_ln_gamma, L0_ffn_ln_beta, L0_ffn_W1, L0_ffn_b1, L0_ffn_W2, L0_ffn_b2, L0_ffn_edge_index, L1_gnn_W_qkv, L1_gnn_b_qkv, L1_gnn_W_out, L1_gnn_b_out, L1_ffn_gate_w, L1_ffn_gate_b, L1_ffn_w1, L1_ffn_b1, L1_ffn_w2, L1_ffn_b2, L1_ffn_gamma, L1_ffn_beta):
    import jax
    import jax.numpy as jnp

    def _L0_gnn_ref(x, rows, cols, edge_vals, weight1, weight2, gamma, beta):
        import jax, jax.numpy as jnp
        import numpy as np
        N_NODES = 3125
        N_EDGES = 50000
        IN_F = 256
        HID = 256
        OUT_F = 256
        BN_EPS = 1e-05

        def make_quaternion_mul(kernel):
            dim = kernel.shape[1] // 4
            r, i, j, k = jnp.split(kernel, 4, axis=1)
            r2 = jnp.concatenate([r, -i, -j, -k], axis=0)
            i2 = jnp.concatenate([i, r, -k, j], axis=0)
            j2 = jnp.concatenate([j, k, r, -i], axis=0)
            k2 = jnp.concatenate([k, -j, i, r], axis=0)
            return jnp.concatenate([r2, i2, j2, k2], axis=1)
        hamilton1 = make_quaternion_mul(weight1)
        hamilton2 = make_quaternion_mul(weight2)
        gathered = edge_vals[:, None] * x[cols]
        new_x = jax.ops.segment_sum(gathered, rows, num_segments=N_NODES)
        out1 = new_x @ hamilton1
        mean = jnp.mean(out1, axis=0)
        var = jnp.mean(jnp.square(out1 - mean), axis=0)
        out1 = (out1 - mean) * jax.lax.rsqrt(var + BN_EPS) * gamma + beta
        out1 = jnp.tanh(out1)
        return out1 @ hamilton2

    def _L0_ffn_ref(x, W_gat, att_src, att_dst, b_gat, ln_gamma, ln_beta, W1, b1, W2, b2, edge_index):
        import jax, jax.numpy as jnp
        import numpy as np
        B, N, D = (16, 128, 256)
        NUM_EXPERTS, TOP_K, HEADS = (4, 2, 4)
        N_EDGES = 32768
        LN_EPS = 1e-05

        def _layernorm(x, g, b):
            mu = x.mean(-1, keepdims=True)
            var = ((x - mu) ** 2).mean(-1, keepdims=True)
            return (x - mu) * jax.lax.rsqrt(var + LN_EPS) * g + b

        def _forward(x, edge_index, W_gat, att_src, att_dst, b_gat, ln_gamma, ln_beta, W1, b1, W2, b2):
            Bc, Nc, Dc = x.shape
            M = Bc * Nc
            x_flat = x.reshape(M, Dc)
            h = (x_flat @ W_gat).reshape(M, HEADS, NUM_EXPERTS)
            loops = jnp.arange(M, dtype=edge_index.dtype)
            src = jnp.concatenate([edge_index[0], loops])
            dst = jnp.concatenate([edge_index[1], loops])
            a_src = (h * att_src).sum(-1)
            a_dst = (h * att_dst).sum(-1)
            e = jax.nn.leaky_relu(a_src[src] + a_dst[dst], negative_slope=0.2)
            e_max = jax.ops.segment_max(e, dst, num_segments=M)
            ee = jnp.exp(e - e_max[dst])
            denom = jax.ops.segment_sum(ee, dst, num_segments=M)
            alpha = ee / (denom[dst] + 1e-16)
            msg = h[src] * alpha[:, :, None]
            agg = jax.ops.segment_sum(msg, dst, num_segments=M).reshape(M, HEADS * NUM_EXPERTS) + b_gat
            scores = _layernorm(agg, ln_gamma, ln_beta).reshape(M, HEADS, NUM_EXPERTS).mean(1)
            scores = scores.reshape(Bc, Nc, NUM_EXPERTS)
            topk_s, topk_i = jax.lax.top_k(scores, TOP_K)
            w = jax.nn.softmax(topk_s, axis=-1)
            out = jnp.zeros_like(x)
            for ei in range(NUM_EXPERTS):
                g = jnp.where(topk_i == ei, w, 0.0).sum(-1)
                hh = jax.nn.gelu(x @ W1[ei] + b1[ei], approximate=False)
                out = out + g[..., None] * (hh @ W2[ei] + b2[ei])
            return out
        return _forward(x, edge_index, W_gat, att_src, att_dst, b_gat, ln_gamma, ln_beta, W1, b1, W2, b2)

    def _L1_gnn_ref(h, src, dst, W_qkv, b_qkv, W_out, b_out):
        import jax, jax.numpy as jnp
        import numpy as np
        N = 50000
        E = 25000
        DIM = 256
        H = 8
        DH = DIM // H
        SCALE = DH ** (-0.5)
        n = h.shape[0]
        qkv = (h @ W_qkv + b_qkv).reshape(n, 3, H, DH)
        q, k, v = (qkv[:, 0], qkv[:, 1], qkv[:, 2])
        score = jnp.einsum('ehd,ehd->eh', q[dst], k[src]) * SCALE
        mx = jax.ops.segment_max(score, dst, num_segments=n)
        ex = jnp.exp(score - mx[dst])
        denom = jax.ops.segment_sum(ex, dst, num_segments=n)
        attn = ex / denom[dst]
        msg = attn[:, :, None] * v[src]
        h_new = jax.ops.segment_sum(msg, dst, num_segments=n)
        h_out = jnp.transpose(h_new, (0, 2, 1)).reshape(n, DIM)
        return (h_out + h) @ W_out + b_out

    def _L1_ffn_ref(x, gate_w, gate_b, w1, b1, w2, b2, gamma, beta):
        import jax, jax.numpy as jnp
        import numpy as np
        B, S, H, F, E, K = (8, 128, 256, 512, 16, 2)
        EPS = 1e-05
        gate_logits = x @ gate_w + gate_b
        topk_vals, topk_idx = jax.lax.top_k(gate_logits, K)
        topk_w = jax.nn.softmax(topk_vals, axis=-1)
        h = jax.nn.relu(jnp.einsum('bsh,ehf->bsef', x, w1) + b1)
        expert_out = jnp.einsum('bsef,efh->bseh', h, w2) + b2
        sel = jnp.take_along_axis(expert_out, topk_idx[:, :, :, None], axis=2)
        moe = jnp.sum(topk_w[..., None] * sel, axis=2)
        y = x + moe
        mu = jnp.mean(y, axis=-1, keepdims=True)
        var = jnp.var(y, axis=-1, keepdims=True)
        return (y - mu) / jnp.sqrt(var + EPS) * gamma + beta
    x = x + _L0_gnn_ref(_layernorm(x, axis=-1), src, dst, edge_weight, L0_gnn_weight1, L0_gnn_weight2, L0_gnn_gamma, L0_gnn_beta)
    x = x + _L0_ffn_ref(_layernorm(x, axis=-1)[None], L0_ffn_W_gat, L0_ffn_att_src, L0_ffn_att_dst, L0_ffn_b_gat, L0_ffn_ln_gamma, L0_ffn_ln_beta, L0_ffn_W1, L0_ffn_b1, L0_ffn_W2, L0_ffn_b2, L0_ffn_edge_index)[0]
    x = x + _L1_gnn_ref(_layernorm(x, axis=-1), src, dst, L1_gnn_W_qkv, L1_gnn_b_qkv, L1_gnn_W_out, L1_gnn_b_out)
    x = x + _L1_ffn_ref(_layernorm(x, axis=-1)[None], L1_ffn_gate_w, L1_ffn_gate_b, L1_ffn_w1, L1_ffn_b1, L1_ffn_w2, L1_ffn_b2, L1_ffn_gamma, L1_ffn_beta)[0]
    return x

_drawn_inputs = setup_inputs


def setup_inputs(seed=0):
    import zlib

    import numpy as np

    out = dict(_drawn_inputs(seed))
    spreads = {'L0_gnn_gamma': (1.0, 0.2),
     'L0_gnn_beta': (0.0, 0.1),
     'L0_ffn_b_gat': (0.0, 0.1),
     'L0_ffn_ln_gamma': (1.0, 0.2),
     'L0_ffn_ln_beta': (0.0, 0.1),
     'L0_ffn_b1': (0.0, 0.1),
     'L0_ffn_b2': (0.0, 0.1),
     'L1_gnn_b_qkv': (0.0, 0.1),
     'L1_gnn_b_out': (0.0, 0.1),
     'L1_ffn_gate_b': (0.0, 0.347),
     'L1_ffn_b1': (0.0, 0.8),
     'L1_ffn_b2': (0.0, 0.301),
     'L1_ffn_gamma': (1.0, 0.2),
     'L1_ffn_beta': (0.0, 0.1)}
    factors = {}
    for name, (base, spread) in spreads.items():
        noise = np.random.default_rng([zlib.crc32(name.encode()), seed]).standard_normal(out[name].shape)
        drawn = base * np.exp(spread * noise) if base else spread * noise
        out[name] = jnp.asarray(drawn.astype(out[name].dtype))
    for name, factor in factors.items():
        out[name] = (out[name] * factor).astype(out[name].dtype)
    return out
```

```python
from contextlib import ExitStack

import concourse.bass as bass
from concourse import mybir

F32 = mybir.dt.float32
BF16 = mybir.dt.bfloat16
I32 = mybir.dt.int32
ALU = mybir.AluOpType
ACT = mybir.ActivationFunctionType
AX = mybir.AxisListType.X

P = 128
N = 3125
D = 256
NT = -(-N // P)
NP = NT * P
TAIL_ROWS = N - (NT - 1) * P
GT = 5
NG = NT // GT
assert NG * GT == NT
LN_EPS = 1e-5
BIG = 1e30

NH = 32
E1 = 50000
J1 = 14
NJ1 = 392
NB1 = NJ1 // J1
FULL1 = E1 // NJ1
REST1 = E1 - FULL1 * NJ1
E2 = 32768
J2 = 16
NJ2 = E2 // P
NB2 = NJ2 // J2
PAD_DST = NH * P - 1
assert NB1 * J1 == NJ1 and NB1 % 2 == 0 and NB2 * J2 == NJ2 and NB2 % 2 == 0
LAST_PHASE = 99


class Count:

    def __init__(self, eng, sem):
        self.eng, self.sem, self.base, self.n, self.start = eng, sem, 0, 0, 0

    def inc(self, ins):
        ins.then_inc(self.sem, 1)
        self.n += 1

    def wait(self):
        if not (isinstance(self.base, int) and self.base + self.n == 0):
            self.eng.wait_ge(self.sem, self.base + self.n)

    def seq(self, ins):
        self.inc(ins)
        self.wait()

    def at(self, i, per):
        if isinstance(i, int) and i == 0:
            self.start = self.base + self.n
        self.base, self.n, self.per = self.start + i * per, 0, per

    def end(self, trips):
        assert self.n == self.per, f"passes count {self.n}, said {self.per}"
        self.base, self.n = self.start + trips * self.per, 0


def loop(eng, trips, body):
    body(0)
    if trips > 1:
        with eng.Fori(1, trips) as i:
            body(i)


def zero(i):
    return isinstance(i, int) and i == 0


def row(tile, t):
    return tile[:, bass.ds(t, 1), :].rearrange("p a d -> p (a d)")


def table_rows(tab):
    return tab.rearrange("(t p) f -> p t f", p=P)


def bass_gnn_moe_kernel(nc, x, src, dst, edge_weight, g0_w1, g0_w2, g0_gamma, g0_beta, f0_wgat,
                        f0_att_src, f0_att_dst, f0_bgat, f0_lng, f0_lnb, f0_w1, f0_b1, f0_w2, f0_b2,
                        f0_edges, g1_wqkv, g1_bqkv, g1_wout, g1_bout, f1_gw, f1_gb, f1_w1, f1_b1,
                        f1_w2, f1_b2, f1_gamma, f1_beta, out):
    top = ExitStack()
    v, a = nc.vector, nc.scalar
    count = [0]

    def dram(name, shape, dt=F32):
        return nc.dram_tensor(name, shape, dt, kind="Internal").ap()

    def phase():
        ctx = ExitStack()
        count[0] += 1
        tag = f"_{count[0]}"
        own_sems = []

        def close():
            nc.clear_and_free_semaphores(own_sems)
            nc.all_engine_barrier()
        ctx.callback(close)

        def sb(name, shape, dt=F32):
            return ctx.enter_context(nc.sbuf_tensor(name + tag, shape, dt))

        def ps(name, shape, dt=F32):
            return ctx.enter_context(nc.psum_tensor(name + tag, shape, dt))

        def sem(name):
            own_sems.append(nc.alloc_semaphore(name=name + tag))
            return own_sems[-1]
        return ctx, sb, ps, sem

    def keep_sb(ctx, name, shape, dt=F32):
        return ctx.enter_context(nc.sbuf_tensor(name, shape, dt))

    ticks = {}

    def hold(eng, sem, value):
        if isinstance(value, int):
            eng.wait_ge(sem, value)
        else:
            name = str(eng.engine)
            if name not in ticks:
                ticks[name] = top.enter_context(nc.semaphore("tick_" + name.split(".")[-1]))
            eng.wait_ge(sem, value)
            eng.sem_inc(ticks[name], 1)

    with top:
        X = keep_sb(top, "X", [P, NT, D])
        ident = keep_sb(top, "ident", [P, P])
        ones = keep_sb(top, "ones", [P, P])
        iota_free = keep_sb(top, "iota_free", [P, P])
        iota_part = keep_sb(top, "iota_part", [P, 1])
        upper = keep_sb(top, "upper", [P, P])
        below = keep_sb(top, "below", [P, P])
        eps_col = keep_sb(top, "eps_col", [P, 1])
        src1 = keep_sb(top, "src1", [P, NJ1], I32)
        dst1 = keep_sb(top, "dst1", [P, NJ1], I32)
        keep1 = keep_sb(top, "keep1", [P, NJ1])
        pen1 = keep_sb(top, "pen1", [P, NJ1])
        cont1 = keep_sb(top, "cont1", [P, 1])
        end1 = keep_sb(top, "end1", [P, NT], I32)
        nbr0 = keep_sb(top, "nbr0", [P, NJ1], I32)
        keep0 = keep_sb(top, "keep0", [P, NJ1])
        cont0 = keep_sb(top, "cont0", [P, 1])
        end0 = keep_sb(top, "end0", [P, NT], I32)
        w0 = keep_sb(top, "w0", [P, NJ1])
        src2 = keep_sb(top, "src2", [P, NJ2], I32)
        dst2 = keep_sb(top, "dst2", [P, NJ2], I32)
        keep2 = keep_sb(top, "keep2", [P, NJ2])
        pen2 = keep_sb(top, "pen2", [P, NJ2])
        cont2 = keep_sb(top, "cont2", [P, 1])
        end2 = keep_sb(top, "end2", [P, NT], I32)

        xn_tab = dram("xn_tab", [NP, D])
        sum_tab = dram("sum_tab", [P * NJ1 + 1, D])
        by_src_tab = dram("by_src_tab", [P * NJ1, 3], I32)
        by_dst_tab = dram("by_dst_tab", [P * NJ2, 2], I32)
        key_tab = [dram("key_tab0", [P * NJ1]), dram("key_tab1", [P * NJ2])]
        h_tab = dram("h_tab", [NP, 24])
        gat_tab = dram("gat_tab", [E2 + 1, 24])
        q_tab = dram("q_tab", [NP, D])
        kv_tab = dram("kv_tab", [NP, 2 * D])
        att_tab = dram("att_tab", [P * NJ1 + 1, 16 + D])

        def start_phase():
            ctx, sb, ps, sem = phase()
            with ctx:
                ii = sb("ii", [P, P], I32)
                ip = sb("ip", [P, 1], I32)
                iotas, made, cleared, x_in = sem("iotas"), sem("made"), sem("cleared"), sem("x_in")
                with nc.Block() as block:
                    @block.gpsimd
                    def _(pool):
                        nc.gpsimd.iota(ii[:, :], pattern=[[1, P]], base=0, channel_multiplier=0).then_inc(iotas, 1)
                        nc.gpsimd.iota(ip[:, :], pattern=[[0, 1]], base=0, channel_multiplier=1).then_inc(iotas, 1)

                    @block.sync
                    def _(sp):
                        sp.dma_start(X[:, 0:NT - 1, :], table_rows(x[0:(NT - 1) * P, :])).then_inc(x_in, 16)
                        sp.wait_ge(cleared, 1)
                        sp.dma_start(X[0:TAIL_ROWS, NT - 1, :], x[(NT - 1) * P:N, :]).then_inc(x_in, 16)
                        sp.wait_ge(x_in, 32)

                    @block.vector
                    def _(dve):
                        c = Count(dve, made)
                        v.memset(X[:, NT - 1, :], 0.0).then_inc(cleared, 1)
                        c.inc(v.memset(ones[:, :], 1.0))
                        c.inc(v.memset(eps_col[:, :], LN_EPS))
                        dve.wait_ge(iotas, 2)
                        c.inc(v.tensor_copy(iota_free[:, :], ii[:, :]))
                        c.seq(v.tensor_copy(iota_part[:, :], ip[:, :]))
                        for tile, op in ((ident, ALU.is_equal), (upper, ALU.is_ge), (below, ALU.is_lt)):
                            c.seq(v.tensor_scalar(tile[:, :], iota_free[:, :], iota_part[:, :], None, op))

        def norm_phase(table=None, rows_keep=None, cols_keep=None, project=None):
            ctx, sb, ps, sem = phase()
            with ctx:
                turn = cols_keep is not None or project is not None
                st, mv = sb("st", [P, GT, 6]), sb("mv", [P, GT, 2])
                sd, rs = sb("sd", [P, GT]), sb("rs", [P, GT])
                xn = sb("xn", [P, GT, D])
                stats, rooted, chain, normed = sem("stats"), sem("rooted"), sem("chain"), sem("normed")
                stored, copied, group_free = sem("stored"), sem("copied"), sem("group_free")
                if turn:
                    turned, columns = sem("turned"), sem("columns")
                    psT = ps("psT", [P, 2, 512])
                    xt = sb("xt", [P, 2, GT, P])
                to_tables = False
                if project:
                    w_dram, PN, bias, sink = project
                    w_in, projected, evacuated, p_stored = sem("w_in"), sem("projected"), sem("evacuated"), sem("p_stored")
                    wp = sb("wp", [P, 2, PN])
                    psP = ps("psP", [P, 2, 512 * -(-PN // 512)])
                    bb = sb("bb", [P, PN])
                    to_tables = isinstance(sink, list)
                    if to_tables:
                        pr = sb("pr", [P, GT, PN])
                    cuts = [(0, PN, 0)] if PN <= 512 else [(0, 256, 0), (256, PN, 512)]
                    n_w = 16 * (1 + (bias is not None))
                n_keep = (rows_keep is not None) + (cols_keep is not None)
                with nc.Block() as block:
                    @block.sync
                    def _(sp):
                        if project:
                            sp.dma_start(wp[:, :, :], w_dram.rearrange("(k p) n -> p k n", p=P)).then_inc(w_in, 16)
                            if bias is not None:
                                sp.dma_start(bb[:, :], bias.partition_broadcast(P)).then_inc(w_in, 16)
                        with sp.Fori(0, NG) as g:
                            if table is not None:
                                sp.wait_ge(normed, (g + 1) * GT)
                                sp.dma_start(table_rows(table)[:, bass.ds(g * GT, GT), :], xn[:, :, :]).then_inc(stored, 16)
                            if to_tables:
                                hold(sp, evacuated, (g + 1) * GT)
                                for tab, a0, w in sink:
                                    sp.dma_start(table_rows(tab)[:, bass.ds(g * GT, GT), :], pr[:, :, a0:a0 + w]).then_inc(p_stored, 16)
                        if table is not None:
                            sp.wait_ge(stored, 16 * NG)
                        if to_tables:
                            sp.wait_ge(p_stored, 16 * NG * len(sink))

                    @block.vector
                    def _(dve):
                        c = Count(dve, chain)

                        def group(g):
                            c.at(g, 2 * GT + 1)
                            for s in range(GT):
                                c.inc(v.bn_stats(st[:, s, :], row(X, g * GT + s)))
                            hold(dve, chain, c.base + c.n)
                            for s in range(GT):
                                c.inc(v.bn_aggr(mv[:, s, :], st[:, s, :]))
                            hold(dve, chain, c.base + c.n)
                            dve.sem_inc(stats, 1)
                            hold(dve, rooted, g + 1)
                            c.inc(v.reciprocal(rs[:, :], sd[:, :]))
                            hold(dve, chain, c.base + c.n)
                            if not zero(g):
                                hold(dve, group_free, g)
                            for s in range(GT):
                                v.tensor_scalar(xn[:, s, :], row(X, g * GT + s), mv[:, s, 0:1], rs[:, s:s + 1],
                                                ALU.subtract, ALU.mult).then_inc(normed, 1)
                            if project:
                                for s in range(GT):
                                    hold(dve, projected, g * GT + s + 1)
                                    for a0, a1, spot in cuts:
                                        o = pr[:, s, a0:a1] if to_tables else row(sink, g * GT + s)[:, a0:a1]
                                        i0 = psP[:, s % 2, spot:spot + a1 - a0]
                                        ins = v.tensor_tensor(o, i0, bb[:, a0:a1], ALU.add) if bias is not None else v.tensor_copy(o, i0)
                                    ins.then_inc(evacuated, 1)
                        if project:
                            dve.wait_ge(w_in, n_w)
                        loop(dve, NG, group)

                    @block.scalar
                    def _(act):
                        with act.Fori(0, NG) as g:
                            hold(act, stats, g + 1)
                            a.activation(sd[:, :], mv[:, :, 1], ACT.Sqrt, bias=eps_col[:, :]).then_inc(rooted, 1)
                            if turn:
                                for s in range(GT):
                                    hold(act, turned, g * GT + s + 1)
                                    a.copy(xt[:, :, s, :], psT[:, s % 2, 0:D].rearrange("p (k c) -> p k c", k=2)).then_inc(columns, 1)

                    @block.tensor
                    def _(pe):
                        if project:
                            pe.wait_ge(w_in, n_w)

                        def group(g):
                                for s in range(GT):
                                    hold(pe, normed, g * GT + s + 1)
                                    if not zero(g) or s >= 2:
                                        hold(pe, columns, g * GT + max(s - 1, 0))
                                    nc.tensor.transpose(psT[:, s % 2, 0:P], xn[:, s, 0:P], ident[:, :])
                                    nc.tensor.transpose(psT[:, s % 2, P:D], xn[:, s, P:D], ident[:, :]).then_inc(turned, 1)
                                if project:
                                    for s in range(GT):
                                        hold(pe, columns, g * GT + s + 1)
                                        if not zero(g) or s >= 2:
                                            hold(pe, evacuated, g * GT + max(s - 1, 0))
                                        for a0, a1, spot in cuts:
                                            for k in range(2):
                                                ins = nc.tensor.matmul(psP[:, s % 2, spot:spot + a1 - a0], xt[:, k, s, :],
                                                                       wp[:, k, a0:a1], start=(k == 0), stop=(k == 1))
                                        ins.then_inc(projected, 1)
                        if turn:
                            loop(pe, NG, group)

                    @block.gpsimd
                    def _(pool):
                        with pool.Fori(0, NG) as g:
                            hold(pool, normed, (g + 1) * GT)
                            if rows_keep is not None:
                                nc.gpsimd.tensor_copy(rows_keep[:, bass.ds(g * GT, GT), :], xn[:, :, :]).then_inc(copied, 1)
                            if turn:
                                hold(pool, columns, (g + 1) * GT)
                            if cols_keep is not None:
                                nc.gpsimd.tensor_copy(cols_keep[:, bass.ds(g, 1), :, :].rearrange("p a k c -> p (a k c)"),
                                                      xt[:, :, :, :].rearrange("p k s c -> p (k s c)")).then_inc(copied, 1)
                            if table is not None:
                                hold(pool, stored, 16 * (g + 1))
                            if project:
                                hold(pool, evacuated, (g + 1) * GT)
                            if to_tables:
                                hold(pool, p_stored, 16 * len(sink) * (g + 1))
                            if n_keep:
                                hold(pool, copied, n_keep * (g + 1))
                            pool.sem_inc(group_free, 1)

        def count_block(lo, hi, columns, J, counts):
            ctx, sb, ps, sem = phase()
            with ctx:
                onelo, onehi = sb("onelo", [P, 2, J, P], BF16), sb("onehi", [P, 2, J, NH], BF16)
                zerob = sb("zerob", [P, P], BF16)
                psC = ps("psC", [P, NH])
                built, used, counted, chain = sem("built"), sem("used"), sem("counted"), sem("chain")
                trips = columns // J // 2
                with nc.Block() as block:
                    @block.vector
                    def _(dve):
                        v.memset(zerob[:, :], 0.0).then_inc(chain, 1)
                        dve.wait_ge(chain, 1)

                        def body(i):
                            for s in range(2):
                                cols = bass.ds((i * 2 + s) * J, J)
                                if not zero(i):
                                    hold(dve, used, (i - 1) * 2 + s + 1)
                                v.tensor_tensor(onelo[:, s, :, :], iota_free[:, :].unsqueeze(1).broadcast_to([P, J, P]),
                                                lo[:, cols].unsqueeze(2).broadcast_to([P, J, P]), ALU.is_equal)
                                v.tensor_tensor(onehi[:, s, :, :], iota_free[:, 0:NH].unsqueeze(1).broadcast_to([P, J, NH]),
                                                hi[:, cols].unsqueeze(2).broadcast_to([P, J, NH]), ALU.is_equal).then_inc(built, 1)
                        loop(dve, trips, body)
                        dve.wait_ge(counted, 1)
                        v.tensor_copy(counts[:, :], psC[:, :]).then_inc(chain, 1)
                        dve.wait_ge(chain, 2)

                    @block.tensor
                    def _(pe):
                        pe.wait_ge(chain, 1)
                        nc.tensor.matmul(psC[:, :], zerob[:, :], zerob[:, 0:NH], start=True, stop=False)
                        with pe.Fori(0, trips) as i:
                            for s in range(2):
                                hold(pe, built, i * 2 + s + 1)
                                for j in range(J):
                                    ins = nc.tensor.matmul(psC[:, :], onelo[:, s, j, :], onehi[:, s, j, :], start=False, stop=False)
                                ins.then_inc(used, 1)
                        nc.tensor.matmul(psC[:, :], zerob[:, :], zerob[:, 0:NH], start=False, stop=True).then_inc(counted, 1)

        def prefix_block(counts, first, end, endrow, none_row):
            ctx, sb, ps, sem = phase()
            with ctx:
                psI, psT = ps("psI", [P, 512]), ps("psTot", [P, 512])
                tot, scan, t1 = sb("tot", [P, NH]), sb("scan", [P, NH]), sb("t1", [P, NH])
                summed, chain = sem("summed"), sem("chain")
                with nc.Block() as block:
                    @block.tensor
                    def _(pe):
                        nc.tensor.matmul(psI[:, 0:NH], upper[:, :], counts[:, :], start=True, stop=True)
                        nc.tensor.matmul(psT[:, 0:NH], ones[:, :], counts[:, :], start=True, stop=True).then_inc(summed, 1)

                    @block.vector
                    def _(dve):
                        c = Count(dve, chain)
                        dve.wait_ge(summed, 1)
                        c.seq(v.tensor_copy(tot[:, :], psT[:, 0:NH]))
                        c.seq(v.tensor_tensor_scan(scan[:, :], ones[:, 0:NH], tot[:, :], 0.0, ALU.mult, ALU.add))
                        c.seq(v.tensor_tensor(scan[:, :], scan[:, :], tot[:, :], ALU.subtract))
                        c.seq(v.tensor_tensor(end[:, :], scan[:, :], psI[:, 0:NH], ALU.add))
                        c.seq(v.tensor_tensor(first[:, :], end[:, :], counts[:, :], ALU.subtract))
                        c.seq(v.tensor_scalar(t1[:, :], counts[:, :], 0.5, None, ALU.is_ge))
                        c.seq(v.scalar_tensor_tensor(scan[:, :], end[:, :], -1.0 - none_row, t1[:, :], ALU.add, ALU.mult))
                        c.seq(v.tensor_scalar(endrow[:, :], scan[:, 0:NT], float(none_row), None, ALU.add))

        def run_flags(dve, c, dstf, nextf, NJ, keep, pen, cont, tmp):
            c.seq(v.memset(keep[:, 0:1], 0.0))
            c.seq(v.tensor_tensor(keep[:, 1:NJ], dstf[:, 1:NJ], dstf[:, 0:NJ - 1], ALU.is_equal))
            c.seq(v.tensor_scalar(pen[:, :], keep[:, :], 1.0, BIG, ALU.subtract, ALU.mult))
            c.seq(v.tensor_tensor(tmp[:, 0:1], dstf[:, NJ - 1:NJ], nextf[:, :], ALU.is_equal))
            c.seq(v.scalar_tensor_tensor(cont[:, :], dstf[:, NJ - 1:NJ], 1.0, tmp[:, 0:1], ALU.add, ALU.mult))
            c.seq(v.tensor_scalar(cont[:, :], cont[:, :], 1.0, None, ALU.subtract))

        def graph_phase():
            ctx, sb, ps, sem = phase()
            with ctx:
                dstf, nexti, nextf = sb("dstf", [P, NJ1]), sb("nexti", [P, 1], I32), sb("nextf", [P, 1])
                loi, lo, hi, tmp = sb("loi", [P, NJ1], I32), sb("lo", [P, NJ1]), sb("hi", [P, NJ1]), sb("tmp", [P, 1])
                counts, first, end = sb("counts", [P, NH]), sb("first", [P, NH]), sb("end", [P, NH])
                cleared, e_in, chain = sem("cleared"), sem("e_in"), sem("chain")
                with nc.Block() as block:
                    @block.sync
                    def _(sp):
                        sp.wait_ge(cleared, 1)
                        for tile, dr in ((src1, src), (dst1, dst)):
                            sp.dma_start(tile[0:FULL1, :], dr[0:FULL1 * NJ1].rearrange("(p j) -> p j", j=NJ1)).then_inc(e_in, 16)
                            sp.dma_start(tile[FULL1:FULL1 + 1, 0:REST1], dr[FULL1 * NJ1:E1].unsqueeze(0)).then_inc(e_in, 16)
                        sp.dma_start(nexti[0:FULL1, :], dst.rearrange("(e o) -> e o", o=1)[NJ1:(FULL1 * NJ1 + 1):NJ1, :], allow_slow_non_contiguous=True).then_inc(e_in, 16)

                    @block.vector
                    def _(dve):
                        c = Count(dve, chain)
                        c.inc(v.memset(src1[:, :], 0))
                        c.inc(v.memset(dst1[:, :], PAD_DST))
                        c.seq(v.memset(nexti[:, :], PAD_DST))
                        dve.sem_inc(cleared, 1)
                        dve.wait_ge(e_in, 16 * 5)
                        c.inc(v.tensor_copy(dstf[:, :], dst1[:, :]))
                        c.seq(v.tensor_copy(nextf[:, :], nexti[:, :]))
                        run_flags(dve, c, dstf, nextf, NJ1, keep1, pen1, cont1, tmp)
                        c.seq(v.tensor_single_scalar(loi[:, :], dst1[:, :], P - 1, ALU.bitwise_and))
                        c.seq(v.tensor_copy(lo[:, :], loi[:, :]))
                        c.seq(v.tensor_single_scalar(loi[:, :], dst1[:, :], 7, ALU.logical_shift_right))
                        c.seq(v.tensor_copy(hi[:, :], loi[:, :]))
                        c.seq(v.tensor_scalar(dstf[:, :], dstf[:, :], float(N - 1), None, ALU.min))
                        c.seq(v.tensor_copy(dst1[:, :], dstf[:, :]))
                count_block(lo, hi, NJ1, J1, counts)
                prefix_block(counts, first, end, end1, P * NJ1)

        def sort_phase(E, T, J, key_dram, payloads, keys_dram, table, endrow, none_row):
            W = 1 + len(payloads)
            outer, osb, _, osem = phase()
            with outer:
                B = -(-T // P)
                TB = T // B
                assert TB * B == T
                full, rest = E // P, E % P
                key, pay = osb("key", [P, T]), osb("pay", [P, T, W])
                loi = osb("loi", [P, T], I32)
                lo, hi = osb("lo", [P, T + J]), osb("hi", [P, T + J])
                counts, first, end = osb("counts", [P, NH]), osb("first", [P, NH]), osb("end", [P, NH])

                def load_block():
                    ctx, sb, ps, sem = phase()
                    with ctx:
                        raw = [sb(f"raw{n}", [P, B, P], I32) for n in range(W)]
                        rawf = [sb(f"rawf{n}", [P, B, P]) for n in range(W)]
                        psT = ps("psT", [P, 2, 512])
                        cleared, r_in, floats, turned, copied, k_out = (sem(n) for n in ("cleared", "r_in", "floats", "turned", "copied", "k_out"))
                        n_in, drained = [0], sem("drained")
                        with nc.Block() as block:
                            @block.sync
                            def _(sp):
                                if full < T:
                                    sp.wait_ge(cleared, 1)
                                for n, dr in enumerate([key_dram] + payloads):
                                    for b in range(B):
                                        whole = min(TB, full - b * TB)
                                        o = raw[n] if dr.dtype == I32 else raw[n][:, :, :].bitcast(F32)
                                        sp.dma_start(o[0:whole, b, :], dr[b * TB * P:(b * TB + whole) * P].rearrange("(t e) -> t e", e=P)).then_inc(r_in, 16)
                                        n_in[0] += 16
                                    if rest:
                                        sp.dma_start(o[full % TB:full % TB + 1, full // TB, 0:rest], dr[full * P:E].unsqueeze(0)).then_inc(r_in, 16)
                                        n_in[0] += 16
                                sp.wait_ge(floats, 1)
                                sp.dma_start(keys_dram.rearrange("(b t e) -> t b e", t=TB, e=P), rawf[0][0:TB, :, :]).then_inc(k_out, 16)
                                sp.wait_ge(k_out, 16)

                            @block.vector
                            def _(dve):
                                c = Count(dve, copied)
                                if full < T:
                                    c.inc(v.memset(raw[0][:, :, :], PAD_DST))
                                    for n in range(1, W):
                                        c.inc(v.memset(raw[n][:, :, :], 0))
                                    c.wait()
                                    dve.sem_inc(cleared, 1)
                                dve.wait_ge(r_in, n_in[0])
                                for n, dr in enumerate([key_dram] + payloads):
                                    i0 = raw[n][0:TB, :, :] if dr.dtype == I32 else raw[n][:, :, :].bitcast(F32)[0:TB, :, :]
                                    c.inc(v.tensor_copy(rawf[n][0:TB, :, :], i0))
                                c.wait()
                                dve.sem_inc(floats, 1)
                                m = 0
                                for n, dr in enumerate([key_dram] + payloads):
                                    for b in range(B):
                                        m += 1
                                        dve.wait_ge(turned, m)
                                        o = pay[:, b * TB:(b + 1) * TB, n]
                                        if dr.dtype == I32:
                                            o = o.bitcast(I32)
                                        if n == 0:
                                            c.inc(v.tensor_copy(key[:, b * TB:(b + 1) * TB], psT[:, m % 2, 0:TB]))
                                        c.seq(v.tensor_copy(o, psT[:, m % 2, 0:TB]))
                                        dve.sem_inc(drained, 1)
                                keyi = pay[:, :, 0].bitcast(I32)
                                c.seq(v.tensor_single_scalar(loi[:, :], keyi, P - 1, ALU.bitwise_and))
                                c.inc(v.memset(lo[:, T:T + J], 0.0))
                                c.seq(v.tensor_copy(lo[:, 0:T], loi[:, :]))
                                c.seq(v.tensor_single_scalar(loi[:, :], keyi, 7, ALU.logical_shift_right))
                                c.inc(v.memset(hi[:, T:T + J], 0.0))
                                c.seq(v.tensor_copy(hi[:, 0:T], loi[:, :]))

                            @block.tensor
                            def _(pe):
                                pe.wait_ge(floats, 1)
                                m = 0
                                for n in range(W):
                                    for b in range(B):
                                        m += 1
                                        if m > 2:
                                            pe.wait_ge(drained, m - 2)
                                        nc.tensor.transpose(psT[:, m % 2, 0:TB], rawf[n][0:TB, b, :], ident[0:TB, 0:TB]).then_inc(turned, 1)

                def place_block():
                    ctx, sb, ps, sem = phase()
                    with ctx:
                        onelo, onehi = sb("onelo", [P, 2, J, P], BF16), sb("onehi", [P, 2, J, NH], BF16)
                        lowT = sb("lowT", [P, 2, J, P], BF16)
                        identb = sb("identb", [P, P], BF16)
                        keyS = sb("keyS", [P, 2, J])
                        kb = sb("kb", [P, 2, J, P])
                        grown, base, resets = sb("grown", [P, NH, J + 1]), sb("base", [P, NH, J + 1]), sb("resets", [P, NH, J + 1])
                        split = sb("split", [P, 2, J, 2, NH], BF16)
                        posA, posB = sb("posA", [P, 2, J]), sb("posB", [P, 2, J])
                        posS, payS = sb("posS", [P, 2, J], I32), sb("payS", [P, 2, J, W])
                        junk1, junk2 = sb("junk1", [P, J // 2, 2, NH]), sb("junk2", [P, J, P], BF16)
                        psH, psL = ps("psH", [P, 2, 512]), ps("psL", [P, 2, 512])
                        assert J * NH <= 512
                        psT = ps("psT", [P, 2, 1024], BF16)
                        kb_in = [sem("kb_in0"), sem("kb_in1")]
                        moved = [sem("moved0"), sem("moved1")]
                        built, turned, lows, splits, histed, looked, selected, placed, chain = (
                            sem(n) for n in ("built", "turned", "lows", "splits", "histed", "looked", "selected", "placed", "chain"))
                        QT = 4
                        quads = [(q, min(q + QT, J)) for q in range(0, J, QT)]
                        NQ = len(quads)
                        assert NQ % 2 == 0 and J % 2 == 0
                        trips = T // J // 2
                        with nc.Block() as block:
                            @block.sync
                            def _(sp):
                                def body(i):
                                    for s in range(2):
                                        if not zero(i):
                                            hold(sp, placed, 2 * i + s - 1)
                                        sp.dma_start(kb[:, s, :, :].rearrange("p j e -> p (j e)"),
                                                     keys_dram[bass.ds((2 * i + s) * J * P, J * P)].partition_broadcast(P)).then_inc(kb_in[s], 16)
                                loop(sp, trips, body)

                            @block.vector
                            def _(dve):
                                c = Count(dve, chain)
                                c.seq(v.tensor_copy(identb[:, :], ident[:, :]))

                                def build(m, s):
                                    cols = bass.ds(m * J, J)
                                    v.tensor_tensor(onelo[:, s, :, :], iota_free[:, :].unsqueeze(1).broadcast_to([P, J, P]),
                                                    lo[:, cols].unsqueeze(2).broadcast_to([P, J, P]), ALU.is_equal)
                                    v.tensor_tensor(onehi[:, s, :, :], iota_free[:, 0:NH].unsqueeze(1).broadcast_to([P, J, NH]),
                                                    hi[:, cols].unsqueeze(2).broadcast_to([P, J, NH]), ALU.is_equal).then_inc(built, 1)
                                c.inc(v.memset(resets[:, :, 1:J + 1], 1.0))
                                c.inc(v.memset(resets[:, :, 0:1], 0.0))
                                c.seq(v.tensor_copy(base[:, :, J], first[:, :]))
                                build(0, 0)

                                def body(i):
                                    c.at(i, 2 * 10)
                                    for s in range(2):
                                        m = 2 * i + s
                                        cols = bass.ds(m * J, J)
                                        if s or not zero(i):
                                            hold(dve, turned, m * NQ)
                                        build(m + 1, 1 - s)
                                        if not zero(i):
                                            hold(dve, moved[s], 16 * J * i)
                                        c.inc(v.tensor_copy(keyS[:, s, :], key[:, cols]))
                                        c.inc(v.tensor_copy(grown[:, :, 0], base[:, :, J]))
                                        hold(dve, histed, m + 1)
                                        c.inc(v.tensor_copy(grown[:, :, 1:J + 1], psH[:, s, 0:J * NH].rearrange("p (j h) -> p h j", h=NH)))
                                        hold(dve, chain, c.base + c.n)
                                        c.seq(v.tensor_tensor_scan(base[:, :, :].rearrange("p h j -> p (h j)"), resets[:, :, :].rearrange("p h j -> p (h j)"),
                                                                   grown[:, :, :].rearrange("p h j -> p (h j)"), 0.0, ALU.mult, ALU.add))
                                        before = base[:, :, 0:J].rearrange("p h j -> p j h")
                                        c.seq(v.tensor_copy(split[:, s, :, 0, :], before))
                                        v.tensor_tensor(split[:, s, :, 1, :], before, split[:, s, :, 0, :], ALU.subtract).then_inc(splits, 1)
                                        hold(dve, kb_in[s], 16 * (i + 1))
                                        for u in range(J):
                                            v.scalar_tensor_tensor(junk2[:, u, :], kb[:, s, u, :], keyS[:, s, u:u + 1], below[:, :],
                                                                   ALU.is_equal, ALU.mult, accum_out=posB[:, s, u:u + 1])
                                        hold(dve, looked, m + 1)
                                        for hf in range(2):
                                            js = slice(hf * (J // 2), (hf + 1) * (J // 2))
                                            ins = v.tensor_tensor(junk1[:, :, :, :], psL[:, hf, 0:J * NH].rearrange("p (u a h) -> p u a h", a=2, h=NH),
                                                                  onehi[:, s, js, :].unsqueeze(2).broadcast_to([P, J // 2, 2, NH]), ALU.mult)
                                            c.seq(ins)
                                            ins = v.tensor_reduce(posA[:, s, js], junk1[:, :, :, :].rearrange("p u a h -> p u (a h)"), AX, ALU.add)
                                            c.seq(ins)
                                        dve.sem_inc(selected, 1)
                                        c.seq(v.tensor_tensor(posA[:, s, :], posA[:, s, :], posB[:, s, :], ALU.add))
                                        v.tensor_copy(posS[:, s, :], posA[:, s, :])
                                        v.tensor_copy(payS[:, s, :, :], pay[:, cols, :]).then_inc(placed, 1)
                                        hold(dve, placed, m + 1)
                                loop(dve, trips, body)
                                c.end(trips)

                            @block.tensor
                            def _(pe):
                                pe.wait_ge(chain, 1)

                                def hist_and_turn(m, s, first_two):
                                    hold(pe, built, m + 1)
                                    for u in range(J):
                                        ins = nc.tensor.matmul(psH[:, s, u * NH:(u + 1) * NH], onelo[:, s, u, :], onehi[:, s, u, :], start=True, stop=True)
                                    ins.then_inc(histed, 1)
                                    for q, (a0, a1) in enumerate(quads):
                                        if q >= 2 or not first_two:
                                            hold(pe, lows, m * NQ + q - 1)
                                        for u in range(a0, a1):
                                            ins = nc.tensor.transpose(psT[:, q % 2, (u - a0) * P:(u - a0 + 1) * P], onelo[:, s, u, :], identb[:, :])
                                        ins.then_inc(turned, 1)
                                hist_and_turn(0, 0, True)

                                def body(i):
                                    for s in range(2):
                                        m = 2 * i + s
                                        if s or not zero(i):
                                            hold(pe, splits, m)
                                        hist_and_turn(m + 1, 1 - s, False)
                                        hold(pe, splits, m + 1)
                                        if s or not zero(i):
                                            hold(pe, selected, m)
                                        for u in range(J):
                                            hf, at = u // (J // 2), u % (J // 2)
                                            ins = nc.tensor.matmul(psL[:, hf, at * 2 * NH:(at + 1) * 2 * NH], lowT[:, s, u, :],
                                                                   split[:, s, u, :, :].rearrange("p a h -> p (a h)"), start=True, stop=True)
                                        ins.then_inc(looked, 1)
                                loop(pe, trips, body)

                            @block.scalar
                            def _(act):
                                def lower(m, s, q, a0, a1):
                                    hold(act, turned, m * NQ + q + 1)
                                    a.copy(lowT[:, s, a0:a1, :].rearrange("p u e -> p (u e)"), psT[:, q % 2, 0:(a1 - a0) * P]).then_inc(lows, 1)
                                for q, (a0, a1) in enumerate(quads):
                                    lower(0, 0, q, a0, a1)

                                def body(i):
                                    for s in range(2):
                                        m = 2 * i + s
                                        if s or not zero(i):
                                            hold(act, looked, m)
                                        for q, (a0, a1) in enumerate(quads):
                                            lower(m + 1, 1 - s, q, a0, a1)
                                loop(act, trips, body)

                            @block.gpsimd
                            def _(pool):
                                with pool.Fori(0, trips) as i:
                                    for s in range(2):
                                        hold(pool, placed, 2 * i + s + 1)
                                        for u in range(J):
                                            pool.indirect_dma_start(out=table, out_offset=bass.IndirectOffsetOnAxis(ap=posS[:, s, u:u + 1], axis=0),
                                                                    in_=payS[:, s, u, :].bitcast(I32), in_offset=None).then_inc(moved[s], 16)
                                for s in range(2):
                                    pool.wait_ge(moved[s], 16 * J * trips)
                load_block()
                count_block(lo, hi, T, J, counts)
                prefix_block(counts, first, end, endrow, none_row)
                place_block()

        def reload_phase(table, NJ, fields, keep, pen, cont):
            ctx, sb, ps, sem = phase()
            with ctx:
                W = table.shape[1]
                rows_in = sb("rows_in", [P, NJ, W], I32)
                keyf, nexti, nextf, tmp = sb("keyf", [P, NJ]), sb("nexti", [P, 1], I32), sb("nextf", [P, 1]), sb("tmp", [P, 1])
                penx = pen if pen is not None else sb("penx", [P, NJ])
                r_in, cleared, chain = sem("r_in"), sem("cleared"), sem("chain")
                with nc.Block() as block:
                    @block.sync
                    def _(sp):
                        grid = table.rearrange("(p j) w -> p j w", j=NJ)
                        sp.dma_start(rows_in[:, :, :], grid).then_inc(r_in, 16)
                        sp.wait_ge(cleared, 1)
                        sp.dma_start(nexti[0:P - 1, :], grid[1:P, 0, 0:1], allow_slow_non_contiguous=True).then_inc(r_in, 16)

                    @block.vector
                    def _(dve):
                        c = Count(dve, chain)
                        c.seq(v.memset(nexti[:, :], -2))
                        dve.sem_inc(cleared, 1)
                        dve.wait_ge(r_in, 32)
                        c.inc(v.tensor_copy(keyf[:, :], rows_in[:, :, 0]))
                        c.inc(v.tensor_copy(nextf[:, :], nexti[:, :]))
                        for n, tile in fields:
                            i0 = rows_in[:, :, n] if tile.dtype == I32 else rows_in[:, :, n].bitcast(F32)
                            c.inc(v.tensor_copy(tile[:, :], i0))
                        c.wait()
                        run_flags(dve, c, keyf, nextf, NJ, keep, penx, cont, tmp)

        def gnn0_phase():
            ctx, sb, ps, sem = phase()
            with ctx:
                G = sb("G", [P, 2, J1, D])
                wS, kS = sb("wS", [P, 2, J1]), sb("kS", [P, 2, J1])
                iS = sb("iS", [P, 2, J1], I32)
                carry = sb("carry", [P, D])
                zrow = sb("zrow", [1, D])
                got, stored = [sem("got0"), sem("got1")], [sem("stored0"), sem("stored1")]
                staged, cols, scaled, summed = sem("staged"), sem("cols"), sem("scaled"), sem("summed")
                chain, z_ready, z_stored = sem("chain"), sem("z_ready"), sem("z_stored")
                with nc.Block() as block:
                    @block.gpsimd
                    def _(pool):
                        def body(i):
                            for s in range(2):
                                if not zero(i):
                                    hold(pool, stored[s], 16 * i)
                                nc.gpsimd.tensor_copy(iS[:, s, :], nbr0[:, bass.ds((2 * i + s) * J1, J1)]).then_inc(staged, 1)
                                hold(pool, staged, 2 * i + s + 1)
                                for j in range(J1):
                                    pool.indirect_dma_start(out=G[:, s, j, :], out_offset=None, in_=xn_tab,
                                                            in_offset=bass.IndirectOffsetOnAxis(ap=iS[:, s, j:j + 1], axis=0)).then_inc(got[s], 16)
                        loop(pool, NB1 // 2, body)

                    @block.scalar
                    def _(act):
                        with act.Fori(0, NB1 // 2) as i:
                            for s in range(2):
                                hold(act, cols, 2 * i + s + 1)
                                hold(act, got[s], 16 * J1 * (i + 1))
                                for j in range(J1):
                                    a.mul(G[:, s, j, :], G[:, s, j, :], wS[:, s, j:j + 1]).then_inc(scaled, 1)

                    @block.vector
                    def _(dve):
                        c = Count(dve, chain)
                        v.memset(zrow[:, :], 0.0).then_inc(z_ready, 1)
                        c.seq(v.memset(carry[:, :], 0.0))

                        def body(i):
                            c.at(i, 2 * (J1 + 1))
                            for s in range(2):
                                b = 2 * i + s
                                sl = bass.ds(b * J1, J1)
                                if not zero(i):
                                    hold(dve, scaled, (b - 1) * J1)
                                v.tensor_copy(wS[:, s, :], w0[:, sl])
                                v.tensor_copy(kS[:, s, :], keep0[:, sl]).then_inc(cols, 1)
                                hold(dve, cols, b + 1)
                                for j in range(J1):
                                    hold(dve, scaled, b * J1 + j + 1)
                                    prev = carry[:, :] if j == 0 else G[:, s, j - 1, :]
                                    c.seq(v.scalar_tensor_tensor(G[:, s, j, :], prev, kS[:, s, j:j + 1], G[:, s, j, :], ALU.mult, ALU.add))
                                c.seq(v.tensor_copy(carry[:, :], G[:, s, J1 - 1, :]))
                                dve.sem_inc(summed, 1)
                        loop(dve, NB1 // 2, body)
                        c.end(NB1 // 2)

                    @block.sync
                    def _(sp):
                        sp.wait_ge(z_ready, 1)
                        sp.dma_start(sum_tab[P * NJ1:P * NJ1 + 1, :], zrow[:, :]).then_inc(z_stored, 16)
                        tab = sum_tab[0:P * NJ1, :].rearrange("(p j) f -> p j f", j=NJ1)
                        with sp.Fori(0, NB1 // 2) as i:
                            for s in range(2):
                                sp.wait_ge(summed, 2 * i + s + 1)
                                sp.dma_start(tab[:, bass.ds((2 * i + s) * J1, J1), :], G[:, s, :, :]).then_inc(stored[s], 16)
                        sp.wait_ge(z_stored, 16)
                        for s in range(2):
                            sp.wait_ge(stored[s], 16 * (NB1 // 2))
                gnn0_dense(carry)

        def gnn0_dense(tails):
            ctx, sb, ps, sem = phase()
            with ctx:
                own = sb("own", [P, NT, D])
                HW = NP // 8
                NXT, O1T = sb("NXT", [P, 2, NP]), sb("O1T", [P, 2, NP])
                H = [sb("H1", [P, 2, D]), sb("H2", [P, 2, D])]
                gam, bet = sb("gam", [P, 2]), sb("bet", [P, 2])
                cm, cmS, oh = sb("cm", [P, NT]), sb("cmS", [P, GT]), sb("oh", [P, GT, P])
                nx = sb("nx", [P, GT, D])
                mean, var, scl, bia, junk = (sb(n, [P, 2]) for n in ("mean", "var", "scl", "bia", "junk"))
                big = own
                psA, psT = ps("psA", [P, 2, 512]), ps("psT", [P, 2, 512])
                ps1 = ps("ps1", [P, 2, 512])
                h_in, own_in, chain, signed = sem("h_in"), sem("own_in"), sem("chain"), sem("signed")
                hots, tailed, added, turned, columns = sem("hots"), sem("tailed"), sem("added"), sem("turned"), sem("columns")
                mm1, ev1 = sem("mm1"), sem("ev1")
                a_stat, v_stat, tanhs, mm2, resid = sem("a_stat"), sem("v_stat"), sem("tanhs"), sem("mm2"), sem("resid")
                tt = sb("tt", [P, 2, GT * P])
                minus = {(1, 0), (2, 0), (3, 0), (2, 1), (3, 2), (1, 3)}
                with nc.Block() as block:
                    @block.sync
                    def _(sp):
                        for Ht, wd in zip(H, (g0_w1, g0_w2)):
                            for ra in range(4):
                                for cb in range(4):
                                    comp = ra ^ cb
                                    sp.dma_start(Ht[64 * (ra % 2):64 * (ra % 2) + 64, ra // 2, 64 * cb:64 * cb + 64],
                                                 wd[:, 64 * comp:64 * comp + 64]).then_inc(h_in, 16)
                        sp.dma_start(gam[:, :], g0_gamma.rearrange("(m p) -> p m", p=P), allow_slow_non_contiguous=True).then_inc(h_in, 16)
                        sp.dma_start(bet[:, :], g0_beta.rearrange("(m p) -> p m", p=P), allow_slow_non_contiguous=True).then_inc(h_in, 16)

                    @block.gpsimd
                    def _(pool):
                        for t in range(NT):
                            pool.indirect_dma_start(out=own[:, t, :], out_offset=None, in_=sum_tab,
                                                    in_offset=bass.IndirectOffsetOnAxis(ap=end0[:, t:t + 1], axis=0)).then_inc(own_in, 16)

                    @block.vector
                    def _(dve):
                        c = Count(dve, chain)
                        c.seq(v.tensor_scalar(cm[:, :], iota_free[:, 0:NT], -float(P), cont0[:, :], ALU.mult, ALU.add))
                        dve.wait_ge(h_in, 16 * 34)
                        for Ht in H:
                            for ra, cb in sorted(minus):
                                blk = Ht[64 * (ra % 2):64 * (ra % 2) + 64, ra // 2, 64 * cb:64 * cb + 64]
                                c.seq(v.tensor_scalar(blk, blk, -1.0, None, ALU.mult))
                        dve.sem_inc(signed, 1)
                        dve.wait_ge(own_in, 16 * NT)

                        def body(g):
                            c.at(g, 1)
                            c.inc(v.tensor_copy(cmS[:, :], cm[:, bass.ds(g * GT, GT)]))
                            hold(dve, chain, c.base + c.n)
                            if not zero(g):
                                hold(dve, tailed, g * GT)
                                hold(dve, turned, g * GT)
                            for s in range(GT):
                                v.tensor_scalar(oh[:, s, :], iota_free[:, :], cmS[:, s:s + 1], None, ALU.is_equal).then_inc(hots, 1)
                            for s in range(GT):
                                hold(dve, tailed, g * GT + s + 1)
                                v.tensor_tensor(nx[:, s, :], psA[:, s % 2, 0:D], row(own, g * GT + s), ALU.add).then_inc(added, 1)
                        loop(dve, NG, body)
                        c.end(NG)
                        dve.wait_ge(ev1, 16)
                        for m in range(2):
                            c.inc(v.tensor_reduce(junk[:, m:m + 1], O1T[:, m, 0:N], AX, ALU.add))
                        c.wait()
                        c.seq(v.tensor_scalar(mean[:, :], junk[:, :], -1.0 / N, None, ALU.mult))
                        dve.sem_inc(v_stat, 1)
                        dve.wait_ge(a_stat, 3)
                        c.seq(v.reciprocal(scl[:, :], scl[:, :]))
                        c.seq(v.tensor_tensor(scl[:, :], scl[:, :], gam[:, :], ALU.mult))
                        c.seq(v.tensor_tensor(bia[:, :], mean[:, :], scl[:, :], ALU.mult))
                        c.seq(v.tensor_tensor(bia[:, :], bia[:, :], bet[:, :], ALU.add))
                        dve.sem_inc(v_stat, 1)
                        with dve.Fori(0, NG) as g:
                            for s in range(GT):
                                hold(dve, mm2, g * GT + s + 1)
                                v.tensor_tensor(row(X, g * GT + s), psA[:, s % 2, 0:D], row(X, g * GT + s), ALU.add).then_inc(resid, 1)

                    @block.tensor
                    def _(pe):
                        def sums(g):
                            for s in range(GT):
                                hold(pe, hots, g * GT + s + 1)
                                if not zero(g) or s >= 2:
                                    hold(pe, added, g * GT + max(s - 1, 0))
                                nc.tensor.matmul(psA[:, s % 2, 0:D], oh[:, s, :], tails[:, :], start=True, stop=True).then_inc(tailed, 1)
                            for s in range(GT):
                                hold(pe, added, g * GT + s + 1)
                                if not zero(g) or s >= 2:
                                    hold(pe, columns, g * GT + max(s - 1, 0))
                                nc.tensor.transpose(psT[:, s % 2, 0:P], nx[:, s, 0:P], ident[:, :])
                                nc.tensor.transpose(psT[:, s % 2, P:D], nx[:, s, P:D], ident[:, :]).then_inc(turned, 1)
                        loop(pe, NG, sums)
                        pe.wait_ge(columns, NT)
                        pe.wait_ge(signed, 1)

                        def dense(n):
                            for m in range(2):
                                if not zero(n):
                                    hold(pe, ev1, 2 * n + m - 1)
                                for k in range(2):
                                    ins = nc.tensor.matmul(ps1[:, m, 0:HW], H[0][:, k, m * P:(m + 1) * P], NXT[:, k, bass.ds(n * HW, HW)],
                                                           start=(k == 0), stop=(k == 1))
                                ins.then_inc(mm1, 1)
                        loop(pe, 8, dense)

                        def last(g):
                            hold(pe, tanhs, g + 1)
                            for s in range(GT):
                                if not zero(g) or s >= 2:
                                    hold(pe, resid, g * GT + max(s - 1, 0))
                                for k in range(2):
                                    ins = nc.tensor.matmul(psA[:, s % 2, 0:D], tt[:, k, s * P:(s + 1) * P], H[1][:, k, :], start=(k == 0), stop=(k == 1))
                                ins.then_inc(mm2, 1)
                        loop(pe, NG, last)

                    @block.scalar
                    def _(act):
                        with act.Fori(0, NG) as g:
                            for s in range(GT):
                                hold(act, turned, g * GT + s + 1)
                                a.copy(NXT[:, :, bass.ds((g * GT + s) * P, P)], psT[:, s % 2, 0:D].rearrange("p (k c) -> p k c", k=2)).then_inc(columns, 1)
                        with act.Fori(0, 8) as n:
                            for m in range(2):
                                hold(act, mm1, 2 * n + m + 1)
                                a.copy(O1T[:, m, bass.ds(n * HW, HW)], ps1[:, m, 0:HW]).then_inc(ev1, 1)
                        act.wait_ge(v_stat, 1)
                        flat = own[:, :, :].rearrange("p t d -> p (t d)")
                        for m in range(2):
                            a.activation(flat[:, m * N:(m + 1) * N], O1T[:, m, 0:N], ACT.Square, bias=mean[:, m:m + 1],
                                         accum_out=var[:, m:m + 1]).then_inc(a_stat, 1)
                        act.wait_ge(a_stat, 2)
                        a.activation(scl[:, :], var[:, :], ACT.Sqrt, bias=eps_col[:, :], scale=1.0 / N).then_inc(a_stat, 1)
                        act.wait_ge(v_stat, 2)

                        def body(g):
                            if not zero(g):
                                hold(act, mm2, g * GT)
                            for m in range(2):
                                ins = a.activation(tt[:, m, :], O1T[:, m, bass.ds(g * GT * P, GT * P)], ACT.Tanh,
                                                   bias=bia[:, m:m + 1], scale=scl[:, m:m + 1])
                            ins.then_inc(tanhs, 1)
                        loop(act, NG, body)

        def merge_phase(H, F, tails, cont, endrow, table, agg, self_score=None, self_rows=None, eps=None):
            W, C = 2 * H + F, F // H
            CW = 2 * H + F + 1
            ctx, sb, ps, sem = phase()
            with ctx:
                own, other = sb("own", [P, NT, W]), sb("other", [P, NT, CW])
                diag, eqm, tmp = sb("diag", [P, H + 1, P]), sb("eqm", [P, P]), sb("tmp", [P, P])
                penm, ref, lead, tw = sb("penm", [P, P]), sb("ref", [P, H]), sb("lead", [P, 1]), sb("tw", [P, H])
                tw_rows = sb("tw_rows", [P, CW])
                cm, cmS, oh = sb("cm", [P, NT]), sb("cmS", [P, GT]), sb("oh", [P, GT, P])
                top_, wts, den = sb("top_", [P, NT, H]), sb("wts", [P, 3, NT, H]), sb("den", [P, NT, H])
                zrow = sb("zrow", [1, W])
                HB = -(-(H + 1) // 4)
                psB, psA = ps("psB", [P, HB, 512]), ps("psA", [P, 2, 512])
                own_in, diags, spread, targ, texp, hots, tailed, taken, warg, wexp, chain = (
                    sem(n) for n in ("own_in", "diags", "spread", "targ", "texp", "hots", "tailed", "taken", "warg", "wexp", "chain"))
                z_ready, z_stored = sem("z_ready"), sem("z_stored")
                n_self = 1 if self_score is not None else 0
                with nc.Block() as block:
                    @block.sync
                    def _(sp):
                        sp.wait_ge(z_ready, 1)
                        sp.dma_start(table[table.shape[0] - 1:table.shape[0], :], zrow[:, :]).then_inc(z_stored, 16)

                    @block.gpsimd
                    def _(pool):
                        pool.wait_ge(z_stored, 16)
                        for t in range(NT):
                            pool.indirect_dma_start(out=own[:, t, :], out_offset=None, in_=table,
                                                    in_offset=bass.IndirectOffsetOnAxis(ap=endrow[:, t:t + 1], axis=0)).then_inc(own_in, 16)

                    @block.vector
                    def _(dve):
                        c = Count(dve, chain)
                        c.seq(v.memset(zrow[:, H:W], 0.0))
                        c.seq(v.memset(zrow[:, 0:H], -BIG))
                        dve.sem_inc(z_ready, 1)
                        for h in range(H):
                            c.inc(v.tensor_scalar(diag[:, h, :], ident[:, :], tails[:, h:h + 1], None, ALU.mult))
                        c.inc(v.tensor_scalar(diag[:, H, :], ident[:, :], cont[:, :], None, ALU.mult))
                        c.inc(v.tensor_scalar(cm[:, :], iota_free[:, 0:NT], -float(P), cont[:, :], ALU.mult, ALU.add))
                        c.wait()
                        dve.sem_inc(diags, 1)
                        dve.wait_ge(spread, 1)
                        bc = lambda h: psB[:, h // 4, (h % 4) * P:(h % 4 + 1) * P]
                        c.seq(v.tensor_scalar(eqm[:, :], bc(H), cont[:, :], None, ALU.is_equal))
                        c.seq(v.tensor_scalar(penm[:, :], eqm[:, :], 1.0, BIG, ALU.subtract, ALU.mult))
                        for h in range(H):
                            c.seq(v.tensor_tensor(tmp[:, :], bc(h), penm[:, :], ALU.add))
                            c.seq(v.tensor_reduce(ref[:, h:h + 1], tmp[:, :], AX, ALU.max))
                        c.seq(v.tensor_tensor(tmp[:, :], eqm[:, :], upper[:, :], ALU.mult))
                        c.seq(v.tensor_reduce(lead[:, :], tmp[:, :], AX, ALU.add))
                        c.seq(v.tensor_scalar(lead[:, :], lead[:, :], 1.5, None, ALU.is_lt))
                        c.seq(v.tensor_tensor(tw[:, :], tails[:, 0:H], ref[:, :], ALU.subtract))
                        dve.sem_inc(targ, 1)
                        dve.wait_ge(texp, 1)
                        c.inc(v.tensor_scalar(tw_rows[:, 0:H], ref[:, :], lead[:, :], None, ALU.mult))
                        c.inc(v.tensor_copy(tw_rows[:, CW - 1:CW], lead[:, :]))
                        c.inc(v.tensor_tensor(tw_rows[:, H:2 * H], tails[:, H:2 * H], tw[:, :], ALU.mult))
                        c.seq(v.tensor_tensor(tw_rows[:, 2 * H:W].rearrange("p (h c) -> p h c", c=C), tails[:, 2 * H:W].rearrange("p (h c) -> p h c", c=C),
                                              tw[:, :].unsqueeze(2).broadcast_to([P, H, C]), ALU.mult))

                        def body(g):
                            c.at(g, 1)
                            if not zero(g):
                                hold(dve, tailed, g * GT)
                            c.inc(v.tensor_copy(cmS[:, :], cm[:, bass.ds(g * GT, GT)]))
                            hold(dve, chain, c.base + c.n)
                            for s in range(GT):
                                v.tensor_scalar(oh[:, s, :], iota_free[:, :], cmS[:, s:s + 1], None, ALU.is_equal).then_inc(hots, 1)
                            for s in range(GT):
                                hold(dve, tailed, g * GT + s + 1)
                                v.tensor_copy(row(other, g * GT + s), psA[:, s % 2, 0:CW]).then_inc(taken, 1)
                        loop(dve, NG, body)
                        c.end(NG)
                        dve.wait_ge(taken, NT)
                        dve.wait_ge(own_in, 16 * NT)
                        om, oR = own[:, :, 0:H], other[:, :, 0:H]
                        has = other[:, :, CW - 1:CW]
                        c.seq(v.tensor_scalar(has, has, 1.0, BIG, ALU.subtract, ALU.mult))
                        c.seq(v.tensor_tensor(oR, oR, has.broadcast_to([P, NT, H]), ALU.add))
                        c.seq(v.tensor_tensor(top_[:, :, :], om, oR, ALU.max))
                        if n_self:
                            c.seq(v.tensor_tensor(top_[:, :, :], top_[:, :, :], self_score, ALU.max))
                            c.inc(v.tensor_tensor(wts[:, 2, :, :], self_score, top_[:, :, :], ALU.subtract))
                        c.inc(v.tensor_tensor(wts[:, 0, :, :], om, top_[:, :, :], ALU.subtract))
                        c.seq(v.tensor_tensor(wts[:, 1, :, :], oR, top_[:, :, :], ALU.subtract))
                        dve.sem_inc(warg, 1)
                        dve.wait_ge(wexp, 1)
                        wide = lambda n: wts[:, n, :, :].unsqueeze(3).broadcast_to([P, NT, H, C])
                        heads = lambda t, a0: t[:, :, a0:a0 + F].rearrange("p t (h c) -> p t h c", c=C)
                        c.inc(v.tensor_tensor(own[:, :, H:2 * H], own[:, :, H:2 * H], wts[:, 0, :, :], ALU.mult))
                        c.seq(v.tensor_tensor(other[:, :, H:2 * H], other[:, :, H:2 * H], wts[:, 1, :, :], ALU.mult))
                        c.seq(v.tensor_tensor(den[:, :, :], own[:, :, H:2 * H], other[:, :, H:2 * H], ALU.add))
                        for t in range(NT):
                            hs = lambda tile: tile[:, t, 2 * H:2 * H + F].rearrange("p (h c) -> p h c", c=C)
                            wv = lambda n: wts[:, n, t, :].unsqueeze(2).broadcast_to([P, H, C])
                            c.inc(v.tensor_tensor(hs(own), hs(own), wv(0), ALU.mult))
                            c.inc(v.tensor_tensor(hs(other), hs(other), wv(1), ALU.mult))
                        c.wait()
                        c.seq(v.tensor_tensor(agg[:, :, :], own[:, :, 2 * H:W], other[:, :, 2 * H:W], ALU.add))
                        if n_self:
                            c.seq(v.tensor_tensor(den[:, :, :], den[:, :, :], wts[:, 2, :, :], ALU.add))
                            for t in range(NT):
                                c.inc(v.tensor_tensor(own[:, t, 2 * H:W].rearrange("p (h c) -> p h c", c=C), self_rows[:, t, 0:F].rearrange("p (h c) -> p h c", c=C),
                                                      wts[:, 2, t, :].unsqueeze(2).broadcast_to([P, H, C]), ALU.mult))
                            c.wait()
                            c.seq(v.tensor_tensor(agg[:, :, :], agg[:, :, :], own[:, :, 2 * H:W], ALU.add))
                        c.seq(v.tensor_scalar(den[:, :, :], den[:, :, :], eps or 0.0, 1e-30, ALU.add, ALU.max))
                        c.seq(v.reciprocal(den[:, :, :], den[:, :, :]))
                        for t in range(NT):
                            c.inc(v.tensor_tensor(agg[:, t, :].rearrange("p (h c) -> p h c", c=C), agg[:, t, :].rearrange("p (h c) -> p h c", c=C),
                                                  den[:, t, :].unsqueeze(2).broadcast_to([P, H, C]), ALU.mult))
                        c.wait()

                    @block.tensor
                    def _(pe):
                        pe.wait_ge(diags, 1)
                        for b in range(HB):
                            w = min(4, H + 1 - 4 * b)
                            ins = nc.tensor.matmul(psB[:, b, 0:w * P], ones[:, :], diag[:, 4 * b:4 * b + w, :].rearrange("p h c -> p (h c)"), start=True, stop=True)
                        ins.then_inc(spread, 1)

                        def body(g):
                            for s in range(GT):
                                hold(pe, hots, g * GT + s + 1)
                                if not zero(g) or s >= 2:
                                    hold(pe, taken, g * GT + max(s - 1, 0))
                                nc.tensor.matmul(psA[:, s % 2, 0:CW], oh[:, s, :], tw_rows[:, :], start=True, stop=True).then_inc(tailed, 1)
                        loop(pe, NG, body)

                    @block.scalar
                    def _(act):
                        act.wait_ge(targ, 1)
                        a.activation(tw[:, :], tw[:, :], ACT.Exp).then_inc(texp, 1)
                        act.wait_ge(warg, 1)
                        n = 2 + n_self
                        a.activation(wts[:, 0:n, :, :].rearrange("p n t h -> p (n t h)"), wts[:, 0:n, :, :].rearrange("p n t h -> p (n t h)"), ACT.Exp).then_inc(wexp, 1)

        def gat_phase(HG, self_score, agg):
            H, F, W = 4, 16, 24
            ctx, sb, ps, sem = phase()
            with ctx:
                att = sb("att", [P, 2, F])
                prod = sb("prod", [P, NT, F])
                att_in, chain, stored = sem("att_in"), sem("chain"), sem("stored")
                with nc.Block() as block:
                    @block.sync
                    def _(sp):
                        for n, dr in enumerate((f0_att_src, f0_att_dst)):
                            sp.dma_start(att[:, n, :], dr.rearrange("h e -> (h e)").partition_broadcast(P)).then_inc(att_in, 16)
                        sp.wait_ge(chain, 7)
                        sp.dma_start(table_rows(h_tab), HG[:, :, :]).then_inc(stored, 16)
                        sp.wait_ge(stored, 16)

                    @block.vector
                    def _(dve):
                        c = Count(dve, chain)
                        dve.wait_ge(att_in, 32)
                        for n in range(2):
                            c.seq(v.tensor_tensor(prod[:, :, :], HG[:, :, 0:F], att[:, n, :].unsqueeze(1).broadcast_to([P, NT, F]), ALU.mult))
                            c.seq(v.tensor_reduce(HG[:, :, F + H * n:F + H * (n + 1)], prod[:, :, :].rearrange("p t (h c) -> p t h c", h=H), AX, ALU.add))
                        c.seq(v.tensor_tensor(self_score[:, :, :], HG[:, :, F:F + H], HG[:, :, F + H:F + 2 * H], ALU.add))
                        c.seq(v.scalar_tensor_tensor(self_score[:, :, :], self_score[:, :, :], 0.2, self_score[:, :, :], ALU.mult, ALU.max))
                        c.seq(v.memset(prod[:, 0, 0:1], 0.0))
            ctx, sb, ps, sem = phase()
            with ctx:
                hs, hd = sb("hs", [P, 2, J2, W]), sb("hd", [P, 2, J2, W])
                iS = sb("iS", [P, 2, 2, J2], I32)
                feat, score = sb("feat", [P, F, NJ2]), sb("score", [P, H, NJ2])
                M, AE = sb("M", [P, H, NJ2 + 1]), sb("AE", [P, 2, H, NJ2])
                ST = sb("ST", [P, NJ2, W])
                got = [sem("got0"), sem("got1")]
                staged, spread, args, exps, states, stored, chain = (sem(n) for n in ("staged", "spread", "args", "exps", "states", "stored", "chain"))
                with nc.Block() as block:
                    @block.gpsimd
                    def _(pool):
                        def body(i):
                            for s in range(2):
                                if not zero(i):
                                    hold(pool, spread, 2 * i + s - 1)
                                cols = bass.ds((2 * i + s) * J2, J2)
                                nc.gpsimd.tensor_copy(iS[:, s, 0, :], src2[:, cols])
                                nc.gpsimd.tensor_copy(iS[:, s, 1, :], dst2[:, cols]).then_inc(staged, 1)
                                hold(pool, staged, 2 * i + s + 1)
                                for n, tile in ((0, hs), (1, hd)):
                                    for j in range(J2):
                                        pool.indirect_dma_start(out=tile[:, s, j, :], out_offset=None, in_=h_tab,
                                                                in_offset=bass.IndirectOffsetOnAxis(ap=iS[:, s, n, j:j + 1], axis=0)).then_inc(got[s], 16)
                        loop(pool, NB2 // 2, body)

                    @block.vector
                    def _(dve):
                        c = Count(dve, chain)
                        with dve.Fori(0, NB2 // 2) as i:
                            for s in range(2):
                                cols = bass.ds((2 * i + s) * J2, J2)
                                hold(dve, got[s], 32 * J2 * (i + 1))
                                v.tensor_copy(feat[:, :, cols], hs[:, s, :, 0:F].rearrange("p j f -> p f j"))
                                v.tensor_tensor(score[:, :, cols], hs[:, s, :, F:F + H].rearrange("p j f -> p f j"),
                                                hd[:, s, :, F + H:W].rearrange("p j f -> p f j"), ALU.add).then_inc(spread, 1)
                        dve.wait_ge(spread, NB2)
                        c.seq(v.scalar_tensor_tensor(score[:, :, :], score[:, :, :], 0.2, score[:, :, :], ALU.mult, ALU.max))
                        c.seq(v.memset(M[:, :, 0:1], -BIG))
                        for h in range(H):
                            c.inc(v.tensor_tensor_scan(M[:, h, 1:NJ2 + 1], pen2[:, :], score[:, h, :], -BIG, ALU.add, ALU.max))
                        c.wait()
                        c.inc(v.tensor_tensor(AE[:, 0, :, :], M[:, :, 0:NJ2], pen2[:, :].unsqueeze(1).broadcast_to([P, H, NJ2]), ALU.add))
                        c.seq(v.tensor_tensor(AE[:, 1, :, :], score[:, :, :], M[:, :, 1:NJ2 + 1], ALU.subtract))
                        c.seq(v.tensor_tensor(AE[:, 0, :, :], AE[:, 0, :, :], M[:, :, 1:NJ2 + 1], ALU.subtract))
                        dve.sem_inc(args, 1)
                        c.inc(v.tensor_copy(ST[:, :, 0:H], M[:, :, 1:NJ2 + 1].rearrange("p h j -> p j h")))
                        dve.wait_ge(exps, 1)
                        for h in range(H):
                            c.inc(v.tensor_tensor(feat[:, 4 * h:4 * h + 4, :], feat[:, 4 * h:4 * h + 4, :],
                                                  AE[:, 1, h, :].unsqueeze(1).broadcast_to([P, 4, NJ2]), ALU.mult))
                            c.inc(v.tensor_tensor_scan(ST[:, :, H + h], AE[:, 0, h, :], AE[:, 1, h, :], 0.0, ALU.mult, ALU.add))
                        c.wait()
                        for f in range(F):
                            c.inc(v.tensor_tensor_scan(ST[:, :, 2 * H + f], AE[:, 0, f // 4, :], feat[:, f, :], 0.0, ALU.mult, ALU.add))
                        c.wait()
                        dve.sem_inc(states, 1)

                    @block.scalar
                    def _(act):
                        act.wait_ge(args, 1)
                        flat = AE[:, :, :, :].rearrange("p n h j -> p (n h j)")
                        a.activation(flat, flat, ACT.Exp).then_inc(exps, 1)

                    @block.sync
                    def _(sp):
                        sp.wait_ge(states, 1)
                        sp.dma_start(gat_tab[0:E2, :].rearrange("(p j) w -> p j w", j=NJ2), ST[:, :, :]).then_inc(stored, 16)
                        sp.wait_ge(stored, 16)
                merge_phase(H, F, ST[:, NJ2 - 1, :], cont2, end2, gat_tab, agg, self_score[:, :, :], HG, 1e-16)

        def router_phase(agg, SC):
            F = 16
            ctx, sb, ps, sem = phase()
            with ctx:
                prm = sb("prm", [P, 3, F])
                mu, var, sq = sb("mu", [P, NT]), sb("var", [P, NT]), sb("sq", [P, NT, F])
                prm_in, vars_, rooted, chain = sem("prm_in"), sem("vars"), sem("rooted"), sem("chain")
                with nc.Block() as block:
                    @block.sync
                    def _(sp):
                        for n, dr in enumerate((f0_bgat, f0_lng, f0_lnb)):
                            sp.dma_start(prm[:, n, :], dr.partition_broadcast(P)).then_inc(prm_in, 16)

                    @block.vector
                    def _(dve):
                        c = Count(dve, chain)
                        A = agg[:, :, :]
                        par = lambda n: prm[:, n, :].unsqueeze(1).broadcast_to([P, NT, F])
                        tok = lambda t: t[:, :].unsqueeze(2).broadcast_to([P, NT, F])
                        dve.wait_ge(prm_in, 48)
                        c.seq(v.tensor_tensor(A, A, par(0), ALU.add))
                        c.seq(v.tensor_reduce(mu[:, :], A, AX, ALU.add))
                        c.seq(v.tensor_scalar(mu[:, :], mu[:, :], 1.0 / F, None, ALU.mult))
                        c.seq(v.tensor_tensor(A, A, tok(mu), ALU.subtract))
                        c.seq(v.tensor_tensor(sq[:, :, :], A, A, ALU.mult))
                        c.seq(v.tensor_reduce(var[:, :], sq[:, :, :], AX, ALU.add))
                        dve.sem_inc(vars_, 1)
                        dve.wait_ge(rooted, 1)
                        c.seq(v.reciprocal(var[:, :], var[:, :]))
                        c.seq(v.tensor_tensor(A, A, tok(var), ALU.mult))
                        c.seq(v.tensor_tensor(A, A, par(1), ALU.mult))
                        c.seq(v.tensor_tensor(A, A, par(2), ALU.add))
                        c.seq(v.tensor_reduce(SC[:, :, :], A.rearrange("p t (h e) -> p t e h", h=4), AX, ALU.add))
                        c.seq(v.tensor_scalar(SC[:, :, :], SC[:, :, :], 0.25, None, ALU.mult))

                    @block.scalar
                    def _(act):
                        act.wait_ge(vars_, 1)
                        a.activation(var[:, :], var[:, :], ACT.Sqrt, bias=eps_col[:, :], scale=1.0 / F).then_inc(rooted, 1)

        def gate_phase(SC, E, G, SC_bias=None):
            ctx, sb, ps, sem = phase()
            with ctx:
                t1, mask = sb("t1", [P, NT, E]), [sb("mask0", [P, NT, E]), sb("mask1", [P, NT, E])]
                m, first = sb("m", [P, 2, NT]), sb("first", [P, NT])
                e2, w = sb("e2", [P, NT]), sb("w", [P, 2, NT])
                arg, exped, chain = sem("arg"), sem("exped"), sem("chain")
                with nc.Block() as block:
                    @block.vector
                    def _(dve):
                        c = Count(dve, chain)
                        over = lambda t: t.unsqueeze(2).broadcast_to([P, NT, E])
                        numbers = iota_free[:, 0:E].unsqueeze(1).broadcast_to([P, NT, E])
                        for n in range(2):
                            c.seq(v.tensor_reduce(m[:, n, :], SC[:, :, :], AX, ALU.max))
                            c.seq(v.tensor_tensor(t1[:, :, :], SC[:, :, :], over(m[:, n, :]), ALU.is_equal))
                            c.seq(v.scalar_tensor_tensor(t1[:, :, :], t1[:, :, :], -float(P), numbers, ALU.mult, ALU.add))
                            c.seq(v.tensor_reduce(first[:, :], t1[:, :, :], AX, ALU.min))
                            c.seq(v.tensor_tensor(mask[n][:, :, :], t1[:, :, :], over(first[:, :]), ALU.is_equal))
                            if n == 0:
                                c.seq(v.scalar_tensor_tensor(SC[:, :, :], mask[n][:, :, :], -BIG, SC[:, :, :], ALU.mult, ALU.add))
                        c.seq(v.tensor_tensor(e2[:, :], m[:, 1, :], m[:, 0, :], ALU.subtract))
                        dve.sem_inc(arg, 1)
                        dve.wait_ge(exped, 1)
                        c.seq(v.tensor_scalar(w[:, 0, :], e2[:, :], 1.0, None, ALU.add))
                        c.seq(v.reciprocal(w[:, 0, :], w[:, 0, :]))
                        c.seq(v.tensor_tensor(w[:, 1, :], w[:, 0, :], e2[:, :], ALU.mult))
                        for n in range(2):
                            c.seq(v.tensor_tensor(mask[n][:, :, :], mask[n][:, :, :], over(w[:, n, :]), ALU.mult))
                        c.seq(v.tensor_tensor(G[:, :, :].rearrange("p e t -> p t e"), mask[0][:, :, :], mask[1][:, :, :], ALU.add))

                    @block.scalar
                    def _(act):
                        act.wait_ge(arg, 1)
                        a.activation(e2[:, :], e2[:, :], ACT.Exp).then_inc(exped, 1)

        def experts_phase(E, func, XNT, G, w1, b1, w2, b2, acc):
            FF = w1.shape[2]
            FC = FF // P
            HN = GT * P // 2
            PAIRS, IT = E // 2, 2 * NG
            ctx, sb, ps, sem = phase()
            with ctx:
                b1r, b1T = sb("b1r", [E * FC, P]), sb("b1T", [P, E * FC])
                b2s, gS, gT = sb("b2s", [E, D]), sb("gS", [P, GT, E]), sb("gT", [E, GT, P])
                psG, psA = ps("psG", [P, 2, 512]), ps("psA", [P, 2, 512])
                b_in, b1_turned, gs, turned, gts, biased, added, chain = (
                    sem(n) for n in ("b_in", "b1_turned", "gs", "turned", "gts", "biased", "added", "chain"))
                W1s, W2s = sb("W1s", [P, 2, 2, FF]), sb("W2s", [P, 2, FC, D])
                hT = sb("hT", [P, 2, FC, GT * P])
                with nc.Block() as block:
                    @block.sync
                    def _(sp):
                        sp.dma_start(b1r[:, :], b1.rearrange("e (c p) -> (e c) p", p=P)).then_inc(b_in, 16)
                        sp.dma_start(b2s[:, :], b2).then_inc(b_in, 16)

                    @block.tensor
                    def _(pe):
                        pe.wait_ge(b_in, 32)
                        nc.tensor.transpose(psA[:, 0, 0:E * FC], b1r[:, :], ident[0:E * FC, 0:E * FC]).then_inc(b1_turned, 1)
                        pe.wait_ge(chain, 1)

                        def body(g):
                            for s in range(GT):
                                hold(pe, gs, g + 1)
                                if not zero(g) or s >= 2:
                                    hold(pe, gts, g * GT + max(s - 1, 0))
                                nc.tensor.transpose(psG[0:E, s % 2, 0:P], gS[:, s, :], ident[:, :]).then_inc(turned, 1)
                            for s in range(GT):
                                hold(pe, gts, g * GT + s + 1)
                                if not zero(g) or s >= 2:
                                    hold(pe, added, g * GT + max(s - 1, 0))
                                nc.tensor.matmul(psA[:, s % 2, 0:D], gT[:, s, :], b2s[:, :], start=True, stop=True).then_inc(biased, 1)
                        loop(pe, NG, body)

                    @block.scalar
                    def _(act):
                        def body(g):
                            for s in range(GT):
                                hold(act, turned, g * GT + s + 1)
                                if not zero(g):
                                    hold(act, biased, g * GT)
                                a.copy(gT[:, s, :], psG[0:E, s % 2, 0:P]).then_inc(gts, 1)
                        loop(act, NG, body)

                    @block.vector
                    def _(dve):
                        dve.wait_ge(b1_turned, 1)
                        v.tensor_copy(b1T[:, :], psA[:, 0, 0:E * FC]).then_inc(chain, 1)
                        dve.wait_ge(chain, 1)

                        def body(g):
                            if not zero(g):
                                hold(dve, turned, g * GT)
                            v.tensor_copy(gS[:, :, :], G[:, :, bass.ds(g * GT, GT)].rearrange("p e t -> p t e")).then_inc(gs, 1)
                            for s in range(GT):
                                hold(dve, biased, g * GT + s + 1)
                                v.tensor_tensor(row(acc, g * GT + s), psA[:, s % 2, 0:D], row(acc, g * GT + s), ALU.add).then_inc(added, 1)
                        loop(dve, NG, body)
                psH_, psY_ = None, None
                experts_main(E, func, XNT, G, w1, w2, acc, b1T, W1s, W2s, hT, FF, FC, HN, PAIRS, IT, psG, psA)

        def experts_main(E, func, XNT, G, w1, w2, acc, b1T, W1s, W2s, hT, FF, FC, HN, PAIRS, IT, psG, psA):
            ctx, sb, ps, sem = phase()
            with ctx:
                psH4 = [psG, psA]
                psY = ps("psY", [P, 3, 512])
                w_in = [sem("w_in0"), sem("w_in1")]
                hidden, acted, rows_out, rows_read = sem("hidden"), sem("acted"), sem("rows_out"), sem("rows_read")
                with nc.Block() as block:
                    @block.sync
                    def _(sp):
                        def body(i):
                            for s in range(2):
                                if not zero(i):
                                    hold(sp, rows_out, NT * (2 * i + s - 1))
                                sp.dma_start(W1s[:, s, :, :], w1[bass.ds(2 * i + s, 1), :, :].rearrange("a (k p) f -> p (a k) f", p=P)).then_inc(w_in[s], 16)
                                sp.dma_start(W2s[:, s, :, :], w2[bass.ds(2 * i + s, 1), :, :].rearrange("a (c p) d -> p (a c) d", p=P)).then_inc(w_in[s], 16)
                        loop(sp, PAIRS, body)

                    def passes(eng, body):
                        body(0, PAIRS == 1)
                        if PAIRS > 2:
                            with eng.Fori(1, PAIRS - 1) as i:
                                body(i, False)
                        if PAIRS > 1:
                            body(PAIRS - 1, True)

                    @block.tensor
                    def _(pe):
                        def up(i, n):
                            s, g = n // NG, n % NG
                            if g == 0:
                                hold(pe, w_in[s], 32 * (i + 1))
                            for f in range(FC):
                                if f >= 2 or n or not zero(i):
                                    hold(pe, acted, (i * IT + n) * FC + f - 1)
                                for hf in range(2):
                                    for k in range(2):
                                        ins = nc.tensor.matmul(psH4[f % 2][:, hf, 0:HN], W1s[:, s, k, f * P:(f + 1) * P],
                                                               XNT[:, g, k, hf * HN:(hf + 1) * HN], start=(k == 0), stop=(k == 1))
                                ins.then_inc(hidden, 1)

                        def down(i, n):
                            s, g = n // NG, n % NG
                            hold(pe, acted, (i * IT + n + 1) * FC)
                            for t in range(GT):
                                if t >= 2 or n or not zero(i):
                                    hold(pe, rows_read, (i * IT + n) * GT + t - 1)
                                for f in range(FC):
                                    ins = nc.tensor.matmul(psY[:, t % 3, 0:D], hT[:, n % 2, f, t * P:(t + 1) * P], W2s[:, s, f, :],
                                                           start=(f == 0), stop=(f == FC - 1))
                                ins.then_inc(rows_out, 1)
                        up(0, 0)

                        def body(i, last):
                            for n in range(IT):
                                if n + 1 < IT:
                                    up(i, n + 1)
                                elif not last:
                                    up(i + 1, 0)
                                down(i, n)
                        passes(pe, body)

                    @block.scalar
                    def _(act):
                        def body(i, last):
                            for n in range(IT):
                                s = n // NG
                                if n >= 2 or not zero(i):
                                    hold(act, rows_out, (i * IT + n - 1) * GT)
                                for f in range(FC):
                                    hold(act, hidden, (i * IT + n) * FC + f + 1)
                                    a.activation(hT[:, n % 2, f, :].rearrange("p (a c) -> p a c", a=2), psH4[f % 2][:, :, 0:HN], func,
                                                 bias=b1T[:, bass.ds((2 * i + s) * FC + f, 1)]).then_inc(acted, 1)
                        passes(act, body)

                    @block.vector
                    def _(dve):
                        def body(i, last):
                            for n in range(IT):
                                s, g = n // NG, n % NG
                                for t in range(GT):
                                    hold(dve, rows_out, (i * IT + n) * GT + t + 1)
                                    o = acc[:, g * GT + t, :]
                                    gate = G[:, bass.ds(2 * i + s, 1), g * GT + t:g * GT + t + 1].rearrange("p a b -> p (a b)")
                                    v.scalar_tensor_tensor(o, psY[:, t % 3, 0:D], gate, o, ALU.mult, ALU.add).then_inc(rows_read, 1)
                        passes(dve, body)

        def attention_phase(tails):
            H, DH = 8, 32
            W = 2 * H + D
            SCALE = DH ** -0.5
            ctx, sb, ps, sem = phase()
            with ctx:
                Q, KV = sb("Q", [P, 2, J1, D]), sb("KV", [P, 2, J1, 2 * D])
                iS = sb("iS", [P, 2, 2, J1], I32)
                S, pen, M = sb("S", [P, 2, H, J1 + 1]), sb("pen", [P, 2, H, J1 + 1]), sb("M", [P, 2, H, J1 + 1])
                AE, L = sb("AE", [P, 2, 2, H, J1 + 1]), sb("L", [P, 2, H, J1 + 1])
                ST = sb("ST", [P, 2, J1, W])
                tmp = sb("tmp", [P, 2, D])
                got, stored = [sem("got0"), sem("got1")], [sem("stored0"), sem("stored1")]
                staged, read, args, exps, states, chain = (sem(n) for n in ("staged", "read", "args", "exps", "states", "chain"))
                with nc.Block() as block:
                    @block.gpsimd
                    def _(pool):
                        def body(i):
                            for s in range(2):
                                if not zero(i):
                                    hold(pool, read, 2 * i + s - 1)
                                cols = bass.ds((2 * i + s) * J1, J1)
                                nc.gpsimd.tensor_copy(iS[:, s, 0, :], dst1[:, cols])
                                nc.gpsimd.tensor_copy(iS[:, s, 1, :], src1[:, cols]).then_inc(staged, 1)
                                hold(pool, staged, 2 * i + s + 1)
                                for j in range(J1):
                                    for n, tile, tab in ((0, Q, q_tab), (1, KV, kv_tab)):
                                        pool.indirect_dma_start(out=tile[:, s, j, :], out_offset=None, in_=tab,
                                                                in_offset=bass.IndirectOffsetOnAxis(ap=iS[:, s, n, j:j + 1], axis=0)).then_inc(got[s], 16)
                        loop(pool, NB1 // 2, body)

                    @block.vector
                    def _(dve):
                        c = Count(dve, chain)
                        for s in range(2):
                            c.inc(v.memset(pen[:, s, :, 0:1], -BIG))
                            c.inc(v.memset(AE[:, s, 0, :, 0:1], 0.0))
                        c.inc(v.memset(M[:, 1, :, :], -BIG))
                        c.inc(v.memset(L[:, 1, :, :], 0.0))
                        c.seq(v.memset(ST[:, 1, J1 - 1, :], 0.0))

                        def body(i):
                            per = 2 * (14 + 2 * J1)
                            c.at(i, per)
                            for s in range(2):
                                b, o = 2 * i + s, 1 - s
                                cols = bass.ds(b * J1, J1)
                                flat = lambda t: t.rearrange("p h j -> p (h j)")
                                c.inc(v.tensor_copy(pen[:, s, :, 1:J1 + 1], pen1[:, cols].unsqueeze(1).broadcast_to([P, H, J1])))
                                c.inc(v.tensor_copy(S[:, s, :, 0], M[:, o, :, J1]))
                                hold(dve, got[s], 32 * J1 * (i + 1))
                                c.seq(v.tensor_tensor(Q[:, s, :, :], Q[:, s, :, :], KV[:, s, :, 0:D], ALU.mult))
                                c.seq(v.tensor_reduce(S[:, s, :, 1:J1 + 1].rearrange("p h j -> p j h"),
                                                      Q[:, s, :, :].rearrange("p j (h c) -> p j h c", c=DH), AX, ALU.add))
                                c.seq(v.tensor_scalar(S[:, s, :, 1:J1 + 1], S[:, s, :, 1:J1 + 1], SCALE, None, ALU.mult))
                                c.seq(v.tensor_tensor_scan(flat(M[:, s, :, :]), flat(pen[:, s, :, :]), flat(S[:, s, :, :]), -BIG, ALU.add, ALU.max))
                                c.inc(v.tensor_tensor(AE[:, s, 0, :, 1:J1 + 1], M[:, s, :, 0:J1], pen[:, s, :, 1:J1 + 1], ALU.add))
                                c.seq(v.tensor_tensor(AE[:, s, 1, :, 1:J1 + 1], S[:, s, :, 1:J1 + 1], M[:, s, :, 1:J1 + 1], ALU.subtract))
                                c.seq(v.tensor_tensor(AE[:, s, 0, :, 1:J1 + 1], AE[:, s, 0, :, 1:J1 + 1], M[:, s, :, 1:J1 + 1], ALU.subtract))
                                dve.sem_inc(args, 1)
                                hold(dve, exps, b + 1)
                                c.seq(v.tensor_copy(AE[:, s, 1, :, 0], L[:, o, :, J1]))
                                c.inc(v.tensor_tensor_scan(flat(L[:, s, :, :]), flat(AE[:, s, 0, :, :]), flat(AE[:, s, 1, :, :]), 0.0, ALU.mult, ALU.add))
                                vals = lambda j0, n: KV[:, s, j0:j0 + n, D:2 * D].rearrange("p j (h c) -> p j h c", c=DH)
                                for j in range(J1):
                                    hv = KV[:, s, j, D:2 * D].rearrange("p (h c) -> p h c", c=DH)
                                    ins = v.tensor_tensor(hv, hv, AE[:, s, 1, :, j + 1].unsqueeze(2).broadcast_to([P, H, DH]), ALU.mult)
                                c.seq(ins)
                                if not zero(i):
                                    hold(dve, stored[s], 16 * i)
                                for j in range(J1):
                                    prev = ST[:, o, J1 - 1, 2 * H:W] if j == 0 else ST[:, s, j - 1, 2 * H:W]
                                    c.seq(v.tensor_tensor(tmp[:, j % 2, :].rearrange("p (h c) -> p h c", c=DH), prev.rearrange("p (h c) -> p h c", c=DH),
                                                          AE[:, s, 0, :, j + 1].unsqueeze(2).broadcast_to([P, H, DH]), ALU.mult))
                                    c.seq(v.tensor_tensor(ST[:, s, j, 2 * H:W], tmp[:, j % 2, :], KV[:, s, j, D:2 * D], ALU.add))
                                dve.sem_inc(read, 1)
                                c.inc(v.tensor_copy(ST[:, s, :, 0:H], M[:, s, :, 1:J1 + 1].rearrange("p h j -> p j h")))
                                c.seq(v.tensor_copy(ST[:, s, :, H:2 * H], L[:, s, :, 1:J1 + 1].rearrange("p h j -> p j h")))
                                dve.sem_inc(states, 1)
                        loop(dve, NB1 // 2, body)
                        c.end(NB1 // 2)
                        c.seq(v.tensor_copy(tails[:, :], ST[:, 1, J1 - 1, :]))

                    @block.scalar
                    def _(act):
                        with act.Fori(0, NB1 // 2) as i:
                            for s in range(2):
                                hold(act, args, 2 * i + s + 1)
                                e = AE[:, s, :, :, 1:J1 + 1].rearrange("p n h j -> p (n h) j")
                                a.activation(e, e, ACT.Exp).then_inc(exps, 1)

                    @block.sync
                    def _(sp):
                        tab = att_tab[0:P * NJ1, :].rearrange("(p j) w -> p j w", j=NJ1)
                        with sp.Fori(0, NB1 // 2) as i:
                            for s in range(2):
                                sp.wait_ge(states, 2 * i + s + 1)
                                sp.dma_start(tab[:, bass.ds((2 * i + s) * J1, J1), :], ST[:, s, :, :]).then_inc(stored[s], 16)
                        for s in range(2):
                            sp.wait_ge(stored[s], 16 * (NB1 // 2))

        def out_phase(agg, XNR):
            H, DH = 8, 32
            ctx, sb, ps, sem = phase()
            with ctx:
                wo, bo = sb("wo", [P, 2, D]), sb("bo", [P, D])
                u, ut = sb("u", [P, GT, D]), sb("ut", [P, 2, GT, P])
                psT, psO = ps("psT", [P, 2, 512]), ps("psO", [P, 2, 512])
                w_in, summed, turned, columns, done, added, chain = (sem(n) for n in ("w_in", "summed", "turned", "columns", "done", "added", "chain"))
                with nc.Block() as block:
                    @block.sync
                    def _(sp):
                        sp.dma_start(wo[:, :, :], g1_wout.rearrange("(k p) n -> p k n", p=P)).then_inc(w_in, 16)
                        sp.dma_start(bo[:, :], g1_bout.partition_broadcast(P)).then_inc(w_in, 16)

                    @block.vector
                    def _(dve):
                        dve.wait_ge(w_in, 32)

                        def body(g):
                            if not zero(g):
                                hold(dve, turned, g * GT)
                            for s in range(GT):
                                t = g * GT + s
                                v.tensor_tensor(u[:, s, :].rearrange("p (c h) -> p c h", h=H), row(agg, t).rearrange("p (h c) -> p c h", h=H),
                                                row(XNR, t).rearrange("p (c h) -> p c h", h=H), ALU.add).then_inc(summed, 1)
                            for s in range(GT):
                                t = g * GT + s
                                v.tensor_tensor(row(X, t), row(X, t), bo[:, :], ALU.add).then_inc(chain, 1)
                            for s in range(GT):
                                t = g * GT + s
                                hold(dve, done, t + 1)
                                hold(dve, chain, t + 1)
                                v.tensor_tensor(row(X, t), row(X, t), psO[:, s % 2, 0:D], ALU.add).then_inc(added, 1)
                        loop(dve, NG, body)

                    @block.tensor
                    def _(pe):
                        pe.wait_ge(w_in, 32)

                        def body(g):
                            for s in range(GT):
                                hold(pe, summed, g * GT + s + 1)
                                if not zero(g) or s >= 2:
                                    hold(pe, columns, g * GT + max(s - 1, 0))
                                nc.tensor.transpose(psT[:, s % 2, 0:P], u[:, s, 0:P], ident[:, :])
                                nc.tensor.transpose(psT[:, s % 2, P:D], u[:, s, P:D], ident[:, :]).then_inc(turned, 1)
                            for s in range(GT):
                                hold(pe, columns, g * GT + s + 1)
                                if not zero(g) or s >= 2:
                                    hold(pe, added, g * GT + max(s - 1, 0))
                                for k in range(2):
                                    ins = nc.tensor.matmul(psO[:, s % 2, 0:D], ut[:, k, s, :], wo[:, k, :], start=(k == 0), stop=(k == 1))
                                ins.then_inc(done, 1)
                        loop(pe, NG, body)

                    @block.scalar
                    def _(act):
                        def body(g):
                            for s in range(GT):
                                hold(act, turned, g * GT + s + 1)
                                if not zero(g):
                                    hold(act, done, g * GT)
                                a.copy(ut[:, :, s, :], psT[:, s % 2, 0:D].rearrange("p (k c) -> p k c", k=2)).then_inc(columns, 1)
                        loop(act, NG, body)

        def last_norm_phase(Y):
            ctx, sb, ps, sem = phase()
            with ctx:
                st, mv, sd, rs = sb("st", [P, NT, 6]), sb("mv", [P, NT, 2]), sb("sd", [P, NT]), sb("rs", [P, NT])
                gam, bet = sb("gam", [P, D]), sb("bet", [P, D])
                p_in, stats, rooted, chain = sem("p_in"), sem("stats"), sem("rooted"), sem("chain")
                with nc.Block() as block:
                    @block.sync
                    def _(sp):
                        sp.dma_start(gam[:, :], f1_gamma.partition_broadcast(P)).then_inc(p_in, 16)
                        sp.dma_start(bet[:, :], f1_beta.partition_broadcast(P)).then_inc(p_in, 16)

                    @block.vector
                    def _(dve):
                        c = Count(dve, chain)
                        dve.wait_ge(p_in, 32)
                        for t in range(NT):
                            c.inc(v.bn_stats(st[:, t, :], Y[:, t, :]))
                        c.wait()
                        for t in range(NT):
                            c.inc(v.bn_aggr(mv[:, t, :], st[:, t, :]))
                        c.wait()
                        dve.sem_inc(stats, 1)
                        dve.wait_ge(rooted, 1)
                        c.seq(v.reciprocal(rs[:, :], sd[:, :]))
                        for t in range(NT):
                            c.inc(v.tensor_scalar(Y[:, t, :], Y[:, t, :], mv[:, t, 0:1], rs[:, t:t + 1], ALU.subtract, ALU.mult))
                        c.wait()
                        all_rows = lambda tile: tile[:, :].unsqueeze(1).broadcast_to([P, NT, D])
                        c.seq(v.tensor_tensor(Y[:, :, :], Y[:, :, :], all_rows(gam), ALU.mult))
                        c.seq(v.tensor_tensor(Y[:, :, :], Y[:, :, :], all_rows(bet), ALU.add))
                        c.seq(v.tensor_tensor(X[:, :, :], X[:, :, :], Y[:, :, :], ALU.add))

                    @block.scalar
                    def _(act):
                        act.wait_ge(stats, 1)
                        a.activation(sd[:, :], mv[:, :, 1], ACT.Sqrt, bias=eps_col[:, :]).then_inc(rooted, 1)

        def finish_phase(tile):
            ctx, sb, ps, sem = phase()
            with ctx:
                out_stored = sem("out_stored")
                with nc.Block() as block:
                    @block.sync
                    def _(sp):
                        sp.dma_start(table_rows(out[0:(NT - 1) * P, :]), tile[:, 0:NT - 1, :]).then_inc(out_stored, 16)
                        sp.dma_start(out[(NT - 1) * P:N, :], tile[0:TAIL_ROWS, NT - 1, :]).then_inc(out_stored, 16)
                        sp.wait_ge(out_stored, 32)

        start_phase()
        if LAST_PHASE >= 1:
            sort_phase(E1, NJ1, J1, src, [dst, edge_weight], key_tab[0], by_src_tab, end0, P * NJ1)
            reload_phase(by_src_tab, NJ1, [(1, nbr0), (2, w0)], keep0, None, cont0)
            norm_phase(table=xn_tab)
            gnn0_phase()
        if LAST_PHASE >= 2:
            f_ctx = ExitStack()
            with f_ctx:
                G0 = keep_sb(f_ctx, "G0", [P, 4, NT])
                XNT0 = keep_sb(f_ctx, "XNT0", [P, NG, 2, GT * P])
                r_ctx = ExitStack()
                sort_phase(E2, NJ2, J2, f0_edges[1, :], [f0_edges[0, :]], key_tab[1], by_dst_tab, end2, E2)
                reload_phase(by_dst_tab, NJ2, [(0, dst2), (1, src2)], keep2, pen2, cont2)
                with r_ctx:
                    HG = keep_sb(r_ctx, "HG", [P, NT, 24])
                    agg0 = keep_sb(r_ctx, "agg0", [P, NT, 16])
                    self_score = keep_sb(r_ctx, "self_score", [P, NT, 4])
                    SC0 = keep_sb(r_ctx, "SC0", [P, NT, 4])
                    norm_phase(cols_keep=XNT0, project=(f0_wgat, 16, None, HG))
                    gat_phase(HG, self_score, agg0)
                    router_phase(agg0, SC0)
                    gate_phase(SC0, 4, G0)
                experts_phase(4, ACT.Gelu, XNT0, G0, f0_w1, f0_b1, f0_w2, f0_b2, X)
        if LAST_PHASE >= 3:
            x_ctx = ExitStack()
            with x_ctx:
                graph_phase()
                XNR = keep_sb(x_ctx, "XNR", [P, NT, D])
                tails = keep_sb(x_ctx, "att_tails", [P, 16 + D])
                norm_phase(rows_keep=XNR, project=(g1_wqkv, 3 * D, g1_bqkv, [(q_tab, 0, D), (kv_tab, D, 2 * D)]))
                attention_phase(tails)
                agg1 = keep_sb(x_ctx, "agg1", [P, NT, D])
                merge_phase(8, D, tails[:, :], cont1, end1, att_tab, agg1)
                out_phase(agg1, XNR)
        if LAST_PHASE >= 4:
            e_ctx = ExitStack()
            with e_ctx:
                ACC = keep_sb(e_ctx, "ACC", [P, NT, D])
                G1 = keep_sb(e_ctx, "G1", [P, 16, NT])
                XNT1 = keep_sb(e_ctx, "XNT1", [P, NG, 2, GT * P])
                r_ctx = ExitStack()
                with r_ctx:
                    SC1 = keep_sb(r_ctx, "SC1", [P, NT, 16])
                    norm_phase(rows_keep=ACC, cols_keep=XNT1, project=(f1_gw, 16, f1_gb, SC1))
                    gate_phase(SC1, 16, G1)
                experts_phase(16, ACT.Relu, XNT1, G1, f1_w1, f1_b1, f1_w2, f1_b2, ACC)
                last_norm_phase(ACC)
        finish_phase(X)


_INS = ['x', 'src', 'dst', 'edge_weight', 'L0_gnn_weight1', 'L0_gnn_weight2', 'L0_gnn_gamma', 'L0_gnn_beta',
        'L0_ffn_W_gat', 'L0_ffn_att_src', 'L0_ffn_att_dst', 'L0_ffn_b_gat', 'L0_ffn_ln_gamma', 'L0_ffn_ln_beta',
        'L0_ffn_W1', 'L0_ffn_b1', 'L0_ffn_W2', 'L0_ffn_b2', 'L0_ffn_edge_index', 'L1_gnn_W_qkv', 'L1_gnn_b_qkv',
        'L1_gnn_W_out', 'L1_gnn_b_out', 'L1_ffn_gate_w', 'L1_ffn_gate_b', 'L1_ffn_w1', 'L1_ffn_b1', 'L1_ffn_w2',
        'L1_ffn_b2', 'L1_ffn_gamma', 'L1_ffn_beta']


def kernel(**inputs):
    import numpy as _np
    import concourse.bacc as _bacc
    from concourse import mybir as _mybir
    from concourse.bass_utils import run_bass_kernel_spmd as _run

    nc = _bacc.Bacc("TRN2", target_bir_lowering=False, num_devices=1)
    arrays, args = {}, []
    for name in _INS:
        arr = _np.ascontiguousarray(inputs[name])
        arrays[f"in_{name}_dram"] = arr
        args.append(nc.dram_tensor(f"in_{name}_dram", arr.shape, _mybir.dt.from_np(arr.dtype), kind="ExternalInput").ap())
    out = nc.dram_tensor("out_0_dram", (N, D), F32, kind="ExternalOutput").ap()
    bass_gnn_moe_kernel(nc, *args, out)
    r = _run(nc, [arrays], core_ids=[0])
    return r.results[0]["out_0_dram"]
```

```python
from contextlib import ExitStack

import concourse.bass as bass
from concourse import mybir

F32 = mybir.dt.float32
BF16 = mybir.dt.bfloat16
I32 = mybir.dt.int32
ALU = mybir.AluOpType
ACT = mybir.ActivationFunctionType
AX = mybir.AxisListType.X

P = 128
N = 3125
D = 256
NT = -(-N // P)
NP = NT * P
TAIL_ROWS = N - (NT - 1) * P
GT = 5
NG = NT // GT
assert NG * GT == NT
LN_EPS = 1e-5
BIG = 1e30

NH = 32
E1 = 50000
J1 = 14
NJ1 = 392
NB1 = NJ1 // J1
FULL1 = E1 // NJ1
REST1 = E1 - FULL1 * NJ1
E2 = 32768
J2 = 16
NJ2 = E2 // P
NB2 = NJ2 // J2
PAD_DST = NH * P - 1
assert NB1 * J1 == NJ1 and NB1 % 4 == 0 and NB2 * J2 == NJ2 and NB2 % 2 == 0
LAST_PHASE = 99


class Count:

    def __init__(self, eng, sem):
        self.eng, self.sem, self.base, self.n, self.start = eng, sem, 0, 0, 0

    def inc(self, ins):
        ins.then_inc(self.sem, 1)
        self.n += 1

    def wait(self):
        if not (isinstance(self.base, int) and self.base + self.n == 0):
            self.eng.wait_ge(self.sem, self.base + self.n)

    def seq(self, ins):
        self.inc(ins)
        self.wait()

    def at(self, i, per):
        if isinstance(i, int) and i == 0:
            self.start = self.base + self.n
        self.base, self.n, self.per = self.start + i * per, 0, per

    def end(self, trips):
        assert self.n == self.per, f"passes count {self.n}, said {self.per}"
        self.base, self.n = self.start + trips * self.per, 0


def loop(eng, trips, body):
    body(0)
    if trips > 1:
        with eng.Fori(1, trips) as i:
            body(i)


def zero(i):
    return isinstance(i, int) and i == 0


def row(tile, t):
    return tile[:, bass.ds(t, 1), :].rearrange("p a d -> p (a d)")


def table_rows(tab):
    return tab.rearrange("(t p) f -> p t f", p=P)


def bass_gnn_moe_kernel(nc, x, src, dst, edge_weight, g0_w1, g0_w2, g0_gamma, g0_beta, f0_wgat,
                        f0_att_src, f0_att_dst, f0_bgat, f0_lng, f0_lnb, f0_w1, f0_b1, f0_w2, f0_b2,
                        f0_edges, g1_wqkv, g1_bqkv, g1_wout, g1_bout, f1_gw, f1_gb, f1_w1, f1_b1,
                        f1_w2, f1_b2, f1_gamma, f1_beta, out):
    top = ExitStack()
    v, a = nc.vector, nc.scalar
    count = [0]

    def dram(name, shape, dt=F32):
        return nc.dram_tensor(name, shape, dt, kind="Internal").ap()

    def phase():
        ctx = ExitStack()
        count[0] += 1
        tag = f"_{count[0]}"
        own_sems = []

        def close():
            nc.clear_and_free_semaphores(own_sems)
            nc.all_engine_barrier()
        ctx.callback(close)

        def sb(name, shape, dt=F32):
            return ctx.enter_context(nc.sbuf_tensor(name + tag, shape, dt))

        def ps(name, shape, dt=F32):
            return ctx.enter_context(nc.psum_tensor(name + tag, shape, dt))

        def sem(name):
            own_sems.append(nc.alloc_semaphore(name=name + tag))
            return own_sems[-1]
        return ctx, sb, ps, sem

    def keep_sb(ctx, name, shape, dt=F32):
        return ctx.enter_context(nc.sbuf_tensor(name, shape, dt))

    ticks = {}

    def hold(eng, sem, value):
        if isinstance(value, int):
            eng.wait_ge(sem, value)
        else:
            name = str(eng.engine)
            if name not in ticks:
                ticks[name] = top.enter_context(nc.semaphore("tick_" + name.split(".")[-1]))
            eng.wait_ge(sem, value)
            eng.sem_inc(ticks[name], 1)

    with top:
        weights_in = top.enter_context(nc.semaphore("weights_in"))
        X = keep_sb(top, "X", [P, NT, D])
        ident = keep_sb(top, "ident", [P, P])
        ones = keep_sb(top, "ones", [P, P])
        iota_free = keep_sb(top, "iota_free", [P, P])
        iota_part = keep_sb(top, "iota_part", [P, 1])
        upper = keep_sb(top, "upper", [P, P])
        below = keep_sb(top, "below", [P, P])
        eps_col = keep_sb(top, "eps_col", [P, 1])
        xn_tab = dram("xn_tab", [NP, D])
        sum_tab = dram("sum_tab", [P * NJ1 + NP, D])
        adst_tab = dram("adst_tab", [E2 + NP, 4])
        by_src_tab = dram("by_src_tab", [P * NJ1, 3], I32)
        by_dst_tab = dram("by_dst_tab", [P * NJ2, 2], I32)
        key_tab = [dram("key_tab0", [P * NJ1]), dram("key_tab1", [P * NJ2])]
        h_tab = dram("h_tab", [NP, 24])
        gat_tab = dram("gat_tab", [E2 + 1, 24])
        q_tab = dram("q_tab", [NP, D])
        kv_tab = dram("kv_tab", [NP, 2 * D])
        att_tab = dram("att_tab", [P * NJ1 + 1, 16 + D])

        def start_phase():
            ctx, sb, ps, sem = phase()
            with ctx:
                ii = sb("ii", [P, P], I32)
                ip = sb("ip", [P, 1], I32)
                iotas, made, cleared, x_in = sem("iotas"), sem("made"), sem("cleared"), sem("x_in")
                with nc.Block() as block:
                    @block.gpsimd
                    def _(pool):
                        nc.gpsimd.iota(ii[:, :], pattern=[[1, P]], base=0, channel_multiplier=0).then_inc(iotas, 1)
                        nc.gpsimd.iota(ip[:, :], pattern=[[0, 1]], base=0, channel_multiplier=1).then_inc(iotas, 1)

                    @block.sync
                    def _(sp):
                        sp.dma_start(X[:, 0:NT - 1, :], table_rows(x[0:(NT - 1) * P, :])).then_inc(x_in, 16)
                        sp.wait_ge(cleared, 1)
                        sp.dma_start(X[0:TAIL_ROWS, NT - 1, :], x[(NT - 1) * P:N, :]).then_inc(x_in, 16)
                        sp.wait_ge(x_in, 32)

                    @block.vector
                    def _(dve):
                        c = Count(dve, made)
                        v.memset(X[:, NT - 1, :], 0.0).then_inc(cleared, 1)
                        c.inc(v.memset(ones[:, :], 1.0))
                        c.inc(v.memset(eps_col[:, :], LN_EPS))
                        dve.wait_ge(iotas, 2)
                        c.inc(v.tensor_copy(iota_free[:, :], ii[:, :]))
                        c.seq(v.tensor_copy(iota_part[:, :], ip[:, :]))
                        for tile, op in ((ident, ALU.is_equal), (upper, ALU.is_ge), (below, ALU.is_lt)):
                            c.seq(v.tensor_scalar(tile[:, :], iota_free[:, :], iota_part[:, :], None, op))

        def norm_phase(table=None, rows_keep=None, cols_keep=None, project=None, scatter=None):
            ctx, sb, ps, sem = phase()
            with ctx:
                turn = cols_keep is not None or project is not None
                st, mv = sb("st", [P, GT, 6]), sb("mv", [P, GT, 2])
                sd, rs = sb("sd", [P, GT]), sb("rs", [P, GT])
                xn = sb("xn", [P, GT, D])
                stats, rooted, chain, normed = sem("stats"), sem("rooted"), sem("chain"), sem("normed")
                stored, copied, group_free = sem("stored"), sem("copied"), sem("group_free")
                if turn:
                    turned, columns = sem("turned"), sem("columns")
                    psT = ps("psT", [P, 2, 512])
                    xt = sb("xt", [P, 2, GT, P])
                to_tables = False
                if project:
                    w_dram, PN, bias, sink = project
                    w_in, projected, evacuated, p_stored = sem("w_in"), sem("projected"), sem("evacuated"), sem("p_stored")
                    wp = sb("wp", [P, 2, PN])
                    psP = ps("psP", [P, 2, 512 * -(-PN // 512)])
                    bb = sb("bb", [P, PN])
                    to_tables = isinstance(sink, list)
                    if to_tables:
                        pr = sb("pr", [P, GT, PN])
                    cuts = [(0, PN, 0)] if PN <= 512 else [(0, 256, 0), (256, PN, 512)]
                    n_w = 16 * (1 + (bias is not None))
                n_keep = (rows_keep is not None) + (cols_keep is not None)
                if scatter is not None:
                    spots, spotted, scattered = sb("spots", [P, GT], I32), sem("spotted"), sem("scattered")
                with nc.Block() as block:
                    @block.sync
                    def _(sp):
                        if project:
                            sp.dma_start(wp[:, :, :], w_dram.rearrange("(k p) n -> p k n", p=P)).then_inc(w_in, 16)
                            if bias is not None:
                                sp.dma_start(bb[:, :], bias.partition_broadcast(P)).then_inc(w_in, 16)
                        with sp.Fori(0, NG) as g:
                            if table is not None:
                                sp.wait_ge(normed, (g + 1) * GT)
                                sp.dma_start(table_rows(table)[:, bass.ds(g * GT, GT), :], xn[:, :, :]).then_inc(stored, 16)
                            if to_tables:
                                hold(sp, evacuated, (g + 1) * GT)
                                for tab, a0, w in sink:
                                    sp.dma_start(table_rows(tab)[:, bass.ds(g * GT, GT), :], pr[:, :, a0:a0 + w]).then_inc(p_stored, 16)
                        if table is not None:
                            sp.wait_ge(stored, 16 * NG)
                        if to_tables:
                            sp.wait_ge(p_stored, 16 * NG * len(sink))

                    @block.vector
                    def _(dve):
                        c = Count(dve, chain)

                        def group(g):
                            c.at(g, 2 * GT + 1)
                            for s in range(GT):
                                c.inc(v.bn_stats(st[:, s, :], row(X, g * GT + s)))
                            hold(dve, chain, c.base + c.n)
                            for s in range(GT):
                                c.inc(v.bn_aggr(mv[:, s, :], st[:, s, :]))
                            hold(dve, chain, c.base + c.n)
                            dve.sem_inc(stats, 1)
                            hold(dve, rooted, g + 1)
                            c.inc(v.reciprocal(rs[:, :], sd[:, :]))
                            hold(dve, chain, c.base + c.n)
                            if not zero(g):
                                hold(dve, group_free, g)
                            for s in range(GT):
                                v.tensor_scalar(xn[:, s, :], row(X, g * GT + s), mv[:, s, 0:1], rs[:, s:s + 1],
                                                ALU.subtract, ALU.mult).then_inc(normed, 1)
                            if project:
                                for s in range(GT):
                                    hold(dve, projected, g * GT + s + 1)
                                    for a0, a1, spot in cuts:
                                        o = pr[:, s, a0:a1] if to_tables else row(sink, g * GT + s)[:, a0:a1]
                                        i0 = psP[:, s % 2, spot:spot + a1 - a0]
                                        ins = v.tensor_tensor(o, i0, bb[:, a0:a1], ALU.add) if bias is not None else v.tensor_copy(o, i0)
                                    ins.then_inc(evacuated, 1)
                        if project:
                            dve.wait_ge(w_in, n_w)
                        loop(dve, NG, group)

                    @block.scalar
                    def _(act):
                        with act.Fori(0, NG) as g:
                            hold(act, stats, g + 1)
                            a.activation(sd[:, :], mv[:, :, 1], ACT.Sqrt, bias=eps_col[:, :]).then_inc(rooted, 1)
                            if turn:
                                for s in range(GT):
                                    hold(act, turned, g * GT + s + 1)
                                    a.copy(xt[:, :, s, :], psT[:, s % 2, 0:D].rearrange("p (k c) -> p k c", k=2)).then_inc(columns, 1)

                    @block.tensor
                    def _(pe):
                        if project:
                            pe.wait_ge(w_in, n_w)

                        def group(g):
                                for s in range(GT):
                                    hold(pe, normed, g * GT + s + 1)
                                    if not zero(g) or s >= 2:
                                        hold(pe, columns, g * GT + max(s - 1, 0))
                                    nc.tensor.transpose(psT[:, s % 2, 0:P], xn[:, s, 0:P], ident[:, :])
                                    nc.tensor.transpose(psT[:, s % 2, P:D], xn[:, s, P:D], ident[:, :]).then_inc(turned, 1)
                                if project:
                                    for s in range(GT):
                                        hold(pe, columns, g * GT + s + 1)
                                        if not zero(g) or s >= 2:
                                            hold(pe, evacuated, g * GT + max(s - 1, 0))
                                        for a0, a1, spot in cuts:
                                            for k in range(2):
                                                ins = nc.tensor.matmul(psP[:, s % 2, spot:spot + a1 - a0], xt[:, k, s, :],
                                                                       wp[:, k, a0:a1], start=(k == 0), stop=(k == 1))
                                        ins.then_inc(projected, 1)
                        if turn:
                            loop(pe, NG, group)

                    @block.gpsimd
                    def _(pool):
                        with pool.Fori(0, NG) as g:
                            hold(pool, normed, (g + 1) * GT)
                            if rows_keep is not None:
                                nc.gpsimd.tensor_copy(rows_keep[:, bass.ds(g * GT, GT), :], xn[:, :, :]).then_inc(copied, 1)
                            if turn:
                                hold(pool, columns, (g + 1) * GT)
                            if cols_keep is not None:
                                nc.gpsimd.tensor_copy(cols_keep[:, bass.ds(g, 1), :, :].rearrange("p a k c -> p (a k c)"),
                                                      xt[:, :, :, :].rearrange("p k s c -> p (k s c)")).then_inc(copied, 1)
                            if table is not None:
                                hold(pool, stored, 16 * (g + 1))
                            if project:
                                hold(pool, evacuated, (g + 1) * GT)
                            if scatter is not None:
                                nc.gpsimd.tensor_copy(spots[:, :], scatter[1][:, bass.ds(g * GT, GT)]).then_inc(spotted, 1)
                                hold(pool, spotted, g + 1)
                                for s in range(GT):
                                    pool.indirect_dma_start(out=scatter[0], out_offset=bass.IndirectOffsetOnAxis(ap=spots[:, s:s + 1], axis=0),
                                                            in_=pr[:, s, 0:D], in_offset=None).then_inc(scattered, 16)
                                hold(pool, scattered, 16 * GT * (g + 1))
                            if to_tables:
                                hold(pool, p_stored, 16 * len(sink) * (g + 1))
                            if n_keep:
                                hold(pool, copied, n_keep * (g + 1))
                            pool.sem_inc(group_free, 1)

        def count_block(lo, hi, columns, J, counts):
            ctx, sb, ps, sem = phase()
            with ctx:
                onelo, onehi = sb("onelo", [P, 2, J, P], BF16), sb("onehi", [P, 2, J, NH], BF16)
                zerob = sb("zerob", [P, P], BF16)
                psC = ps("psC", [P, NH])
                built, used, counted, chain = sem("built"), sem("used"), sem("counted"), sem("chain")
                trips = columns // J // 2
                with nc.Block() as block:
                    @block.vector
                    def _(dve):
                        v.memset(zerob[:, :], 0.0).then_inc(chain, 1)
                        dve.wait_ge(chain, 1)

                        def body(i):
                            for s in range(2):
                                cols = bass.ds((i * 2 + s) * J, J)
                                if not zero(i):
                                    hold(dve, used, (i - 1) * 2 + s + 1)
                                v.tensor_tensor(onelo[:, s, :, :], iota_free[:, :].unsqueeze(1).broadcast_to([P, J, P]),
                                                lo[:, cols].unsqueeze(2).broadcast_to([P, J, P]), ALU.is_equal)
                                v.tensor_tensor(onehi[:, s, :, :], iota_free[:, 0:NH].unsqueeze(1).broadcast_to([P, J, NH]),
                                                hi[:, cols].unsqueeze(2).broadcast_to([P, J, NH]), ALU.is_equal).then_inc(built, 1)
                        loop(dve, trips, body)
                        dve.wait_ge(counted, 1)
                        v.tensor_copy(counts[:, :], psC[:, :]).then_inc(chain, 1)
                        dve.wait_ge(chain, 2)

                    @block.tensor
                    def _(pe):
                        pe.wait_ge(chain, 1)
                        nc.tensor.matmul(psC[:, :], zerob[:, :], zerob[:, 0:NH], start=True, stop=False)
                        with pe.Fori(0, trips) as i:
                            for s in range(2):
                                hold(pe, built, i * 2 + s + 1)
                                for j in range(J):
                                    ins = nc.tensor.matmul(psC[:, :], onelo[:, s, j, :], onehi[:, s, j, :], start=False, stop=False)
                                ins.then_inc(used, 1)
                        nc.tensor.matmul(psC[:, :], zerob[:, :], zerob[:, 0:NH], start=False, stop=True).then_inc(counted, 1)

        def prefix_block(counts, first, end, endrow, none_row, firstrow=None):
            ctx, sb, ps, sem = phase()
            with ctx:
                psI, psT = ps("psI", [P, 512]), ps("psTot", [P, 512])
                tot, scan, t1 = sb("tot", [P, NH]), sb("scan", [P, NH]), sb("t1", [P, NH])
                summed, chain = sem("summed"), sem("chain")
                with nc.Block() as block:
                    @block.tensor
                    def _(pe):
                        nc.tensor.matmul(psI[:, 0:NH], upper[:, :], counts[:, :], start=True, stop=True)
                        nc.tensor.matmul(psT[:, 0:NH], ones[:, :], counts[:, :], start=True, stop=True).then_inc(summed, 1)

                    @block.vector
                    def _(dve):
                        c = Count(dve, chain)
                        dve.wait_ge(summed, 1)
                        c.seq(v.tensor_copy(tot[:, :], psT[:, 0:NH]))
                        c.seq(v.tensor_tensor_scan(scan[:, :], ones[:, 0:NH], tot[:, :], 0.0, ALU.mult, ALU.add))
                        c.seq(v.tensor_tensor(scan[:, :], scan[:, :], tot[:, :], ALU.subtract))
                        c.seq(v.tensor_tensor(end[:, :], scan[:, :], psI[:, 0:NH], ALU.add))
                        c.seq(v.tensor_tensor(first[:, :], end[:, :], counts[:, :], ALU.subtract))
                        c.seq(v.tensor_scalar(t1[:, :], counts[:, :], 0.5, None, ALU.is_ge))
                        c.seq(v.scalar_tensor_tensor(scan[:, :], end[:, :], -1.0 - none_row, t1[:, :], ALU.add, ALU.mult))
                        c.seq(v.tensor_scalar(endrow[:, :], scan[:, 0:NT], float(none_row), None, ALU.add))
                        if firstrow is not None:
                            c.seq(v.tensor_scalar(tot[:, :], iota_free[:, 0:NH], float(P), float(none_row), ALU.mult, ALU.add))
                            c.seq(v.tensor_scalar(tot[:, :], tot[:, :], iota_part[:, 0:1], None, ALU.add))
                            c.seq(v.tensor_tensor(scan[:, :], first[:, :], tot[:, :], ALU.subtract))
                            c.seq(v.tensor_tensor(scan[:, :], scan[:, :], t1[:, :], ALU.mult))
                            c.seq(v.tensor_tensor(firstrow[:, :], scan[:, 0:NT], tot[:, 0:NT], ALU.add))

        def run_flags(dve, c, dstf, nextf, NJ, keep, pen, cont, tmp):
            c.seq(v.memset(keep[:, 0:1], 0.0))
            c.seq(v.tensor_tensor(keep[:, 1:NJ], dstf[:, 1:NJ], dstf[:, 0:NJ - 1], ALU.is_equal))
            c.seq(v.tensor_scalar(pen[:, :], keep[:, :], 1.0, BIG, ALU.subtract, ALU.mult))
            c.seq(v.tensor_tensor(tmp[:, 0:1], dstf[:, NJ - 1:NJ], nextf[:, :], ALU.is_equal))
            c.seq(v.scalar_tensor_tensor(cont[:, :], dstf[:, NJ - 1:NJ], 1.0, tmp[:, 0:1], ALU.add, ALU.mult))
            c.seq(v.tensor_scalar(cont[:, :], cont[:, :], 1.0, None, ALU.subtract))

        def graph_phase():
            ctx, sb, ps, sem = phase()
            with ctx:
                dstf, nexti, nextf = sb("dstf", [P, NJ1]), sb("nexti", [P, 1], I32), sb("nextf", [P, 1])
                loi, lo, hi, tmp = sb("loi", [P, NJ1], I32), sb("lo", [P, NJ1]), sb("hi", [P, NJ1]), sb("tmp", [P, 1])
                counts, first, end = sb("counts", [P, NH]), sb("first", [P, NH]), sb("end", [P, NH])
                cleared, e_in, chain = sem("cleared"), sem("e_in"), sem("chain")
                with nc.Block() as block:
                    @block.sync
                    def _(sp):
                        sp.wait_ge(cleared, 1)
                        for tile, dr in ((src1, src), (dst1, dst)):
                            sp.dma_start(tile[0:FULL1, :], dr[0:FULL1 * NJ1].rearrange("(p j) -> p j", j=NJ1)).then_inc(e_in, 16)
                            sp.dma_start(tile[FULL1:FULL1 + 1, 0:REST1], dr[FULL1 * NJ1:E1].unsqueeze(0)).then_inc(e_in, 16)
                        sp.dma_start(nexti[0:FULL1, :], dst.rearrange("(e o) -> e o", o=1)[NJ1:(FULL1 * NJ1 + 1):NJ1, :], allow_slow_non_contiguous=True).then_inc(e_in, 16)

                    @block.vector
                    def _(dve):
                        c = Count(dve, chain)
                        c.inc(v.memset(src1[:, :], 0))
                        c.inc(v.memset(dst1[:, :], PAD_DST))
                        c.seq(v.memset(nexti[:, :], PAD_DST))
                        dve.sem_inc(cleared, 1)
                        dve.wait_ge(e_in, 16 * 5)
                        c.inc(v.tensor_copy(dstf[:, :], dst1[:, :]))
                        c.seq(v.tensor_copy(nextf[:, :], nexti[:, :]))
                        run_flags(dve, c, dstf, nextf, NJ1, keep1, pen1, cont1, tmp)
                        c.seq(v.tensor_single_scalar(loi[:, :], dst1[:, :], P - 1, ALU.bitwise_and))
                        c.seq(v.tensor_copy(lo[:, :], loi[:, :]))
                        c.seq(v.tensor_single_scalar(loi[:, :], dst1[:, :], 7, ALU.logical_shift_right))
                        c.seq(v.tensor_copy(hi[:, :], loi[:, :]))
                        c.seq(v.tensor_scalar(dstf[:, :], dstf[:, :], float(N - 1), None, ALU.min))
                        c.seq(v.tensor_copy(dst1[:, :], dstf[:, :]))
                count_block(lo, hi, NJ1, J1, counts)
                prefix_block(counts, first, end, end1, P * NJ1, first1)

        def sort_phase(E, T, J, key_dram, payloads, keys_dram, table, endrow, none_row, firstrow=None):
            W = 1 + len(payloads)
            outer, osb, _, osem = phase()
            with outer:
                B = -(-T // P)
                TB = T // B
                assert TB * B == T
                full, rest = E // P, E % P
                key, pay = osb("key", [P, T]), osb("pay", [P, T, W])
                loi = osb("loi", [P, T], I32)
                lo, hi = osb("lo", [P, T + J]), osb("hi", [P, T + J])
                counts, first, end = osb("counts", [P, NH]), osb("first", [P, NH]), osb("end", [P, NH])

                def load_block():
                    ctx, sb, ps, sem = phase()
                    with ctx:
                        raw = [sb(f"raw{n}", [P, B, P], I32) for n in range(W)]
                        rawf = [sb(f"rawf{n}", [P, B, P]) for n in range(W)]
                        psT = ps("psT", [P, 2, 512])
                        cleared, r_in, floats, turned, copied, k_out = (sem(n) for n in ("cleared", "r_in", "floats", "turned", "copied", "k_out"))
                        n_in, drained = [0], sem("drained")
                        with nc.Block() as block:
                            @block.sync
                            def _(sp):
                                if full < T:
                                    sp.wait_ge(cleared, 1)
                                for n, dr in enumerate([key_dram] + payloads):
                                    for b in range(B):
                                        whole = min(TB, full - b * TB)
                                        o = raw[n] if dr.dtype == I32 else raw[n][:, :, :].bitcast(F32)
                                        sp.dma_start(o[0:whole, b, :], dr[b * TB * P:(b * TB + whole) * P].rearrange("(t e) -> t e", e=P)).then_inc(r_in, 16)
                                        n_in[0] += 16
                                    if rest:
                                        sp.dma_start(o[full % TB:full % TB + 1, full // TB, 0:rest], dr[full * P:E].unsqueeze(0)).then_inc(r_in, 16)
                                        n_in[0] += 16
                                sp.wait_ge(floats, 1)
                                sp.dma_start(keys_dram.rearrange("(b t e) -> t b e", t=TB, e=P), rawf[0][0:TB, :, :]).then_inc(k_out, 16)
                                sp.wait_ge(k_out, 16)

                            @block.vector
                            def _(dve):
                                c = Count(dve, copied)
                                if full < T:
                                    c.inc(v.memset(raw[0][:, :, :], PAD_DST))
                                    for n in range(1, W):
                                        c.inc(v.memset(raw[n][:, :, :], 0))
                                    c.wait()
                                    dve.sem_inc(cleared, 1)
                                dve.wait_ge(r_in, n_in[0])
                                for n, dr in enumerate([key_dram] + payloads):
                                    i0 = raw[n][0:TB, :, :] if dr.dtype == I32 else raw[n][:, :, :].bitcast(F32)[0:TB, :, :]
                                    c.inc(v.tensor_copy(rawf[n][0:TB, :, :], i0))
                                c.wait()
                                dve.sem_inc(floats, 1)
                                m = 0
                                for n, dr in enumerate([key_dram] + payloads):
                                    for b in range(B):
                                        m += 1
                                        dve.wait_ge(turned, m)
                                        o = pay[:, b * TB:(b + 1) * TB, n]
                                        if dr.dtype == I32:
                                            o = o.bitcast(I32)
                                        if n == 0:
                                            c.inc(v.tensor_copy(key[:, b * TB:(b + 1) * TB], psT[:, m % 2, 0:TB]))
                                        c.seq(v.tensor_copy(o, psT[:, m % 2, 0:TB]))
                                        dve.sem_inc(drained, 1)
                                keyi = pay[:, :, 0].bitcast(I32)
                                c.seq(v.tensor_single_scalar(loi[:, :], keyi, P - 1, ALU.bitwise_and))
                                c.inc(v.memset(lo[:, T:T + J], 0.0))
                                c.seq(v.tensor_copy(lo[:, 0:T], loi[:, :]))
                                c.seq(v.tensor_single_scalar(loi[:, :], keyi, 7, ALU.logical_shift_right))
                                c.inc(v.memset(hi[:, T:T + J], 0.0))
                                c.seq(v.tensor_copy(hi[:, 0:T], loi[:, :]))

                            @block.tensor
                            def _(pe):
                                pe.wait_ge(floats, 1)
                                m = 0
                                for n in range(W):
                                    for b in range(B):
                                        m += 1
                                        if m > 2:
                                            pe.wait_ge(drained, m - 2)
                                        nc.tensor.transpose(psT[:, m % 2, 0:TB], rawf[n][0:TB, b, :], ident[0:TB, 0:TB]).then_inc(turned, 1)

                def place_block():
                    ctx, sb, ps, sem = phase()
                    with ctx:
                        onelo, onehi = sb("onelo", [P, 2, J, P], BF16), sb("onehi", [P, 2, J, NH], BF16)
                        lowT = sb("lowT", [P, 2, J, P], BF16)
                        identb = sb("identb", [P, P], BF16)
                        keyS = sb("keyS", [P, 2, J])
                        kb = sb("kb", [P, 2, J, P])
                        grown, base, resets = sb("grown", [P, NH, J + 1]), sb("base", [P, NH, J + 1]), sb("resets", [P, NH, J + 1])
                        split = sb("split", [P, 2, J, 2, NH], BF16)
                        posA, posB = sb("posA", [P, 2, J]), sb("posB", [P, 2, J])
                        posS, payS = sb("posS", [P, 2, J], I32), sb("payS", [P, 2, J, W])
                        junk1, junk2 = sb("junk1", [P, J // 2, 2, NH]), sb("junk2", [P, J, P], BF16)
                        psH, psL = ps("psH", [P, 2, 512]), ps("psL", [P, 2, 512])
                        assert J * NH <= 512
                        psT = ps("psT", [P, 2, 1024], BF16)
                        kb_in = [sem("kb_in0"), sem("kb_in1")]
                        moved = [sem("moved0"), sem("moved1")]
                        built, turned, lows, splits, histed, looked, selected, placed, chain = (
                            sem(n) for n in ("built", "turned", "lows", "splits", "histed", "looked", "selected", "placed", "chain"))
                        QT = 4
                        quads = [(q, min(q + QT, J)) for q in range(0, J, QT)]
                        NQ = len(quads)
                        assert NQ % 2 == 0 and J % 2 == 0
                        trips = T // J // 2
                        with nc.Block() as block:
                            @block.sync
                            def _(sp):
                                def body(i):
                                    for s in range(2):
                                        if not zero(i):
                                            hold(sp, placed, 2 * i + s - 1)
                                        sp.dma_start(kb[:, s, :, :].rearrange("p j e -> p (j e)"),
                                                     keys_dram[bass.ds((2 * i + s) * J * P, J * P)].partition_broadcast(P)).then_inc(kb_in[s], 16)
                                loop(sp, trips, body)

                            @block.vector
                            def _(dve):
                                c = Count(dve, chain)
                                c.seq(v.tensor_copy(identb[:, :], ident[:, :]))

                                def build(m, s):
                                    cols = bass.ds(m * J, J)
                                    v.tensor_tensor(onelo[:, s, :, :], iota_free[:, :].unsqueeze(1).broadcast_to([P, J, P]),
                                                    lo[:, cols].unsqueeze(2).broadcast_to([P, J, P]), ALU.is_equal)
                                    v.tensor_tensor(onehi[:, s, :, :], iota_free[:, 0:NH].unsqueeze(1).broadcast_to([P, J, NH]),
                                                    hi[:, cols].unsqueeze(2).broadcast_to([P, J, NH]), ALU.is_equal).then_inc(built, 1)
                                c.inc(v.memset(resets[:, :, 1:J + 1], 1.0))
                                c.inc(v.memset(resets[:, :, 0:1], 0.0))
                                c.seq(v.tensor_copy(base[:, :, J], first[:, :]))
                                build(0, 0)

                                def body(i):
                                    c.at(i, 2 * 10)
                                    for s in range(2):
                                        m = 2 * i + s
                                        cols = bass.ds(m * J, J)
                                        if s or not zero(i):
                                            hold(dve, turned, m * NQ)
                                        build(m + 1, 1 - s)
                                        if not zero(i):
                                            hold(dve, moved[s], 16 * J * i)
                                        c.inc(v.tensor_copy(keyS[:, s, :], key[:, cols]))
                                        c.inc(v.tensor_copy(grown[:, :, 0], base[:, :, J]))
                                        hold(dve, histed, m + 1)
                                        c.inc(v.tensor_copy(grown[:, :, 1:J + 1], psH[:, s, 0:J * NH].rearrange("p (j h) -> p h j", h=NH)))
                                        hold(dve, chain, c.base + c.n)
                                        c.seq(v.tensor_tensor_scan(base[:, :, :].rearrange("p h j -> p (h j)"), resets[:, :, :].rearrange("p h j -> p (h j)"),
                                                                   grown[:, :, :].rearrange("p h j -> p (h j)"), 0.0, ALU.mult, ALU.add))
                                        before = base[:, :, 0:J].rearrange("p h j -> p j h")
                                        c.seq(v.tensor_copy(split[:, s, :, 0, :], before))
                                        v.tensor_tensor(split[:, s, :, 1, :], before, split[:, s, :, 0, :], ALU.subtract).then_inc(splits, 1)
                                        hold(dve, kb_in[s], 16 * (i + 1))
                                        for u in range(J):
                                            v.scalar_tensor_tensor(junk2[:, u, :], kb[:, s, u, :], keyS[:, s, u:u + 1], below[:, :],
                                                                   ALU.is_equal, ALU.mult, accum_out=posB[:, s, u:u + 1])
                                        hold(dve, looked, m + 1)
                                        for hf in range(2):
                                            js = slice(hf * (J // 2), (hf + 1) * (J // 2))
                                            ins = v.tensor_tensor(junk1[:, :, :, :], psL[:, hf, 0:J * NH].rearrange("p (u a h) -> p u a h", a=2, h=NH),
                                                                  onehi[:, s, js, :].unsqueeze(2).broadcast_to([P, J // 2, 2, NH]), ALU.mult)
                                            c.seq(ins)
                                            ins = v.tensor_reduce(posA[:, s, js], junk1[:, :, :, :].rearrange("p u a h -> p u (a h)"), AX, ALU.add)
                                            c.seq(ins)
                                        dve.sem_inc(selected, 1)
                                        c.seq(v.tensor_tensor(posA[:, s, :], posA[:, s, :], posB[:, s, :], ALU.add))
                                        v.tensor_copy(posS[:, s, :], posA[:, s, :])
                                        v.tensor_copy(payS[:, s, :, :], pay[:, cols, :]).then_inc(placed, 1)
                                        hold(dve, placed, m + 1)
                                loop(dve, trips, body)
                                c.end(trips)

                            @block.tensor
                            def _(pe):
                                pe.wait_ge(chain, 1)

                                def hist_and_turn(m, s, first_two):
                                    hold(pe, built, m + 1)
                                    for u in range(J):
                                        ins = nc.tensor.matmul(psH[:, s, u * NH:(u + 1) * NH], onelo[:, s, u, :], onehi[:, s, u, :], start=True, stop=True)
                                    ins.then_inc(histed, 1)
                                    for q, (a0, a1) in enumerate(quads):
                                        if q >= 2 or not first_two:
                                            hold(pe, lows, m * NQ + q - 1)
                                        for u in range(a0, a1):
                                            ins = nc.tensor.transpose(psT[:, q % 2, (u - a0) * P:(u - a0 + 1) * P], onelo[:, s, u, :], identb[:, :])
                                        ins.then_inc(turned, 1)
                                hist_and_turn(0, 0, True)

                                def body(i):
                                    for s in range(2):
                                        m = 2 * i + s
                                        if s or not zero(i):
                                            hold(pe, splits, m)
                                        hist_and_turn(m + 1, 1 - s, False)
                                        hold(pe, splits, m + 1)
                                        if s or not zero(i):
                                            hold(pe, selected, m)
                                        for u in range(J):
                                            hf, at = u // (J // 2), u % (J // 2)
                                            ins = nc.tensor.matmul(psL[:, hf, at * 2 * NH:(at + 1) * 2 * NH], lowT[:, s, u, :],
                                                                   split[:, s, u, :, :].rearrange("p a h -> p (a h)"), start=True, stop=True)
                                        ins.then_inc(looked, 1)
                                loop(pe, trips, body)

                            @block.scalar
                            def _(act):
                                def lower(m, s, q, a0, a1):
                                    hold(act, turned, m * NQ + q + 1)
                                    a.copy(lowT[:, s, a0:a1, :].rearrange("p u e -> p (u e)"), psT[:, q % 2, 0:(a1 - a0) * P]).then_inc(lows, 1)
                                for q, (a0, a1) in enumerate(quads):
                                    lower(0, 0, q, a0, a1)

                                def body(i):
                                    for s in range(2):
                                        m = 2 * i + s
                                        if s or not zero(i):
                                            hold(act, looked, m)
                                        for q, (a0, a1) in enumerate(quads):
                                            lower(m + 1, 1 - s, q, a0, a1)
                                loop(act, trips, body)

                            @block.gpsimd
                            def _(pool):
                                with pool.Fori(0, trips) as i:
                                    for s in range(2):
                                        hold(pool, placed, 2 * i + s + 1)
                                        for u in range(J):
                                            pool.indirect_dma_start(out=table, out_offset=bass.IndirectOffsetOnAxis(ap=posS[:, s, u:u + 1], axis=0),
                                                                    in_=payS[:, s, u, :].bitcast(I32), in_offset=None).then_inc(moved[s], 16)
                                for s in range(2):
                                    pool.wait_ge(moved[s], 16 * J * trips)
                load_block()
                count_block(lo, hi, T, J, counts)
                prefix_block(counts, first, end, endrow, none_row, firstrow)
                place_block()

        def reload_phase(table, NJ, fields, keep, pen, cont):
            ctx, sb, ps, sem = phase()
            with ctx:
                W = table.shape[1]
                rows_in = sb("rows_in", [P, NJ, W], I32)
                keyf, nexti, nextf, tmp = sb("keyf", [P, NJ]), sb("nexti", [P, 1], I32), sb("nextf", [P, 1]), sb("tmp", [P, 1])
                penx = pen if pen is not None else sb("penx", [P, NJ])
                r_in, cleared, chain = sem("r_in"), sem("cleared"), sem("chain")
                with nc.Block() as block:
                    @block.sync
                    def _(sp):
                        grid = table.rearrange("(p j) w -> p j w", j=NJ)
                        sp.dma_start(rows_in[:, :, :], grid).then_inc(r_in, 16)
                        sp.wait_ge(cleared, 1)
                        sp.dma_start(nexti[0:P - 1, :], grid[1:P, 0, 0:1], allow_slow_non_contiguous=True).then_inc(r_in, 16)

                    @block.vector
                    def _(dve):
                        c = Count(dve, chain)
                        c.seq(v.memset(nexti[:, :], -2))
                        dve.sem_inc(cleared, 1)
                        dve.wait_ge(r_in, 32)
                        c.inc(v.tensor_copy(keyf[:, :], rows_in[:, :, 0]))
                        c.inc(v.tensor_copy(nextf[:, :], nexti[:, :]))
                        for n, tile in fields:
                            i0 = rows_in[:, :, n] if tile.dtype == I32 else rows_in[:, :, n].bitcast(F32)
                            c.inc(v.tensor_copy(tile[:, :], i0))
                        c.wait()
                        run_flags(dve, c, keyf, nextf, NJ, keep, penx, cont, tmp)

        def gnn0_phase():
            ctx, sb, ps, sem = phase()
            with ctx:
                S = 4
                G = sb("G", [P, S, J1, D])
                wS, kS = sb("wS", [P, S, J1]), sb("kS", [P, S, J1])
                iS = sb("iS", [P, S, J1], I32)
                carry = sb("carry", [P, D])
                zrow = sb("zrow", [1, D])
                got, stored = [sem(f"got{s}") for s in range(S)], [sem(f"stored{s}") for s in range(S)]
                staged, cols, scaled, summed = sem("staged"), sem("cols"), sem("scaled"), sem("summed")
                chain, z_ready, z_stored = sem("chain"), sem("z_ready"), sem("z_stored")
                with nc.Block() as block:
                    @block.gpsimd
                    def _(pool):
                        def body(i):
                            for s in range(S):
                                if not zero(i):
                                    hold(pool, stored[s], 16 * i)
                                nc.gpsimd.tensor_copy(iS[:, s, :], nbr0[:, bass.ds((S * i + s) * J1, J1)]).then_inc(staged, 1)
                                hold(pool, staged, S * i + s + 1)
                                for j in range(J1):
                                    pool.indirect_dma_start(out=G[:, s, j, :], out_offset=None, in_=xn_tab,
                                                            in_offset=bass.IndirectOffsetOnAxis(ap=iS[:, s, j:j + 1], axis=0)).then_inc(got[s], 16)
                        loop(pool, NB1 // S, body)

                    @block.scalar
                    def _(act):
                        with act.Fori(0, NB1 // S) as i:
                            for s in range(S):
                                hold(act, cols, S * i + s + 1)
                                hold(act, got[s], 16 * J1 * (i + 1))
                                for j in range(J1):
                                    a.mul(G[:, s, j, :], G[:, s, j, :], wS[:, s, j:j + 1]).then_inc(scaled, 1)

                    @block.vector
                    def _(dve):
                        c = Count(dve, chain)
                        v.memset(zrow[:, :], 0.0).then_inc(z_ready, 1)
                        c.seq(v.memset(carry[:, :], 0.0))

                        def body(i):
                            c.at(i, S * (J1 + 1))
                            for s in range(S):
                                b = S * i + s
                                sl = bass.ds(b * J1, J1)
                                if not zero(i):
                                    hold(dve, scaled, (b - S + 1) * J1)
                                v.tensor_copy(wS[:, s, :], w0[:, sl])
                                v.tensor_copy(kS[:, s, :], keep0[:, sl]).then_inc(cols, 1)
                                hold(dve, cols, b + 1)
                                for j in range(J1):
                                    hold(dve, scaled, b * J1 + j + 1)
                                    prev = carry[:, :] if j == 0 else G[:, s, j - 1, :]
                                    c.seq(v.scalar_tensor_tensor(G[:, s, j, :], prev, kS[:, s, j:j + 1], G[:, s, j, :], ALU.mult, ALU.add))
                                c.seq(v.tensor_copy(carry[:, :], G[:, s, J1 - 1, :]))
                                dve.sem_inc(summed, 1)
                        loop(dve, NB1 // S, body)
                        c.end(NB1 // S)

                    @block.sync
                    def _(sp):
                        sp.wait_ge(z_ready, 1)
                        sp.dma_start(sum_tab[P * NJ1:P * NJ1 + 1, :], zrow[:, :]).then_inc(z_stored, 16)
                        tab = sum_tab[0:P * NJ1, :].rearrange("(p j) f -> p j f", j=NJ1)
                        with sp.Fori(0, NB1 // S) as i:
                            for s in range(S):
                                sp.wait_ge(summed, S * i + s + 1)
                                sp.dma_start(tab[:, bass.ds((S * i + s) * J1, J1), :], G[:, s, :, :]).then_inc(stored[s], 16)
                        sp.wait_ge(z_stored, 16)
                        for s in range(S):
                            sp.wait_ge(stored[s], 16 * (NB1 // S))
                gnn0_dense(carry)

        def gnn0_dense(tails):
            ctx, sb, ps, sem = phase()
            with ctx:
                own = sb("own", [P, NT, D])
                HW = NP // 8
                NXT, O1T = sb("NXT", [P, 2, NP]), sb("O1T", [P, 2, NP])
                H = [sb("H1", [P, 2, D]), sb("H2", [P, 2, D])]
                gam, bet = sb("gam", [P, 2]), sb("bet", [P, 2])
                cm, cmS, oh = sb("cm", [P, NT]), sb("cmS", [P, GT]), sb("oh", [P, GT, P])
                nx = sb("nx", [P, GT, D])
                mean, var, scl, bia, junk = (sb(n, [P, 2]) for n in ("mean", "var", "scl", "bia", "junk"))
                big = own
                psA, psT = ps("psA", [P, 2, 512]), ps("psT", [P, 2, 512])
                ps1 = ps("ps1", [P, 2, 512])
                h_in, own_in, chain, signed = sem("h_in"), sem("own_in"), sem("chain"), sem("signed")
                hots, tailed, added, turned, columns = sem("hots"), sem("tailed"), sem("added"), sem("turned"), sem("columns")
                mm1, ev1 = sem("mm1"), sem("ev1")
                a_stat, v_stat, tanhs, mm2, resid = sem("a_stat"), sem("v_stat"), sem("tanhs"), sem("mm2"), sem("resid")
                tt = sb("tt", [P, 2, GT * P])
                minus = {(1, 0), (2, 0), (3, 0), (2, 1), (3, 2), (1, 3)}
                with nc.Block() as block:
                    @block.sync
                    def _(sp):
                        for Ht, wd in zip(H, (g0_w1, g0_w2)):
                            for ra in range(4):
                                for cb in range(4):
                                    comp = ra ^ cb
                                    sp.dma_start(Ht[64 * (ra % 2):64 * (ra % 2) + 64, ra // 2, 64 * cb:64 * cb + 64],
                                                 wd[:, 64 * comp:64 * comp + 64]).then_inc(h_in, 16)
                        sp.dma_start(gam[:, :], g0_gamma.rearrange("(m p) -> p m", p=P), allow_slow_non_contiguous=True).then_inc(h_in, 16)
                        sp.dma_start(bet[:, :], g0_beta.rearrange("(m p) -> p m", p=P), allow_slow_non_contiguous=True).then_inc(h_in, 16)

                    @block.gpsimd
                    def _(pool):
                        for t in range(NT):
                            pool.indirect_dma_start(out=own[:, t, :], out_offset=None, in_=sum_tab[0:P * NJ1 + 1, :],
                                                    in_offset=bass.IndirectOffsetOnAxis(ap=end0[:, t:t + 1], axis=0)).then_inc(own_in, 16)

                    @block.vector
                    def _(dve):
                        c = Count(dve, chain)
                        c.seq(v.tensor_scalar(cm[:, :], iota_free[:, 0:NT], -float(P), cont0[:, :], ALU.mult, ALU.add))
                        dve.wait_ge(h_in, 16 * 34)
                        for Ht in H:
                            for ra, cb in sorted(minus):
                                blk = Ht[64 * (ra % 2):64 * (ra % 2) + 64, ra // 2, 64 * cb:64 * cb + 64]
                                c.seq(v.tensor_scalar(blk, blk, -1.0, None, ALU.mult))
                        dve.sem_inc(signed, 1)
                        dve.wait_ge(own_in, 16 * NT)

                        def body(g):
                            c.at(g, 1)
                            c.inc(v.tensor_copy(cmS[:, :], cm[:, bass.ds(g * GT, GT)]))
                            hold(dve, chain, c.base + c.n)
                            if not zero(g):
                                hold(dve, tailed, g * GT)
                                hold(dve, turned, g * GT)
                            for s in range(GT):
                                v.tensor_scalar(oh[:, s, :], iota_free[:, :], cmS[:, s:s + 1], None, ALU.is_equal).then_inc(hots, 1)
                            for s in range(GT):
                                hold(dve, tailed, g * GT + s + 1)
                                v.tensor_tensor(nx[:, s, :], psA[:, s % 2, 0:D], row(own, g * GT + s), ALU.add).then_inc(added, 1)
                        loop(dve, NG, body)
                        c.end(NG)
                        dve.wait_ge(ev1, 16)
                        for m in range(2):
                            c.inc(v.tensor_reduce(junk[:, m:m + 1], O1T[:, m, 0:N], AX, ALU.add))
                        c.wait()
                        c.seq(v.tensor_scalar(mean[:, :], junk[:, :], -1.0 / N, None, ALU.mult))
                        dve.sem_inc(v_stat, 1)
                        dve.wait_ge(a_stat, 3)
                        c.seq(v.reciprocal(scl[:, :], scl[:, :]))
                        c.seq(v.tensor_tensor(scl[:, :], scl[:, :], gam[:, :], ALU.mult))
                        c.seq(v.tensor_tensor(bia[:, :], mean[:, :], scl[:, :], ALU.mult))
                        c.seq(v.tensor_tensor(bia[:, :], bia[:, :], bet[:, :], ALU.add))
                        dve.sem_inc(v_stat, 1)
                        with dve.Fori(0, NG) as g:
                            for s in range(GT):
                                hold(dve, mm2, g * GT + s + 1)
                                v.tensor_tensor(row(X, g * GT + s), psA[:, s % 2, 0:D], row(X, g * GT + s), ALU.add).then_inc(resid, 1)

                    @block.tensor
                    def _(pe):
                        def sums(g):
                            for s in range(GT):
                                hold(pe, hots, g * GT + s + 1)
                                if not zero(g) or s >= 2:
                                    hold(pe, added, g * GT + max(s - 1, 0))
                                nc.tensor.matmul(psA[:, s % 2, 0:D], oh[:, s, :], tails[:, :], start=True, stop=True).then_inc(tailed, 1)
                            for s in range(GT):
                                hold(pe, added, g * GT + s + 1)
                                if not zero(g) or s >= 2:
                                    hold(pe, columns, g * GT + max(s - 1, 0))
                                nc.tensor.transpose(psT[:, s % 2, 0:P], nx[:, s, 0:P], ident[:, :])
                                nc.tensor.transpose(psT[:, s % 2, P:D], nx[:, s, P:D], ident[:, :]).then_inc(turned, 1)
                        loop(pe, NG, sums)
                        pe.wait_ge(columns, NT)
                        pe.wait_ge(signed, 1)

                        def dense(n):
                            for m in range(2):
                                if not zero(n):
                                    hold(pe, ev1, 2 * n + m - 1)
                                for k in range(2):
                                    ins = nc.tensor.matmul(ps1[:, m, 0:HW], H[0][:, k, m * P:(m + 1) * P], NXT[:, k, bass.ds(n * HW, HW)],
                                                           start=(k == 0), stop=(k == 1))
                                ins.then_inc(mm1, 1)
                        loop(pe, 8, dense)

                        def last(g):
                            hold(pe, tanhs, g + 1)
                            for s in range(GT):
                                if not zero(g) or s >= 2:
                                    hold(pe, resid, g * GT + max(s - 1, 0))
                                for k in range(2):
                                    ins = nc.tensor.matmul(psA[:, s % 2, 0:D], tt[:, k, s * P:(s + 1) * P], H[1][:, k, :], start=(k == 0), stop=(k == 1))
                                ins.then_inc(mm2, 1)
                        loop(pe, NG, last)

                    @block.scalar
                    def _(act):
                        with act.Fori(0, NG) as g:
                            for s in range(GT):
                                hold(act, turned, g * GT + s + 1)
                                a.copy(NXT[:, :, bass.ds((g * GT + s) * P, P)], psT[:, s % 2, 0:D].rearrange("p (k c) -> p k c", k=2)).then_inc(columns, 1)
                        with act.Fori(0, 8) as n:
                            for m in range(2):
                                hold(act, mm1, 2 * n + m + 1)
                                a.copy(O1T[:, m, bass.ds(n * HW, HW)], ps1[:, m, 0:HW]).then_inc(ev1, 1)
                        act.wait_ge(v_stat, 1)
                        flat = own[:, :, :].rearrange("p t d -> p (t d)")
                        for m in range(2):
                            a.activation(flat[:, m * N:(m + 1) * N], O1T[:, m, 0:N], ACT.Square, bias=mean[:, m:m + 1],
                                         accum_out=var[:, m:m + 1]).then_inc(a_stat, 1)
                        act.wait_ge(a_stat, 2)
                        a.activation(scl[:, :], var[:, :], ACT.Sqrt, bias=eps_col[:, :], scale=1.0 / N).then_inc(a_stat, 1)
                        act.wait_ge(v_stat, 2)

                        def body(g):
                            if not zero(g):
                                hold(act, mm2, g * GT)
                            for m in range(2):
                                ins = a.activation(tt[:, m, :], O1T[:, m, bass.ds(g * GT * P, GT * P)], ACT.Tanh,
                                                   bias=bia[:, m:m + 1], scale=scl[:, m:m + 1])
                            ins.then_inc(tanhs, 1)
                        loop(act, NG, body)

        def merge_phase(H, F, tails, cont, endrow, table, agg, self_score=None, self_rows=None, eps=None):
            W, C = 2 * H + F, F // H
            CW = 2 * H + F + 1
            ctx, sb, ps, sem = phase()
            with ctx:
                own, other = sb("own", [P, NT, W]), sb("other", [P, NT, CW])
                diag, eqm, tmp = sb("diag", [P, H + 1, P]), sb("eqm", [P, P]), sb("tmp", [P, P])
                penm, ref, lead, tw = sb("penm", [P, P]), sb("ref", [P, H]), sb("lead", [P, 1]), sb("tw", [P, H])
                tw_rows = sb("tw_rows", [P, CW])
                cm, cmS, oh = sb("cm", [P, NT]), sb("cmS", [P, GT]), sb("oh", [P, GT, P])
                top_, wts, den = sb("top_", [P, NT, H]), sb("wts", [P, 3, NT, H]), sb("den", [P, NT, H])
                zrow = sb("zrow", [1, W])
                HB = -(-(H + 1) // 4)
                psB, psA = ps("psB", [P, HB, 512]), ps("psA", [P, 2, 512])
                own_in, diags, spread, targ, texp, hots, tailed, taken, warg, wexp, chain = (
                    sem(n) for n in ("own_in", "diags", "spread", "targ", "texp", "hots", "tailed", "taken", "warg", "wexp", "chain"))
                z_ready, z_stored = sem("z_ready"), sem("z_stored")
                n_self = 1 if self_score is not None else 0
                with nc.Block() as block:
                    @block.sync
                    def _(sp):
                        sp.wait_ge(z_ready, 1)
                        sp.dma_start(table[table.shape[0] - 1:table.shape[0], :], zrow[:, :]).then_inc(z_stored, 16)

                    @block.gpsimd
                    def _(pool):
                        pool.wait_ge(z_stored, 16)
                        for t in range(NT):
                            pool.indirect_dma_start(out=own[:, t, :], out_offset=None, in_=table,
                                                    in_offset=bass.IndirectOffsetOnAxis(ap=endrow[:, t:t + 1], axis=0)).then_inc(own_in, 16)

                    @block.vector
                    def _(dve):
                        c = Count(dve, chain)
                        c.seq(v.memset(zrow[:, H:W], 0.0))
                        c.seq(v.memset(zrow[:, 0:H], -BIG))
                        dve.sem_inc(z_ready, 1)
                        for h in range(H):
                            c.inc(v.tensor_scalar(diag[:, h, :], ident[:, :], tails[:, h:h + 1], None, ALU.mult))
                        c.inc(v.tensor_scalar(diag[:, H, :], ident[:, :], cont[:, :], None, ALU.mult))
                        c.inc(v.tensor_scalar(cm[:, :], iota_free[:, 0:NT], -float(P), cont[:, :], ALU.mult, ALU.add))
                        c.wait()
                        dve.sem_inc(diags, 1)
                        dve.wait_ge(spread, 1)
                        bc = lambda h: psB[:, h // 4, (h % 4) * P:(h % 4 + 1) * P]
                        c.seq(v.tensor_scalar(eqm[:, :], bc(H), cont[:, :], None, ALU.is_equal))
                        c.seq(v.tensor_scalar(penm[:, :], eqm[:, :], 1.0, BIG, ALU.subtract, ALU.mult))
                        for h in range(H):
                            c.seq(v.tensor_tensor(tmp[:, :], bc(h), penm[:, :], ALU.add))
                            c.seq(v.tensor_reduce(ref[:, h:h + 1], tmp[:, :], AX, ALU.max))
                        c.seq(v.tensor_tensor(tmp[:, :], eqm[:, :], upper[:, :], ALU.mult))
                        c.seq(v.tensor_reduce(lead[:, :], tmp[:, :], AX, ALU.add))
                        c.seq(v.tensor_scalar(lead[:, :], lead[:, :], 1.5, None, ALU.is_lt))
                        c.seq(v.tensor_tensor(tw[:, :], tails[:, 0:H], ref[:, :], ALU.subtract))
                        dve.sem_inc(targ, 1)
                        dve.wait_ge(texp, 1)
                        c.inc(v.tensor_scalar(tw_rows[:, 0:H], ref[:, :], lead[:, :], None, ALU.mult))
                        c.inc(v.tensor_copy(tw_rows[:, CW - 1:CW], lead[:, :]))
                        c.inc(v.tensor_tensor(tw_rows[:, H:2 * H], tails[:, H:2 * H], tw[:, :], ALU.mult))
                        c.seq(v.tensor_tensor(tw_rows[:, 2 * H:W].rearrange("p (h c) -> p h c", c=C), tails[:, 2 * H:W].rearrange("p (h c) -> p h c", c=C),
                                              tw[:, :].unsqueeze(2).broadcast_to([P, H, C]), ALU.mult))

                        def body(g):
                            c.at(g, 1)
                            if not zero(g):
                                hold(dve, tailed, g * GT)
                            c.inc(v.tensor_copy(cmS[:, :], cm[:, bass.ds(g * GT, GT)]))
                            hold(dve, chain, c.base + c.n)
                            for s in range(GT):
                                v.tensor_scalar(oh[:, s, :], iota_free[:, :], cmS[:, s:s + 1], None, ALU.is_equal).then_inc(hots, 1)
                            for s in range(GT):
                                hold(dve, tailed, g * GT + s + 1)
                                v.tensor_copy(row(other, g * GT + s), psA[:, s % 2, 0:CW]).then_inc(taken, 1)
                        loop(dve, NG, body)
                        c.end(NG)
                        dve.wait_ge(taken, NT)
                        dve.wait_ge(own_in, 16 * NT)
                        om, oR = own[:, :, 0:H], other[:, :, 0:H]
                        has = other[:, :, CW - 1:CW]
                        c.seq(v.tensor_scalar(has, has, 1.0, BIG, ALU.subtract, ALU.mult))
                        c.seq(v.tensor_tensor(oR, oR, has.broadcast_to([P, NT, H]), ALU.add))
                        c.seq(v.tensor_tensor(top_[:, :, :], om, oR, ALU.max))
                        if n_self:
                            c.seq(v.tensor_tensor(top_[:, :, :], top_[:, :, :], self_score, ALU.max))
                            c.inc(v.tensor_tensor(wts[:, 2, :, :], self_score, top_[:, :, :], ALU.subtract))
                        c.inc(v.tensor_tensor(wts[:, 0, :, :], om, top_[:, :, :], ALU.subtract))
                        c.seq(v.tensor_tensor(wts[:, 1, :, :], oR, top_[:, :, :], ALU.subtract))
                        dve.sem_inc(warg, 1)
                        dve.wait_ge(wexp, 1)
                        wide = lambda n: wts[:, n, :, :].unsqueeze(3).broadcast_to([P, NT, H, C])
                        heads = lambda t, a0: t[:, :, a0:a0 + F].rearrange("p t (h c) -> p t h c", c=C)
                        c.inc(v.tensor_tensor(own[:, :, H:2 * H], own[:, :, H:2 * H], wts[:, 0, :, :], ALU.mult))
                        c.seq(v.tensor_tensor(other[:, :, H:2 * H], other[:, :, H:2 * H], wts[:, 1, :, :], ALU.mult))
                        c.seq(v.tensor_tensor(den[:, :, :], own[:, :, H:2 * H], other[:, :, H:2 * H], ALU.add))
                        for t in range(NT):
                            hs = lambda tile: tile[:, t, 2 * H:2 * H + F].rearrange("p (h c) -> p h c", c=C)
                            wv = lambda n: wts[:, n, t, :].unsqueeze(2).broadcast_to([P, H, C])
                            c.inc(v.tensor_tensor(hs(own), hs(own), wv(0), ALU.mult))
                            c.inc(v.tensor_tensor(hs(other), hs(other), wv(1), ALU.mult))
                        c.wait()
                        c.seq(v.tensor_tensor(agg[:, :, :], own[:, :, 2 * H:W], other[:, :, 2 * H:W], ALU.add))
                        if n_self:
                            c.seq(v.tensor_tensor(den[:, :, :], den[:, :, :], wts[:, 2, :, :], ALU.add))
                            for t in range(NT):
                                c.inc(v.tensor_tensor(own[:, t, 2 * H:W].rearrange("p (h c) -> p h c", c=C), self_rows[:, t, 0:F].rearrange("p (h c) -> p h c", c=C),
                                                      wts[:, 2, t, :].unsqueeze(2).broadcast_to([P, H, C]), ALU.mult))
                            c.wait()
                            c.seq(v.tensor_tensor(agg[:, :, :], agg[:, :, :], own[:, :, 2 * H:W], ALU.add))
                        c.seq(v.tensor_scalar(den[:, :, :], den[:, :, :], eps or 0.0, 1e-30, ALU.add, ALU.max))
                        c.seq(v.reciprocal(den[:, :, :], den[:, :, :]))
                        for t in range(NT):
                            c.inc(v.tensor_tensor(agg[:, t, :].rearrange("p (h c) -> p h c", c=C), agg[:, t, :].rearrange("p (h c) -> p h c", c=C),
                                                  den[:, t, :].unsqueeze(2).broadcast_to([P, H, C]), ALU.mult))
                        c.wait()

                    @block.tensor
                    def _(pe):
                        pe.wait_ge(diags, 1)
                        for b in range(HB):
                            w = min(4, H + 1 - 4 * b)
                            ins = nc.tensor.matmul(psB[:, b, 0:w * P], ones[:, :], diag[:, 4 * b:4 * b + w, :].rearrange("p h c -> p (h c)"), start=True, stop=True)
                        ins.then_inc(spread, 1)

                        def body(g):
                            for s in range(GT):
                                hold(pe, hots, g * GT + s + 1)
                                if not zero(g) or s >= 2:
                                    hold(pe, taken, g * GT + max(s - 1, 0))
                                nc.tensor.matmul(psA[:, s % 2, 0:CW], oh[:, s, :], tw_rows[:, :], start=True, stop=True).then_inc(tailed, 1)
                        loop(pe, NG, body)

                    @block.scalar
                    def _(act):
                        act.wait_ge(targ, 1)
                        a.activation(tw[:, :], tw[:, :], ACT.Exp).then_inc(texp, 1)
                        act.wait_ge(warg, 1)
                        n = 2 + n_self
                        a.activation(wts[:, 0:n, :, :].rearrange("p n t h -> p (n t h)"), wts[:, 0:n, :, :].rearrange("p n t h -> p (n t h)"), ACT.Exp).then_inc(wexp, 1)

        def gat_phase(HG, self_score, agg):
            H, F, W = 4, 16, 24
            ctx, sb, ps, sem = phase()
            with ctx:
                att = sb("att", [P, 2, F])
                prod = sb("prod", [P, NT, F])
                zeros = sb("zeros", [P, NJ2 * H])
                att_in, chain, cleared, blank, stored, moved = (sem(n) for n in ("att_in", "chain", "cleared", "blank", "stored", "moved"))
                with nc.Block() as block:
                    @block.sync
                    def _(sp):
                        for n, dr in enumerate((f0_att_src, f0_att_dst)):
                            sp.dma_start(att[:, n, :], dr.rearrange("h e -> (h e)").partition_broadcast(P)).then_inc(att_in, 16)
                        sp.wait_ge(cleared, 1)
                        sp.dma_start(adst_tab[0:E2, :].rearrange("(p j) w -> p (j w)", j=NJ2), zeros[:, :]).then_inc(blank, 16)
                        sp.wait_ge(chain, 6)
                        sp.dma_start(table_rows(h_tab), HG[:, :, :]).then_inc(stored, 16)
                        sp.wait_ge(stored, 16)

                    @block.vector
                    def _(dve):
                        c = Count(dve, chain)
                        v.memset(zeros[:, :], 0.0).then_inc(cleared, 1)
                        dve.wait_ge(att_in, 32)
                        for n in range(2):
                            c.seq(v.tensor_tensor(prod[:, :, :], HG[:, :, 0:F], att[:, n, :].unsqueeze(1).broadcast_to([P, NT, F]), ALU.mult))
                            c.seq(v.tensor_reduce(HG[:, :, F + H * n:F + H * (n + 1)], prod[:, :, :].rearrange("p t (h c) -> p t h c", h=H), AX, ALU.add))
                        c.seq(v.tensor_tensor(self_score[:, :, :], HG[:, :, F:F + H], HG[:, :, F + H:F + 2 * H], ALU.add))
                        c.seq(v.scalar_tensor_tensor(self_score[:, :, :], self_score[:, :, :], 0.2, self_score[:, :, :], ALU.mult, ALU.max))

                    @block.gpsimd
                    def _(pool):
                        pool.wait_ge(blank, 16)
                        pool.wait_ge(chain, 4)
                        for t in range(NT):
                            pool.indirect_dma_start(out=adst_tab, out_offset=bass.IndirectOffsetOnAxis(ap=first2[:, t:t + 1], axis=0),
                                                    in_=HG[:, t, F + H:W], in_offset=None).then_inc(moved, 16)
                        pool.wait_ge(moved, 16 * NT)
            ctx, sb, ps, sem = phase()
            with ctx:
                hs, hd, adst = sb("hs", [P, 2, J2, W]), sb("hd", [P, W]), sb("adst", [P, NJ2, H])
                iS = sb("iS", [P, 2, J2], I32)
                feat, score = sb("feat", [P, F, NJ2]), sb("score", [P, H, NJ2])
                M, AE = sb("M", [P, H, NJ2 + 1]), sb("AE", [P, 2, H, NJ2])
                ST = sb("ST", [P, NJ2, W])
                got = [sem("got0"), sem("got1")]
                first_in, adst_in = sem("first_in"), sem("adst_in")
                staged, spread, args, exps, states, stored, chain = (sem(n) for n in ("staged", "spread", "args", "exps", "states", "stored", "chain"))
                with nc.Block() as block:
                    @block.gpsimd
                    def _(pool):
                        pool.indirect_dma_start(out=hd[:, :], out_offset=None, in_=h_tab,
                                                in_offset=bass.IndirectOffsetOnAxis(ap=dst2[:, 0:1], axis=0)).then_inc(first_in, 16)

                        def body(i):
                            for s in range(2):
                                if not zero(i):
                                    hold(pool, spread, 2 * i + s - 1)
                                cols = bass.ds((2 * i + s) * J2, J2)
                                nc.gpsimd.tensor_copy(iS[:, s, :], src2[:, cols]).then_inc(staged, 1)
                                hold(pool, staged, 2 * i + s + 1)
                                for j in range(J2):
                                    pool.indirect_dma_start(out=hs[:, s, j, :], out_offset=None, in_=h_tab,
                                                            in_offset=bass.IndirectOffsetOnAxis(ap=iS[:, s, j:j + 1], axis=0)).then_inc(got[s], 16)
                        loop(pool, NB2 // 2, body)

                    @block.vector
                    def _(dve):
                        c = Count(dve, chain)
                        dve.wait_ge(first_in, 16)
                        dve.wait_ge(adst_in, 16)
                        c.seq(v.tensor_copy(adst[:, 0, :], hd[:, F + H:W]))
                        for h in range(H):
                            c.inc(v.tensor_tensor_scan(score[:, h, :], keep2[:, :], adst[:, :, h], 0.0, ALU.mult, ALU.add))
                        c.wait()
                        with dve.Fori(0, NB2 // 2) as i:
                            for s in range(2):
                                cols = bass.ds((2 * i + s) * J2, J2)
                                hold(dve, got[s], 16 * J2 * (i + 1))
                                v.tensor_copy(feat[:, :, cols], hs[:, s, :, 0:F].rearrange("p j f -> p f j"))
                                v.tensor_tensor(score[:, :, cols], hs[:, s, :, F:F + H].rearrange("p j f -> p f j"),
                                                score[:, :, cols], ALU.add).then_inc(spread, 1)
                        dve.wait_ge(spread, NB2)
                        c.seq(v.scalar_tensor_tensor(score[:, :, :], score[:, :, :], 0.2, score[:, :, :], ALU.mult, ALU.max))
                        c.seq(v.memset(M[:, :, 0:1], -BIG))
                        for h in range(H):
                            c.inc(v.tensor_tensor_scan(M[:, h, 1:NJ2 + 1], pen2[:, :], score[:, h, :], -BIG, ALU.add, ALU.max))
                        c.wait()
                        c.inc(v.tensor_tensor(AE[:, 0, :, :], M[:, :, 0:NJ2], pen2[:, :].unsqueeze(1).broadcast_to([P, H, NJ2]), ALU.add))
                        c.seq(v.tensor_tensor(AE[:, 1, :, :], score[:, :, :], M[:, :, 1:NJ2 + 1], ALU.subtract))
                        c.seq(v.tensor_tensor(AE[:, 0, :, :], AE[:, 0, :, :], M[:, :, 1:NJ2 + 1], ALU.subtract))
                        dve.sem_inc(args, 1)
                        c.inc(v.tensor_copy(ST[:, :, 0:H], M[:, :, 1:NJ2 + 1].rearrange("p h j -> p j h")))
                        dve.wait_ge(exps, 1)
                        for h in range(H):
                            c.inc(v.tensor_tensor(feat[:, 4 * h:4 * h + 4, :], feat[:, 4 * h:4 * h + 4, :],
                                                  AE[:, 1, h, :].unsqueeze(1).broadcast_to([P, 4, NJ2]), ALU.mult))
                            c.inc(v.tensor_tensor_scan(ST[:, :, H + h], AE[:, 0, h, :], AE[:, 1, h, :], 0.0, ALU.mult, ALU.add))
                        c.wait()
                        for f in range(F):
                            c.inc(v.tensor_tensor_scan(ST[:, :, 2 * H + f], AE[:, 0, f // 4, :], feat[:, f, :], 0.0, ALU.mult, ALU.add))
                        c.wait()
                        dve.sem_inc(states, 1)

                    @block.scalar
                    def _(act):
                        act.wait_ge(args, 1)
                        flat = AE[:, :, :, :].rearrange("p n h j -> p (n h j)")
                        a.activation(flat, flat, ACT.Exp).then_inc(exps, 1)

                    @block.sync
                    def _(sp):
                        sp.dma_start(adst[:, :, :], adst_tab[0:E2, :].rearrange("(p j) w -> p j w", j=NJ2)).then_inc(adst_in, 16)
                        sp.wait_ge(states, 1)
                        sp.dma_start(gat_tab[0:E2, :].rearrange("(p j) w -> p j w", j=NJ2), ST[:, :, :]).then_inc(stored, 16)
                        sp.wait_ge(stored, 16)
                merge_phase(H, F, ST[:, NJ2 - 1, :], cont2, end2, gat_tab, agg, self_score[:, :, :], HG, 1e-16)

        def router_phase(agg, SC):
            F = 16
            ctx, sb, ps, sem = phase()
            with ctx:
                prm = sb("prm", [P, 3, F])
                mu, var, sq = sb("mu", [P, NT]), sb("var", [P, NT]), sb("sq", [P, NT, F])
                prm_in, vars_, rooted, chain = sem("prm_in"), sem("vars"), sem("rooted"), sem("chain")
                with nc.Block() as block:
                    @block.sync
                    def _(sp):
                        for n, dr in enumerate((f0_bgat, f0_lng, f0_lnb)):
                            sp.dma_start(prm[:, n, :], dr.partition_broadcast(P)).then_inc(prm_in, 16)

                    @block.vector
                    def _(dve):
                        c = Count(dve, chain)
                        A = agg[:, :, :]
                        par = lambda n: prm[:, n, :].unsqueeze(1).broadcast_to([P, NT, F])
                        tok = lambda t: t[:, :].unsqueeze(2).broadcast_to([P, NT, F])
                        dve.wait_ge(prm_in, 48)
                        c.seq(v.tensor_tensor(A, A, par(0), ALU.add))
                        c.seq(v.tensor_reduce(mu[:, :], A, AX, ALU.add))
                        c.seq(v.tensor_scalar(mu[:, :], mu[:, :], 1.0 / F, None, ALU.mult))
                        c.seq(v.tensor_tensor(A, A, tok(mu), ALU.subtract))
                        c.seq(v.tensor_tensor(sq[:, :, :], A, A, ALU.mult))
                        c.seq(v.tensor_reduce(var[:, :], sq[:, :, :], AX, ALU.add))
                        dve.sem_inc(vars_, 1)
                        dve.wait_ge(rooted, 1)
                        c.seq(v.reciprocal(var[:, :], var[:, :]))
                        c.seq(v.tensor_tensor(A, A, tok(var), ALU.mult))
                        c.seq(v.tensor_tensor(A, A, par(1), ALU.mult))
                        c.seq(v.tensor_tensor(A, A, par(2), ALU.add))
                        c.seq(v.tensor_reduce(SC[:, :, :], A.rearrange("p t (h e) -> p t e h", h=4), AX, ALU.add))
                        c.seq(v.tensor_scalar(SC[:, :, :], SC[:, :, :], 0.25, None, ALU.mult))

                    @block.scalar
                    def _(act):
                        act.wait_ge(vars_, 1)
                        a.activation(var[:, :], var[:, :], ACT.Sqrt, bias=eps_col[:, :], scale=1.0 / F).then_inc(rooted, 1)

        def gate_phase(SC, E, G, chosen=None, weight=None):
            ctx, sb, ps, sem = phase()
            with ctx:
                t1, mask = sb("t1", [P, NT, E]), [sb("mask0", [P, NT, E]), sb("mask1", [P, NT, E])]
                m, first = sb("m", [P, 2, NT]), sb("first", [P, NT])
                e2, w = sb("e2", [P, NT]), weight if weight is not None else sb("w", [P, 2, NT])
                arg, exped, chain = sem("arg"), sem("exped"), sem("chain")
                with nc.Block() as block:
                    @block.vector
                    def _(dve):
                        c = Count(dve, chain)
                        over = lambda t: t.unsqueeze(2).broadcast_to([P, NT, E])
                        numbers = iota_free[:, 0:E].unsqueeze(1).broadcast_to([P, NT, E])
                        for n in range(2):
                            c.seq(v.tensor_reduce(m[:, n, :], SC[:, :, :], AX, ALU.max))
                            c.seq(v.tensor_tensor(t1[:, :, :], SC[:, :, :], over(m[:, n, :]), ALU.is_equal))
                            c.seq(v.scalar_tensor_tensor(t1[:, :, :], t1[:, :, :], -float(P), numbers, ALU.mult, ALU.add))
                            c.seq(v.tensor_reduce(first[:, :], t1[:, :, :], AX, ALU.min))
                            c.seq(v.tensor_tensor(mask[n][:, :, :], t1[:, :, :], over(first[:, :]), ALU.is_equal))
                            if n == 0:
                                c.seq(v.scalar_tensor_tensor(SC[:, :, :], mask[n][:, :, :], -BIG, SC[:, :, :], ALU.mult, ALU.add))
                        c.seq(v.tensor_tensor(e2[:, :], m[:, 1, :], m[:, 0, :], ALU.subtract))
                        dve.sem_inc(arg, 1)
                        if chosen is not None:
                            for n in range(2):
                                c.inc(v.tensor_copy(chosen[:, n, :, :], mask[n][:, :, :]))
                        dve.wait_ge(exped, 1)
                        c.seq(v.tensor_scalar(w[:, 0, :], e2[:, :], 1.0, None, ALU.add))
                        c.seq(v.reciprocal(w[:, 0, :], w[:, 0, :]))
                        c.seq(v.tensor_tensor(w[:, 1, :], w[:, 0, :], e2[:, :], ALU.mult))
                        for n in range(2):
                            c.seq(v.tensor_tensor(mask[n][:, :, :], mask[n][:, :, :], over(w[:, n, :]), ALU.mult))
                        c.seq(v.tensor_tensor(G[:, :, :].rearrange("p e t -> p t e"), mask[0][:, :, :], mask[1][:, :, :], ALU.add))

                    @block.scalar
                    def _(act):
                        act.wait_ge(arg, 1)
                        a.activation(e2[:, :], e2[:, :], ACT.Exp).then_inc(exped, 1)

        def biases_phase(E, G, b1, b2, b1T, acc, table=None):
            FC = b1.shape[1] // P
            ctx, sb, ps, sem = phase()
            with ctx:
                b1r = sb("b1r", [E * FC, P])
                b2s, gS, gT = sb("b2s", [E, D]), sb("gS", [P, GT, E]), sb("gT", [E, GT, P])
                psG, psA = ps("psG", [P, 2, 512]), ps("psA", [P, 2, 512])
                stored = sem("stored")
                b_in, b1_turned, gs, turned, gts, biased, added, chain = (
                    sem(n) for n in ("b_in", "b1_turned", "gs", "turned", "gts", "biased", "added", "chain"))
                with nc.Block() as block:
                    @block.sync
                    def _(sp):
                        sp.dma_start(b1r[:, :], b1.rearrange("e (c p) -> (e c) p", p=P)).then_inc(b_in, 16)
                        sp.dma_start(b2s[:, :], b2).then_inc(b_in, 16)
                        if table is not None:
                            with sp.Fori(0, NG) as g:
                                hold(sp, added, (g + 1) * GT)
                                sp.dma_start(table_rows(table)[:, bass.ds(g * GT, GT), :], acc[:, bass.ds(g * GT, GT), :]).then_inc(stored, 16)
                            sp.wait_ge(stored, 16 * NG)

                    @block.tensor
                    def _(pe):
                        pe.wait_ge(b_in, 32)
                        nc.tensor.transpose(psA[:, 0, 0:E * FC], b1r[:, :], ident[0:E * FC, 0:E * FC]).then_inc(b1_turned, 1)
                        pe.wait_ge(chain, 1)

                        def body(g):
                            for s in range(GT):
                                hold(pe, gs, g + 1)
                                if not zero(g) or s >= 2:
                                    hold(pe, gts, g * GT + max(s - 1, 0))
                                nc.tensor.transpose(psG[0:E, s % 2, 0:P], gS[:, s, :], ident[:, :]).then_inc(turned, 1)
                            for s in range(GT):
                                hold(pe, gts, g * GT + s + 1)
                                if not zero(g) or s >= 2:
                                    hold(pe, added, g * GT + max(s - 1, 0))
                                nc.tensor.matmul(psA[:, s % 2, 0:D], gT[:, s, :], b2s[:, :], start=True, stop=True).then_inc(biased, 1)
                        loop(pe, NG, body)

                    @block.scalar
                    def _(act):
                        def body(g):
                            for s in range(GT):
                                hold(act, turned, g * GT + s + 1)
                                if not zero(g):
                                    hold(act, biased, g * GT)
                                a.copy(gT[:, s, :], psG[0:E, s % 2, 0:P]).then_inc(gts, 1)
                        loop(act, NG, body)

                    @block.vector
                    def _(dve):
                        dve.wait_ge(b1_turned, 1)
                        v.tensor_copy(b1T[:, :], psA[:, 0, 0:E * FC]).then_inc(chain, 1)
                        dve.wait_ge(chain, 1)

                        def body(g):
                            if not zero(g):
                                hold(dve, turned, g * GT)
                            v.tensor_copy(gS[:, :, :], G[:, :, bass.ds(g * GT, GT)].rearrange("p e t -> p t e")).then_inc(gs, 1)
                            for s in range(GT):
                                hold(dve, biased, g * GT + s + 1)
                                v.tensor_tensor(row(acc, g * GT + s), psA[:, s % 2, 0:D], row(acc, g * GT + s), ALU.add).then_inc(added, 1)
                        loop(dve, NG, body)

        def dense_experts_phase(E, func, XNT, G, w1, w2, b1T, acc):
            FF = w1.shape[2]
            FC = FF // P
            HN = GT * P // 2
            PAIRS, IT = E // 2, 2 * NG
            ctx, sb, ps, sem = phase()
            with ctx:
                W1s, W2s = sb("W1s", [P, 2, 2, FF]), sb("W2s", [P, 2, FC, D])
                hT = sb("hT", [P, 2, FC, GT * P])
                psH4 = [ps("psHa", [P, 2, 512]), ps("psHb", [P, 2, 512])]
                psY = ps("psY", [P, 3, 512])
                w_in = [sem("w_in0"), sem("w_in1")]
                hidden, acted, rows_out, rows_read = sem("hidden"), sem("acted"), sem("rows_out"), sem("rows_read")
                with nc.Block() as block:
                    @block.sync
                    def _(sp):
                        def body(i):
                            for s in range(2):
                                if not zero(i):
                                    hold(sp, rows_out, NT * (2 * i + s - 1))
                                sp.dma_start(W1s[:, s, :, :], w1[bass.ds(2 * i + s, 1), :, :].rearrange("a (k p) f -> p (a k) f", p=P)).then_inc(w_in[s], 16)
                                sp.dma_start(W2s[:, s, :, :], w2[bass.ds(2 * i + s, 1), :, :].rearrange("a (c p) d -> p (a c) d", p=P)).then_inc(w_in[s], 16)
                        loop(sp, PAIRS, body)

                    def passes(eng, body):
                        body(0, PAIRS == 1)
                        if PAIRS > 2:
                            with eng.Fori(1, PAIRS - 1) as i:
                                body(i, False)
                        if PAIRS > 1:
                            body(PAIRS - 1, True)

                    @block.tensor
                    def _(pe):
                        def up(i, n):
                            s, g = n // NG, n % NG
                            if g == 0:
                                hold(pe, w_in[s], 32 * (i + 1))
                            for f in range(FC):
                                if f >= 2 or n or not zero(i):
                                    hold(pe, acted, (i * IT + n) * FC + f - 1)
                                for hf in range(2):
                                    for k in range(2):
                                        ins = nc.tensor.matmul(psH4[f % 2][:, hf, 0:HN], W1s[:, s, k, f * P:(f + 1) * P],
                                                               XNT[:, g, k, hf * HN:(hf + 1) * HN], start=(k == 0), stop=(k == 1))
                                ins.then_inc(hidden, 1)

                        def down(i, n):
                            s, g = n // NG, n % NG
                            hold(pe, acted, (i * IT + n + 1) * FC)
                            for t in range(GT):
                                if t >= 2 or n or not zero(i):
                                    hold(pe, rows_read, (i * IT + n) * GT + t - 1)
                                for f in range(FC):
                                    ins = nc.tensor.matmul(psY[:, t % 3, 0:D], hT[:, n % 2, f, t * P:(t + 1) * P], W2s[:, s, f, :],
                                                           start=(f == 0), stop=(f == FC - 1))
                                ins.then_inc(rows_out, 1)
                        up(0, 0)

                        def body(i, last):
                            for n in range(IT):
                                if n + 1 < IT:
                                    up(i, n + 1)
                                elif not last:
                                    up(i + 1, 0)
                                down(i, n)
                        passes(pe, body)

                    @block.scalar
                    def _(act):
                        def body(i, last):
                            for n in range(IT):
                                s = n // NG
                                if n >= 2 or not zero(i):
                                    hold(act, rows_out, (i * IT + n - 1) * GT)
                                for f in range(FC):
                                    hold(act, hidden, (i * IT + n) * FC + f + 1)
                                    a.activation(hT[:, n % 2, f, :].rearrange("p (a c) -> p a c", a=2), psH4[f % 2][:, :, 0:HN], func,
                                                 bias=b1T[:, bass.ds((2 * i + s) * FC + f, 1)]).then_inc(acted, 1)
                        passes(act, body)

                    @block.vector
                    def _(dve):
                        def body(i, last):
                            for n in range(IT):
                                s, g = n // NG, n % NG
                                for t in range(GT):
                                    hold(dve, rows_out, (i * IT + n) * GT + t + 1)
                                    o = acc[:, g * GT + t, :]
                                    gate = G[:, bass.ds(2 * i + s, 1), g * GT + t:g * GT + t + 1].rearrange("p a b -> p (a b)")
                                    v.scalar_tensor_tensor(o, psY[:, t % 3, 0:D], gate, o, ALU.mult, ALU.add).then_inc(rows_read, 1)
                        passes(dve, body)

        E3, FF3 = f1_w1.shape[0], f1_w1.shape[2]
        FC3 = FF3 // P
        MAX_BLOCKS = (2 * N + E3 * (P - 1)) // P
        SLOTS = 4
        assert MAX_BLOCKS % SLOTS == 0
        disp_tab = sum_tab
        y_tab = dram("y_tab", [MAX_BLOCKS * P, D])

        def load_experts_phase(W1r, W2r):
            ctx, sb, ps, sem = phase()
            with ctx:
                with nc.Block() as block:
                    @block.scalar
                    def _(act):
                        for k in range(2):
                            act.dma_start(W1r[:, k, :, :], f1_w1[:, k * P:(k + 1) * P, :].rearrange("e p f -> p e f")).then_inc(weights_in, 16)
                        for f in range(FC3):
                            act.dma_start(W2r[:, f, :, :], f1_w2[:, f * P:(f + 1) * P, :].rearrange("e p d -> p e d")).then_inc(weights_in, 16)

        def dispatch_phase(chosen, XNR, pos_out, block_expert):
            E = E3
            ctx, sb, ps, sem = phase()
            with ctx:
                both, tot, cum, S = (sb(n, [P, E, NT]) for n in ("both", "tot", "cum", "S"))
                psI, psTot = ps("psI", [P, 512]), ps("psTot", [P, 512])
                valid, pad_row, k128 = sb("valid", [P, 1]), sb("pad_row", [P, 2]), sb("k128", [P, NT])
                cnt, blocks, last, off = (sb(n, [P, E]) for n in ("cnt", "blocks", "last", "off"))
                pf, pos, pick = sb("pf", [P, 2, NT]), sb("pos", [P, 2, NT], I32), sb("pick", [P, NT, E])
                passed, bf = sb("passed", [P, MAX_BLOCKS + 2, E]), sb("bf", [P, MAX_BLOCKS + 2])
                chain, marked, summed, placed, moved = (sem(n) for n in ("chain", "marked", "summed", "placed", "moved"))
                flat = lambda t: t.rearrange("p e t -> p (e t)")
                over_t = lambda t: t.unsqueeze(2).broadcast_to([P, E, NT])
                with nc.Block() as block:
                    @block.tensor
                    def _(pe):
                        pe.wait_ge(marked, 1)
                        nc.tensor.matmul(psI[:, 0:E * NT], upper[:, :], flat(both[:, :, :]), start=True, stop=True)
                        nc.tensor.matmul(psTot[:, 0:E * NT], ones[:, :], flat(both[:, :, :]), start=True, stop=True).then_inc(summed, 1)

                    @block.vector
                    def _(dve):
                        c = Count(dve, chain)
                        c.seq(v.tensor_scalar(valid[:, :], iota_part[:, :], float(TAIL_ROWS), None, ALU.is_lt))
                        for n in range(2):
                            c.inc(v.tensor_scalar(chosen[:, n, NT - 1, :], chosen[:, n, NT - 1, :], valid[:, 0:1], None, ALU.mult))
                        for n in range(2):
                            c.inc(v.tensor_scalar(pad_row[:, n:n + 1], iota_part[:, :], float((MAX_BLOCKS + n) * P + 1), None, ALU.add))
                        c.inc(v.tensor_scalar(k128[:, :], iota_free[:, 0:NT], float(P), None, ALU.mult))
                        c.wait()
                        c.inc(v.tensor_scalar(valid[:, :], valid[:, :], 0.5, None, ALU.is_lt))
                        c.seq(v.tensor_tensor(both[:, :, :].rearrange("p e t -> p t e"), chosen[:, 0, :, :], chosen[:, 1, :, :], ALU.add))
                        dve.sem_inc(marked, 1)
                        c.inc(v.tensor_scalar(pad_row[:, :], pad_row[:, :], valid[:, 0:1], None, ALU.mult))
                        dve.wait_ge(summed, 1)
                        c.seq(v.tensor_copy(flat(tot[:, :, :]), psTot[:, 0:E * NT]))
                        c.inc(v.tensor_tensor_scan(flat(cum[:, :, :]), flat(tot[:, :, :]), flat(tot[:, :, :]), 0.0, ALU.add, ALU.max))
                        c.seq(v.tensor_reduce(cnt[:, :], tot[:, :, :], AX, ALU.add))
                        c.seq(v.tensor_tensor(S[:, :, :], over_t(cnt[:, :]), k128[:, :].unsqueeze(1).broadcast_to([P, E, NT]), ALU.is_gt))
                        c.seq(v.tensor_reduce(blocks[:, :], S[:, :, :], AX, ALU.add))
                        c.seq(v.tensor_tensor_scan(last[:, :], blocks[:, :], blocks[:, :], 0.0, ALU.add, ALU.max))
                        c.seq(v.tensor_tensor(off[:, :], last[:, :], blocks[:, :], ALU.subtract))
                        c.seq(v.scalar_tensor_tensor(off[:, :], off[:, :], float(P), cnt[:, :], ALU.mult, ALU.add))
                        c.seq(v.tensor_tensor(off[:, :], off[:, :], cum[:, :, NT - 1], ALU.subtract))
                        c.inc(v.tensor_tensor(tot[:, :, :], cum[:, :, :], tot[:, :, :], ALU.subtract))
                        c.seq(v.tensor_tensor(S[:, :, :], over_t(off[:, :]), psI[:, 0:E * NT].rearrange("p (e t) -> p e t", t=NT), ALU.add))
                        c.seq(v.tensor_tensor(S[:, :, :], S[:, :, :], tot[:, :, :], ALU.add))
                        for n in range(2):
                            c.seq(v.tensor_tensor(pick[:, :, :], S[:, :, :].rearrange("p e t -> p t e"), chosen[:, n, :, :], ALU.mult))
                            c.seq(v.tensor_reduce(pf[:, n, :], pick[:, :, :], AX, ALU.add))
                            c.seq(v.tensor_tensor(pf[:, n, NT - 1:NT], pf[:, n, NT - 1:NT], pad_row[:, n:n + 1], ALU.add))
                        c.seq(v.tensor_scalar(pf[:, :, :], pf[:, :, :], -1.0, 0.0, ALU.add, ALU.max))
                        c.seq(v.tensor_copy(pos[:, :, :], pf[:, :, :]))
                        dve.sem_inc(placed, 1)
                        c.seq(v.tensor_scalar(pf[:, :, :], pf[:, :, :], float(MAX_BLOCKS * P - 1), None, ALU.min))
                        c.inc(v.tensor_copy(pos_out[:, :, :], pf[:, :, :]))
                        KB = MAX_BLOCKS + 2
                        c.seq(v.tensor_tensor(passed[:, :, :], iota_free[:, 0:KB].unsqueeze(2).broadcast_to([P, KB, E]),
                                              last[:, :].unsqueeze(1).broadcast_to([P, KB, E]), ALU.is_ge))
                        c.seq(v.tensor_reduce(bf[:, :], passed[:, :, :], AX, ALU.add))
                        c.seq(v.tensor_scalar(bf[:, :], bf[:, :], float(E - 1), None, ALU.min))
                        c.seq(v.tensor_copy(block_expert[:, :], bf[:, :]))

                    @block.gpsimd
                    def _(pool):
                        pool.wait_ge(placed, 1)
                        for t in range(NT):
                            for n in range(2):
                                pool.indirect_dma_start(out=disp_tab, out_offset=bass.IndirectOffsetOnAxis(ap=pos[:, n, t:t + 1], axis=0),
                                                        in_=XNR[:, t, :], in_offset=None).then_inc(moved, 16)
                        pool.wait_ge(moved, 16 * 2 * NT)

        def sparse_experts_phase(block_expert, W1r, W2r, b1T):
            KB, S = MAX_BLOCKS, SLOTS
            PASSES = KB // S
            ctx, sb, ps, sem = phase()
            with ctx:
                xb, xT, w1c = sb("xb", [P, S, D]), sb("xT", [P, 2, 2, P]), sb("w1c", [P, 2, 2, FF3])
                hT, yb = sb("hT", [P, 2, FC3, P]), sb("yb", [P, S, D])
                psX, psH, psY = ps("psX", [P, 2, 512]), ps("psH", [P, 2, 512]), ps("psY", [P, 2, 512])
                x_in, y_out = [sem(f"x_in{s}") for s in range(S)], [sem(f"y_out{s}") for s in range(S)]
                turned, columns, w1_copied, hidden, acted, rows_out, rows_read = (
                    sem(n) for n in ("turned", "columns", "w1_copied", "hidden", "acted", "rows_out", "rows_read"))
                disp_rows = disp_tab[0:(KB + S) * P, :].rearrange("(k p) d -> p k d", p=P)
                y_rows = table_rows(y_tab)

                def after(eng, sem_, value):
                    if not isinstance(value, int) or value > 0:
                        hold(eng, sem_, value)

                with nc.Block() as block:
                    @block.sync
                    def _(sp):
                        def load(k, s, turns):
                            sp.dma_start(xb[:, s, :], disp_rows[:, bass.ds(k, 1), :].rearrange("p a d -> p (a d)")).then_inc(x_in[s], 16)
                        for s in range(S):
                            load(s, s, 0)
                        with sp.Fori(0, PASSES) as i:
                            for s in range(S):
                                sp.wait_ge(turned, S * i + s + 1)
                                load(S * i + s + S, s, i)
                                sp.wait_ge(rows_read, S * i + s + 1)
                                sp.dma_start(y_rows[:, bass.ds(S * i + s, 1), :].rearrange("p a d -> p (a d)"), yb[:, s, :]).then_inc(y_out[s], 16)
                        for s in range(S):
                            sp.wait_ge(y_out[s], 16 * PASSES)
                            sp.wait_ge(x_in[s], 16 * (PASSES + 1))

                    @block.tensor
                    def _(pe):
                        def turn(k, s, i):
                            hold(pe, x_in[s], 16 * (i + 1))
                            after(pe, columns, k - 1)
                            nc.tensor.transpose(psX[:, s % 2, 0:P], xb[:, s, 0:P], ident[:, :])
                            nc.tensor.transpose(psX[:, s % 2, P:D], xb[:, s, P:D], ident[:, :]).then_inc(turned, 1)

                        def up(k, s):
                            hold(pe, columns, k + 1)
                            hold(pe, w1_copied, k + 1)
                            after(pe, acted, k - 1)
                            for f in range(FC3):
                                for c in range(2):
                                    ins = nc.tensor.matmul(psH[:, s % 2, f * P:(f + 1) * P], w1c[:, s % 2, c, f * P:(f + 1) * P],
                                                           xT[:, s % 2, c, :], start=(c == 0), stop=(c == 1))
                            ins.then_inc(hidden, 1)

                        def down(k, s):
                            e = pe.value_load(block_expert[0:1, bass.ds(k, 1)], min_val=0, max_val=E3 - 1)
                            hold(pe, acted, k + 1)
                            after(pe, rows_read, k - 1)
                            for f in range(FC3):
                                ins = nc.tensor.matmul(psY[:, s % 2, 0:D], hT[:, s % 2, f, :], W2r[:, f, bass.ds(e, 1), :].rearrange("p a d -> p (a d)"),
                                                       start=(f == 0), stop=(f == FC3 - 1))
                            ins.then_inc(rows_out, 1)
                        turn(0, 0, 0)
                        turn(1, 1, 0)
                        pe.wait_ge(weights_in, 16 * (2 + FC3))
                        up(0, 0)

                        def body(i):
                            for s in range(S):
                                k = S * i + s
                                up(k + 1, (s + 1) % S)
                                turn(k + 2, (s + 2) % S, i if s + 2 < S else i + 1)
                                down(k, s)
                        loop(pe, PASSES, body)

                    @block.scalar
                    def _(act):
                        def relu(k, s):
                            e = act.value_load(block_expert[0:1, bass.ds(k, 1)], min_val=0, max_val=E3 - 1)
                            hold(act, hidden, k + 1)
                            after(act, rows_out, k - 1)
                            for f in range(FC3):
                                ins = a.activation(hT[:, s % 2, f, :], psH[:, s % 2, f * P:(f + 1) * P], ACT.Relu, bias=b1T[:, bass.ds(e * FC3 + f, 1)])
                            ins.then_inc(acted, 1)
                        relu(0, 0)

                        def body(i):
                            for s in range(S):
                                relu(S * i + s + 1, (s + 1) % S)
                        loop(act, PASSES, body)

                    @block.vector
                    def _(dve):
                        def first_weights(k, s):
                            e = dve.value_load(block_expert[0:1, bass.ds(k, 1)], min_val=0, max_val=E3 - 1)
                            after(dve, hidden, k - 1)
                            v.tensor_copy(w1c[:, s % 2, :, :], W1r[:, :, bass.ds(e, 1), :].rearrange("p c a f -> p c (a f)")).then_inc(w1_copied, 1)

                        def spread(k, s):
                            hold(dve, turned, k + 1)
                            after(dve, hidden, k - 1)
                            v.tensor_copy(xT[:, s % 2, :, :].rearrange("p c t -> p (c t)"), psX[:, s % 2, 0:D]).then_inc(columns, 1)
                        dve.wait_ge(weights_in, 16 * (2 + FC3))
                        for k in range(2):
                            spread(k, k)
                            first_weights(k, k)

                        def body(i):
                            for s in range(S):
                                k = S * i + s
                                first_weights(k + 2, (s + 2) % S)
                                spread(k + 2, (s + 2) % S)
                                hold(dve, rows_out, k + 1)
                                if not zero(i):
                                    hold(dve, y_out[s], 16 * i)
                                v.tensor_copy(yb[:, s, :], psY[:, s % 2, 0:D]).then_inc(rows_read, 1)
                        loop(dve, PASSES, body)

        def combine_phase(pos, weight, ACC):
            ctx, sb, ps, sem = phase()
            with ctx:
                Y = sb("Y", [P, 2, NT, D])
                rows_in, chain = sem("rows_in"), sem("chain")
                got = [sem(f"got{g}") for g in range(NG)]
                with nc.Block() as block:
                    @block.sync
                    def _(sp):
                        sp.dma_start(ACC[:, :, :], table_rows(xn_tab)).then_inc(rows_in, 16)

                    @block.gpsimd
                    def _(pool):
                        for t in range(NT):
                            for n in range(2):
                                pool.indirect_dma_start(out=Y[:, n, t, :], out_offset=None, in_=y_tab,
                                                        in_offset=bass.IndirectOffsetOnAxis(ap=pos[:, n, t:t + 1], axis=0)).then_inc(got[t // GT], 16)

                    @block.vector
                    def _(dve):
                        c = Count(dve, chain)
                        dve.wait_ge(rows_in, 16)
                        for g in range(NG):
                            dve.wait_ge(got[g], 16 * 2 * GT)
                            for n in range(2):
                                for t in range(g * GT, (g + 1) * GT):
                                    c.inc(v.scalar_tensor_tensor(ACC[:, t, :], Y[:, n, t, :], weight[:, n, t:t + 1], ACC[:, t, :], ALU.mult, ALU.add))
                                c.wait()

        def attention_phase(tails):
            H, DH = 8, 32
            W = 2 * H + D
            SCALE = DH ** -0.5
            ctx, sb, ps, sem = phase()
            with ctx:
                Q, KV = sb("Q", [P, 2, J1, D]), sb("KV", [P, 2, J1, 2 * D])
                ST, q0 = sb("ST", [P, 2, J1, W]), sb("q0", [P, D])
                S, pen, M = sb("S", [P, 2, H, J1 + 1]), sb("pen", [P, 2, H, J1 + 1]), sb("M", [P, 2, H, J1 + 1])
                AE, L = sb("AE", [P, 2, 2, H, J1 + 1]), sb("L", [P, 2, H, J1 + 1])
                VT, decay = sb("VT", [P, H, DH, J1 + 1]), sb("decay", [P, H, DH, J1 + 1])
                same = sb("same", [P, 2, J1])
                new, newS = sb("new", [P, NJ1]), sb("newS", [P, 2, J1])
                iS = sb("iS", [P, 2, J1], I32)
                got, stored, q_in = ([sem(f"{n}{s}") for s in range(2)] for n in ("got", "stored", "q_in"))
                first_in, flagged, staged, masked, filled, q_free, args, exps, chain = (
                    sem(n) for n in ("first_in", "flagged", "staged", "masked", "filled", "q_free", "args", "exps", "chain"))
                weighed, carried = sem("weighed"), sem("carried")
                decays, summed, states, sums_out = sem("decays"), sem("summed"), sem("states"), sem("sums_out")
                PASSES = NB1 // 2

                def passes(eng, body):
                    body(0, False)
                    with eng.Fori(1, PASSES - 1) as i:
                        body(i, False)
                    body(PASSES - 1, True)

                with nc.Block() as block:
                    @block.gpsimd
                    def _(pool):
                        pool.indirect_dma_start(out=q0[:, :], out_offset=None, in_=q_tab,
                                                in_offset=bass.IndirectOffsetOnAxis(ap=dst1[:, 0:1], axis=0)).then_inc(first_in, 16)
                        pool.wait_ge(flagged, 1)

                        def gather(b, s):
                            cols = bass.ds(b * J1, J1)
                            nc.gpsimd.tensor_copy(newS[:, s, :], new[:, cols])
                            nc.gpsimd.tensor_copy(same[:, s, :], keep1[:, cols])
                            nc.gpsimd.tensor_copy(iS[:, s, :], src1[:, cols]).then_inc(staged, 1)
                            hold(pool, staged, b + 1)
                            for j in range(J1):
                                pool.indirect_dma_start(out=KV[:, s, j, :], out_offset=None, in_=kv_tab,
                                                        in_offset=bass.IndirectOffsetOnAxis(ap=iS[:, s, j:j + 1], axis=0)).then_inc(got[s], 16)
                        gather(0, 0)

                        def body(i, last):
                            for s in range(2):
                                b = 2 * i + s
                                if s or not zero(i):
                                    hold(pool, weighed, b)
                                    hold(pool, filled, b)
                                if not (last and s == 1):
                                    gather(b + 1, 1 - s)
                                hold(pool, got[s], 16 * J1 * (i + 1))
                                hold(pool, exps, b + 1)
                                if s or not zero(i):
                                    hold(pool, sums_out, b)
                                    hold(pool, carried, b)
                                nc.gpsimd.tensor_tensor(VT[:, :, :, 1:J1 + 1].rearrange("p h c j -> p j h c"),
                                                        KV[:, s, :, D:2 * D].rearrange("p j (h c) -> p j h c", c=DH),
                                                        AE[:, s, 1, :, 1:J1 + 1].rearrange("p h j -> p j h").unsqueeze(3).broadcast_to([P, J1, H, DH]),
                                                        ALU.mult).then_inc(weighed, 1)
                        passes(pool, body)

                    @block.vector
                    def _(dve):
                        c = Count(dve, chain)
                        for s in range(2):
                            c.inc(v.memset(pen[:, s, :, 0:1], -BIG))
                            c.inc(v.memset(AE[:, s, 0, :, 0:1], 0.0))
                        c.inc(v.memset(M[:, 1, :, :], -BIG))
                        c.inc(v.memset(L[:, 1, :, :], 0.0))
                        c.inc(v.memset(VT[:, :, :, 0], 0.0))
                        c.inc(v.memset(decay[:, :, :, 0], 0.0))
                        c.seq(v.memset(keep1[:, 0:1], 1.0))
                        c.seq(v.tensor_scalar(new[:, :], keep1[:, :], -SCALE, SCALE, ALU.mult, ALU.add))
                        dve.wait_ge(first_in, 16)
                        c.seq(v.tensor_scalar(q0[:, :], q0[:, :], SCALE, None, ALU.mult))
                        dve.sem_inc(flagged, 1)
                        flat = lambda t: t.rearrange("p h j -> p (h j)")
                        whole = lambda t: t.rearrange("p h c j -> p (h c j)")

                        def fill(b, s):
                            hold(dve, masked, b + 1)
                            for j in range(J1):
                                prev = q0[:, :] if j == 0 else Q[:, s, j - 1, :]
                                c.seq(v.scalar_tensor_tensor(Q[:, s, j, :], prev, same[:, s, j:j + 1], Q[:, s, j, :], ALU.mult, ALU.add))
                            c.seq(v.tensor_copy(q0[:, :], Q[:, s, J1 - 1, :]))
                            dve.sem_inc(filled, 1)
                        fill(0, 0)

                        def body(i, last):
                            c.at(i, 2 * (15 + J1))
                            for s in range(2):
                                b, o = 2 * i + s, 1 - s
                                cols = bass.ds(b * J1, J1)
                                c.inc(v.tensor_copy(pen[:, s, :, 1:J1 + 1], pen1[:, cols].unsqueeze(1).broadcast_to([P, H, J1])))
                                c.inc(v.tensor_copy(S[:, s, :, 0], M[:, o, :, J1]))
                                hold(dve, got[s], 16 * J1 * (i + 1))
                                c.seq(v.tensor_tensor(KV[:, s, :, 0:D], Q[:, s, :, :], KV[:, s, :, 0:D], ALU.mult))
                                dve.sem_inc(q_free, 1)
                                c.seq(v.tensor_reduce(S[:, s, :, 1:J1 + 1].rearrange("p h j -> p j h"),
                                                      KV[:, s, :, 0:D].rearrange("p j (h c) -> p j h c", c=DH), AX, ALU.add))
                                c.seq(v.tensor_tensor_scan(flat(M[:, s, :, :]), flat(pen[:, s, :, :]), flat(S[:, s, :, :]), -BIG, ALU.add, ALU.max))
                                c.inc(v.tensor_tensor(AE[:, s, 0, :, 1:J1 + 1], M[:, s, :, 0:J1], pen[:, s, :, 1:J1 + 1], ALU.add))
                                c.seq(v.tensor_tensor(AE[:, s, 1, :, 1:J1 + 1], S[:, s, :, 1:J1 + 1], M[:, s, :, 1:J1 + 1], ALU.subtract))
                                c.seq(v.tensor_tensor(AE[:, s, 0, :, 1:J1 + 1], AE[:, s, 0, :, 1:J1 + 1], M[:, s, :, 1:J1 + 1], ALU.subtract))
                                dve.sem_inc(args, 1)
                                if not zero(i):
                                    hold(dve, stored[s], 16 * i)
                                c.inc(v.tensor_copy(ST[:, s, :, 0:H], M[:, s, :, 1:J1 + 1].rearrange("p h j -> p j h")))
                                c.inc(v.tensor_copy(AE[:, s, 1, :, 0], L[:, o, :, J1]))
                                if not (last and s == 1):
                                    fill(b + 1, o)
                                else:
                                    c.wait()
                                hold(dve, exps, b + 1)
                                c.seq(v.tensor_tensor_scan(flat(L[:, s, :, :]), flat(AE[:, s, 0, :, :]), flat(AE[:, s, 1, :, :]), 0.0, ALU.mult, ALU.add))
                                c.seq(v.tensor_copy(ST[:, s, :, H:2 * H], L[:, s, :, 1:J1 + 1].rearrange("p h j -> p j h")))
                                dve.sem_inc(states, 1)
                                hold(dve, decays, b + 1)
                                hold(dve, weighed, b + 1)
                                c.seq(v.tensor_tensor_scan(whole(VT[:, :, :, :]), whole(decay[:, :, :, :]), whole(VT[:, :, :, :]), 0.0, ALU.mult, ALU.add))
                                dve.sem_inc(summed, 1)
                                c.seq(v.tensor_copy(VT[:, :, :, 0], VT[:, :, :, J1]))
                                dve.sem_inc(carried, 1)
                        passes(dve, body)
                        c.inc(v.tensor_copy(tails[:, 0:2 * H], ST[:, 1, J1 - 1, 0:2 * H]))
                        c.seq(v.tensor_copy(tails[:, 2 * H:W].rearrange("p (h c) -> p h c", c=DH), VT[:, :, :, J1]))

                    @block.scalar
                    def _(act):
                        def mask(b, s, i):
                            hold(act, staged, b + 1)
                            hold(act, q_in[s], 16 * (i + 1))
                            for j in range(J1):
                                ins = a.mul(Q[:, s, j, :], Q[:, s, j, :], newS[:, s, j:j + 1])
                            ins.then_inc(masked, 1)
                        mask(0, 0, 0)

                        def body(i, last):
                            for s in range(2):
                                b = 2 * i + s
                                if not (last and s == 1):
                                    mask(b + 1, 1 - s, i + s)
                                hold(act, args, b + 1)
                                e = AE[:, s, :, :, 1:J1 + 1].rearrange("p n h j -> p (n h) j")
                                a.activation(e, e, ACT.Exp).then_inc(exps, 1)
                                hold(act, exps, b + 1)
                                if s or not zero(i):
                                    hold(act, summed, b)
                                a.copy(decay[:, :, :, 1:J1 + 1], AE[:, s, 0, :, 1:J1 + 1].unsqueeze(2).broadcast_to([P, H, DH, J1])).then_inc(decays, 1)
                                if not zero(i):
                                    hold(act, stored[s], 16 * i)
                                hold(act, summed, b + 1)
                                a.copy(ST[:, s, :, 2 * H:W].rearrange("p j (h c) -> p h c j", c=DH), VT[:, :, :, 1:J1 + 1]).then_inc(sums_out, 1)
                        passes(act, body)

                    @block.sync
                    def _(sp):
                        tab = att_tab[0:P * NJ1, :].rearrange("(p j) w -> p j w", j=NJ1)
                        q_runs = sum_tab[0:P * NJ1, :].rearrange("(p j) f -> p j f", j=NJ1)

                        def store(b, s):
                            hold(sp, states, b + 1)
                            hold(sp, sums_out, b + 1)
                            sp.dma_start(tab[:, bass.ds(b * J1, J1), :], ST[:, s, :, :]).then_inc(stored[s], 16)

                        def load(b, s):
                            sp.dma_start(Q[:, s, :, :], q_runs[:, bass.ds(b * J1, J1), :]).then_inc(q_in[s], 16)
                        load(0, 0)
                        load(1, 1)

                        def body(i, last):
                            for s in range(2):
                                b = 2 * i + s
                                if not last:
                                    hold(sp, q_free, b + 1)
                                    load(b + 2, s)
                                store(b, s)
                        passes(sp, body)
                        for s in range(2):
                            sp.wait_ge(stored[s], 16 * PASSES)

        def out_phase(agg):
            H, DH = 8, 32
            ctx, sb, ps, sem = phase()
            with ctx:
                XNR = sb("XNR", [P, NT, D])
                wo, bo = sb("wo", [P, 2, D]), sb("bo", [P, D])
                u, ut = sb("u", [P, GT, D]), sb("ut", [P, 2, GT, P])
                psT, psO = ps("psT", [P, 2, 512]), ps("psO", [P, 2, 512])
                w_in, summed, turned, columns, done, added, chain = (sem(n) for n in ("w_in", "summed", "turned", "columns", "done", "added", "chain"))
                with nc.Block() as block:
                    @block.sync
                    def _(sp):
                        sp.dma_start(wo[:, :, :], g1_wout.rearrange("(k p) n -> p k n", p=P)).then_inc(w_in, 16)
                        sp.dma_start(bo[:, :], g1_bout.partition_broadcast(P)).then_inc(w_in, 16)
                        sp.dma_start(XNR[:, :, :], table_rows(xn_tab)).then_inc(w_in, 16)

                    @block.vector
                    def _(dve):
                        dve.wait_ge(w_in, 48)

                        def body(g):
                            if not zero(g):
                                hold(dve, turned, g * GT)
                            for s in range(GT):
                                t = g * GT + s
                                v.tensor_tensor(u[:, s, :].rearrange("p (c h) -> p c h", h=H), row(agg, t).rearrange("p (h c) -> p c h", h=H),
                                                row(XNR, t).rearrange("p (c h) -> p c h", h=H), ALU.add).then_inc(summed, 1)
                            for s in range(GT):
                                t = g * GT + s
                                v.tensor_tensor(row(X, t), row(X, t), bo[:, :], ALU.add).then_inc(chain, 1)
                            for s in range(GT):
                                t = g * GT + s
                                hold(dve, done, t + 1)
                                hold(dve, chain, t + 1)
                                v.tensor_tensor(row(X, t), row(X, t), psO[:, s % 2, 0:D], ALU.add).then_inc(added, 1)
                        loop(dve, NG, body)

                    @block.tensor
                    def _(pe):
                        pe.wait_ge(w_in, 48)

                        def body(g):
                            for s in range(GT):
                                hold(pe, summed, g * GT + s + 1)
                                if not zero(g) or s >= 2:
                                    hold(pe, columns, g * GT + max(s - 1, 0))
                                nc.tensor.transpose(psT[:, s % 2, 0:P], u[:, s, 0:P], ident[:, :])
                                nc.tensor.transpose(psT[:, s % 2, P:D], u[:, s, P:D], ident[:, :]).then_inc(turned, 1)
                            for s in range(GT):
                                hold(pe, columns, g * GT + s + 1)
                                if not zero(g) or s >= 2:
                                    hold(pe, added, g * GT + max(s - 1, 0))
                                for k in range(2):
                                    ins = nc.tensor.matmul(psO[:, s % 2, 0:D], ut[:, k, s, :], wo[:, k, :], start=(k == 0), stop=(k == 1))
                                ins.then_inc(done, 1)
                        loop(pe, NG, body)

                    @block.scalar
                    def _(act):
                        def body(g):
                            for s in range(GT):
                                hold(act, turned, g * GT + s + 1)
                                if not zero(g):
                                    hold(act, done, g * GT)
                                a.copy(ut[:, :, s, :], psT[:, s % 2, 0:D].rearrange("p (k c) -> p k c", k=2)).then_inc(columns, 1)
                        loop(act, NG, body)

        def last_norm_phase(Y):
            ctx, sb, ps, sem = phase()
            with ctx:
                st, mv, sd, rs = sb("st", [P, NT, 6]), sb("mv", [P, NT, 2]), sb("sd", [P, NT]), sb("rs", [P, NT])
                gam, bet = sb("gam", [P, D]), sb("bet", [P, D])
                p_in, stats, rooted, chain = sem("p_in"), sem("stats"), sem("rooted"), sem("chain")
                with nc.Block() as block:
                    @block.sync
                    def _(sp):
                        sp.dma_start(gam[:, :], f1_gamma.partition_broadcast(P)).then_inc(p_in, 16)
                        sp.dma_start(bet[:, :], f1_beta.partition_broadcast(P)).then_inc(p_in, 16)

                    @block.vector
                    def _(dve):
                        c = Count(dve, chain)
                        dve.wait_ge(p_in, 32)
                        for t in range(NT):
                            c.inc(v.bn_stats(st[:, t, :], Y[:, t, :]))
                        c.wait()
                        for t in range(NT):
                            c.inc(v.bn_aggr(mv[:, t, :], st[:, t, :]))
                        c.wait()
                        dve.sem_inc(stats, 1)
                        dve.wait_ge(rooted, 1)
                        c.seq(v.reciprocal(rs[:, :], sd[:, :]))
                        for t in range(NT):
                            c.inc(v.tensor_scalar(Y[:, t, :], Y[:, t, :], mv[:, t, 0:1], rs[:, t:t + 1], ALU.subtract, ALU.mult))
                        c.wait()
                        all_rows = lambda tile: tile[:, :].unsqueeze(1).broadcast_to([P, NT, D])
                        c.seq(v.tensor_tensor(Y[:, :, :], Y[:, :, :], all_rows(gam), ALU.mult))
                        c.seq(v.tensor_tensor(Y[:, :, :], Y[:, :, :], all_rows(bet), ALU.add))
                        c.seq(v.tensor_tensor(X[:, :, :], X[:, :, :], Y[:, :, :], ALU.add))

                    @block.scalar
                    def _(act):
                        act.wait_ge(stats, 1)
                        a.activation(sd[:, :], mv[:, :, 1], ACT.Sqrt, bias=eps_col[:, :]).then_inc(rooted, 1)

        def finish_phase(tile):
            ctx, sb, ps, sem = phase()
            with ctx:
                out_stored = sem("out_stored")
                with nc.Block() as block:
                    @block.sync
                    def _(sp):
                        sp.dma_start(table_rows(out[0:(NT - 1) * P, :]), tile[:, 0:NT - 1, :]).then_inc(out_stored, 16)
                        sp.dma_start(out[(NT - 1) * P:N, :], tile[0:TAIL_ROWS, NT - 1, :]).then_inc(out_stored, 16)
                        sp.wait_ge(out_stored, 32)

        start_phase()
        g_ctx = ExitStack()
        with g_ctx:
            nbr0 = keep_sb(g_ctx, "nbr0", [P, NJ1], I32)
            keep0 = keep_sb(g_ctx, "keep0", [P, NJ1])
            cont0 = keep_sb(g_ctx, "cont0", [P, 1])
            end0 = keep_sb(g_ctx, "end0", [P, NT], I32)
            w0 = keep_sb(g_ctx, "w0", [P, NJ1])
            sort_phase(E1, NJ1, J1, src, [dst, edge_weight], key_tab[0], by_src_tab, end0, P * NJ1)
            reload_phase(by_src_tab, NJ1, [(1, nbr0), (2, w0)], keep0, None, cont0)
            norm_phase(table=xn_tab)
            gnn0_phase()
        if LAST_PHASE >= 2:
            f_ctx = ExitStack()
            with f_ctx:
                G0 = keep_sb(f_ctx, "G0", [P, 4, NT])
                XNT0 = keep_sb(f_ctx, "XNT0", [P, NG, 2, GT * P])
                src2 = keep_sb(f_ctx, "src2", [P, NJ2], I32)
                dst2 = keep_sb(f_ctx, "dst2", [P, NJ2], I32)
                keep2 = keep_sb(f_ctx, "keep2", [P, NJ2])
                pen2 = keep_sb(f_ctx, "pen2", [P, NJ2])
                cont2 = keep_sb(f_ctx, "cont2", [P, 1])
                end2 = keep_sb(f_ctx, "end2", [P, NT], I32)
                first2 = keep_sb(f_ctx, "first2", [P, NT], I32)
                r_ctx = ExitStack()
                sort_phase(E2, NJ2, J2, f0_edges[1, :], [f0_edges[0, :]], key_tab[1], by_dst_tab, end2, E2, first2)
                reload_phase(by_dst_tab, NJ2, [(0, dst2), (1, src2)], keep2, pen2, cont2)
                with r_ctx:
                    HG = keep_sb(r_ctx, "HG", [P, NT, 24])
                    agg0 = keep_sb(r_ctx, "agg0", [P, NT, 16])
                    self_score = keep_sb(r_ctx, "self_score", [P, NT, 4])
                    SC0 = keep_sb(r_ctx, "SC0", [P, NT, 4])
                    norm_phase(cols_keep=XNT0, project=(f0_wgat, 16, None, HG))
                    gat_phase(HG, self_score, agg0)
                    router_phase(agg0, SC0)
                    gate_phase(SC0, 4, G0)
                b1T0 = keep_sb(f_ctx, "b1T0", [P, 16])
                biases_phase(4, G0, f0_b1, f0_b2, b1T0, X)
                dense_experts_phase(4, ACT.Gelu, XNT0, G0, f0_w1, f0_w2, b1T0, X)
        if LAST_PHASE >= 3:
            x_ctx = ExitStack()
            with x_ctx:
                src1 = keep_sb(x_ctx, "src1", [P, NJ1], I32)
                dst1 = keep_sb(x_ctx, "dst1", [P, NJ1], I32)
                keep1 = keep_sb(x_ctx, "keep1", [P, NJ1])
                pen1 = keep_sb(x_ctx, "pen1", [P, NJ1])
                cont1 = keep_sb(x_ctx, "cont1", [P, 1])
                end1 = keep_sb(x_ctx, "end1", [P, NT], I32)
                first1 = keep_sb(x_ctx, "first1", [P, NT], I32)
                graph_phase()
                tails = keep_sb(x_ctx, "att_tails", [P, 16 + D])
                norm_phase(table=xn_tab, project=(g1_wqkv, 3 * D, g1_bqkv, [(q_tab, 0, D), (kv_tab, D, 2 * D)]),
                           scatter=(sum_tab, first1))
                attention_phase(tails)
                agg1 = keep_sb(x_ctx, "agg1", [P, NT, D])
                merge_phase(8, D, tails[:, :], cont1, end1, att_tab, agg1)
                out_phase(agg1)
        if LAST_PHASE >= 4:
            e_ctx = ExitStack()
            with e_ctx:
                G1 = keep_sb(e_ctx, "G1", [P, E3, NT])
                weight1 = keep_sb(e_ctx, "weight1", [P, 2, NT])
                pos1 = keep_sb(e_ctx, "pos1", [P, 2, NT], I32)
                block_expert = keep_sb(e_ctx, "block_expert", [P, MAX_BLOCKS + 2], I32)
                b1T1 = keep_sb(e_ctx, "b1T1", [P, E3 * FC3])
                w_ctx = ExitStack()
                with w_ctx:
                    W1r = keep_sb(w_ctx, "W1r", [P, 2, E3, FF3])
                    W2r = keep_sb(w_ctx, "W2r", [P, FC3, E3, D])
                    load_experts_phase(W1r, W2r)
                    r_ctx = ExitStack()
                    with r_ctx:
                        XNR = keep_sb(r_ctx, "XNR1", [P, NT, D])
                        SC1 = keep_sb(r_ctx, "SC1", [P, NT, E3])
                        chosen = keep_sb(r_ctx, "chosen", [P, 2, NT, E3])
                        norm_phase(rows_keep=XNR, project=(f1_gw, E3, f1_gb, SC1))
                        gate_phase(SC1, E3, G1, chosen, weight1)
                        dispatch_phase(chosen, XNR, pos1, block_expert)
                        biases_phase(E3, G1, f1_b1, f1_b2, b1T1, XNR, table=xn_tab)
                    sparse_experts_phase(block_expert, W1r, W2r, b1T1)
                ACC = keep_sb(e_ctx, "ACC", [P, NT, D])
                combine_phase(pos1, weight1, ACC)
                last_norm_phase(ACC)
        finish_phase(X)


_INS = ['x', 'src', 'dst', 'edge_weight', 'L0_gnn_weight1', 'L0_gnn_weight2', 'L0_gnn_gamma', 'L0_gnn_beta',
        'L0_ffn_W_gat', 'L0_ffn_att_src', 'L0_ffn_att_dst', 'L0_ffn_b_gat', 'L0_ffn_ln_gamma', 'L0_ffn_ln_beta',
        'L0_ffn_W1', 'L0_ffn_b1', 'L0_ffn_W2', 'L0_ffn_b2', 'L0_ffn_edge_index', 'L1_gnn_W_qkv', 'L1_gnn_b_qkv',
        'L1_gnn_W_out', 'L1_gnn_b_out', 'L1_ffn_gate_w', 'L1_ffn_gate_b', 'L1_ffn_w1', 'L1_ffn_b1', 'L1_ffn_w2',
        'L1_ffn_b2', 'L1_ffn_gamma', 'L1_ffn_beta']


def kernel(**inputs):
    import numpy as _np
    import concourse.bacc as _bacc
    from concourse import mybir as _mybir
    from concourse.bass_utils import run_bass_kernel_spmd as _run

    nc = _bacc.Bacc("TRN2", target_bir_lowering=False, num_devices=1)
    arrays, args = {}, []
    for name in _INS:
        arr = _np.ascontiguousarray(inputs[name])
        arrays[f"in_{name}_dram"] = arr
        args.append(nc.dram_tensor(f"in_{name}_dram", arr.shape, _mybir.dt.from_np(arr.dtype), kind="ExternalInput").ap())
    out = nc.dram_tensor("out_0_dram", (N, D), F32, kind="ExternalOutput").ap()
    bass_gnn_moe_kernel(nc, *args, out)
    r = _run(nc, [arrays], core_ids=[0])
    return r.results[0]["out_0_dram"]
```

```python
from contextlib import ExitStack

import concourse.bass as bass
from concourse import mybir

F32 = mybir.dt.float32
BF16 = mybir.dt.bfloat16
I32 = mybir.dt.int32
ALU = mybir.AluOpType
ACT = mybir.ActivationFunctionType
AX = mybir.AxisListType.X

P = 128
N = 3125
D = 256
NT = -(-N // P)
NP = NT * P
TAIL_ROWS = N - (NT - 1) * P
GT = 5
NG = NT // GT
assert NG * GT == NT
LN_EPS = 1e-5
BIG = 1e30

NH = 32
E1 = 50000
J1 = 14
NJ1 = 392
NB1 = NJ1 // J1
FULL1 = E1 // NJ1
REST1 = E1 - FULL1 * NJ1
E2 = 32768
J2 = 16
NJ2 = E2 // P
NB2 = NJ2 // J2
PAD_DST = NH * P - 1
assert NB1 * J1 == NJ1 and NB1 % 4 == 0 and NB2 * J2 == NJ2 and NB2 % 2 == 0


class Count:

    def __init__(self, eng, sem):
        self.eng, self.sem, self.base, self.n, self.start = eng, sem, 0, 0, 0

    def inc(self, ins):
        ins.then_inc(self.sem, 1)
        self.n += 1

    def wait(self):
        if not (isinstance(self.base, int) and self.base + self.n == 0):
            self.eng.wait_ge(self.sem, self.base + self.n)

    def seq(self, ins):
        self.inc(ins)
        self.wait()

    def at(self, i, per):
        if isinstance(i, int) and i == 0:
            self.start = self.base + self.n
        self.base, self.n, self.per = self.start + i * per, 0, per

    def end(self, trips):
        assert self.n == self.per, f"passes count {self.n}, said {self.per}"
        self.base, self.n = self.start + trips * self.per, 0


def loop(eng, trips, body):
    body(0)
    if trips > 1:
        with eng.Fori(1, trips) as i:
            body(i)


def zero(i):
    return isinstance(i, int) and i == 0


def row(tile, t):
    return tile[:, bass.ds(t, 1), :].rearrange("p a d -> p (a d)")


def table_rows(tab):
    return tab.rearrange("(t p) f -> p t f", p=P)


def bass_gnn_moe_kernel(nc, x, src, dst, edge_weight, g0_w1, g0_w2, g0_gamma, g0_beta, f0_wgat,
                        f0_att_src, f0_att_dst, f0_bgat, f0_lng, f0_lnb, f0_w1, f0_b1, f0_w2, f0_b2,
                        f0_edges, g1_wqkv, g1_bqkv, g1_wout, g1_bout, f1_gw, f1_gb, f1_w1, f1_b1,
                        f1_w2, f1_b2, f1_gamma, f1_beta, out):
    top = ExitStack()
    v, a = nc.vector, nc.scalar
    count = [0]

    def dram(name, shape, dt=F32):
        return nc.dram_tensor(name, shape, dt, kind="Internal").ap()

    def phase():
        ctx = ExitStack()
        count[0] += 1
        tag = f"_{count[0]}"
        own_sems = []

        def close():
            nc.clear_and_free_semaphores(own_sems)
            nc.all_engine_barrier()
        ctx.callback(close)

        def sb(name, shape, dt=F32):
            return ctx.enter_context(nc.sbuf_tensor(name + tag, shape, dt))

        def ps(name, shape, dt=F32):
            return ctx.enter_context(nc.psum_tensor(name + tag, shape, dt))

        def sem(name):
            own_sems.append(nc.alloc_semaphore(name=name + tag))
            return own_sems[-1]
        return ctx, sb, ps, sem

    def keep_sb(ctx, name, shape, dt=F32):
        return ctx.enter_context(nc.sbuf_tensor(name, shape, dt))

    ticks = {}

    def hold(eng, sem, value):
        if isinstance(value, int):
            eng.wait_ge(sem, value)
        else:
            name = str(eng.engine)
            if name not in ticks:
                ticks[name] = top.enter_context(nc.semaphore("tick_" + name.split(".")[-1]))
            eng.wait_ge(sem, value)
            eng.sem_inc(ticks[name], 1)

    with top:
        weights_in = top.enter_context(nc.semaphore("weights_in"))
        X = keep_sb(top, "X", [P, NT, D])
        ident = keep_sb(top, "ident", [P, P])
        ones = keep_sb(top, "ones", [P, P])
        iota_free = keep_sb(top, "iota_free", [P, P])
        iota_part = keep_sb(top, "iota_part", [P, 1])
        upper = keep_sb(top, "upper", [P, P])
        below = keep_sb(top, "below", [P, P])
        eps_col = keep_sb(top, "eps_col", [P, 1])
        xn_tab = dram("xn_tab", [NP, D])
        sum_tab = dram("sum_tab", [P * NJ1 + NP, D])
        adst_tab = dram("adst_tab", [E2 + NP, 4])
        by_src_tab = dram("by_src_tab", [P * NJ1, 3], I32)
        by_dst_tab = dram("by_dst_tab", [P * NJ2, 2], I32)
        key_tab = [dram("key_tab0", [P * NJ1]), dram("key_tab1", [P * NJ2])]
        h_tab = dram("h_tab", [NP, 24])
        gat_tab = dram("gat_tab", [E2 + 1, 24])
        q_tab = dram("q_tab", [NP, D])
        kv_tab = dram("kv_tab", [NP, 2 * D])
        att_tab = dram("att_tab", [P * NJ1 + 1, 16 + D])

        def start_phase():
            ctx, sb, ps, sem = phase()
            with ctx:
                ii = sb("ii", [P, P], I32)
                ip = sb("ip", [P, 1], I32)
                iotas, made, cleared, x_in = sem("iotas"), sem("made"), sem("cleared"), sem("x_in")
                with nc.Block() as block:
                    @block.gpsimd
                    def _(pool):
                        nc.gpsimd.iota(ii[:, :], pattern=[[1, P]], base=0, channel_multiplier=0).then_inc(iotas, 1)
                        nc.gpsimd.iota(ip[:, :], pattern=[[0, 1]], base=0, channel_multiplier=1).then_inc(iotas, 1)

                    @block.sync
                    def _(sp):
                        sp.dma_start(X[:, 0:NT - 1, :], table_rows(x[0:(NT - 1) * P, :])).then_inc(x_in, 16)
                        sp.wait_ge(cleared, 1)
                        sp.dma_start(X[0:TAIL_ROWS, NT - 1, :], x[(NT - 1) * P:N, :]).then_inc(x_in, 16)
                        sp.wait_ge(x_in, 32)

                    @block.vector
                    def _(dve):
                        c = Count(dve, made)
                        v.memset(X[:, NT - 1, :], 0.0).then_inc(cleared, 1)
                        c.inc(v.memset(ones[:, :], 1.0))
                        c.inc(v.memset(eps_col[:, :], LN_EPS))
                        dve.wait_ge(iotas, 2)
                        c.inc(v.tensor_copy(iota_free[:, :], ii[:, :]))
                        c.seq(v.tensor_copy(iota_part[:, :], ip[:, :]))
                        for tile, op in ((ident, ALU.is_equal), (upper, ALU.is_ge), (below, ALU.is_lt)):
                            c.seq(v.tensor_scalar(tile[:, :], iota_free[:, :], iota_part[:, :], None, op))

        def norm_phase(table=None, rows_keep=None, cols_keep=None, project=None, scatter=None):
            ctx, sb, ps, sem = phase()
            with ctx:
                turn = cols_keep is not None or project is not None
                st, mv = sb("st", [P, GT, 6]), sb("mv", [P, GT, 2])
                sd, rs = sb("sd", [P, GT]), sb("rs", [P, GT])
                xn = sb("xn", [P, GT, D])
                stats, rooted, chain, normed = sem("stats"), sem("rooted"), sem("chain"), sem("normed")
                stored, copied, xn_free = sem("stored"), sem("copied"), sem("xn_free")
                if turn:
                    turned, columns = sem("turned"), sem("columns")
                    psT = ps("psT", [P, 2, 512])
                    xt = sb("xt", [P, 2, GT, P])
                to_tables = False
                if project:
                    w_dram, PN, bias, sink = project
                    w_in, projected, evacuated, p_stored = sem("w_in"), sem("projected"), sem("evacuated"), sem("p_stored")
                    wp = sb("wp", [P, 2, PN])
                    psP = ps("psP", [P, 2, 512 * -(-PN // 512)])
                    bb = sb("bb", [P, PN])
                    to_tables = isinstance(sink, list)
                    if to_tables:
                        pr, pr_free = sb("pr", [P, GT, PN]), sem("pr_free")
                    cuts = [(0, PN, 0)] if PN <= 512 else [(0, 256, 0), (256, PN, 512)]
                    n_w = 16 * (1 + (bias is not None))
                n_keep = (rows_keep is not None) + (cols_keep is not None)
                if scatter is not None:
                    spots, spotted, scattered = sb("spots", [P, GT], I32), sem("spotted"), sem("scattered")
                with nc.Block() as block:
                    @block.sync
                    def _(sp):
                        if project:
                            sp.dma_start(wp[:, :, :], w_dram.rearrange("(k p) n -> p k n", p=P)).then_inc(w_in, 16)
                            if bias is not None:
                                sp.dma_start(bb[:, :], bias.partition_broadcast(P)).then_inc(w_in, 16)
                        with sp.Fori(0, NG) as g:
                            if table is not None:
                                sp.wait_ge(normed, (g + 1) * GT)
                                sp.dma_start(table_rows(table)[:, bass.ds(g * GT, GT), :], xn[:, :, :]).then_inc(stored, 16)
                            if to_tables:
                                hold(sp, evacuated, (g + 1) * GT)
                                for tab, a0, w in sink:
                                    sp.dma_start(table_rows(tab)[:, bass.ds(g * GT, GT), :], pr[:, :, a0:a0 + w]).then_inc(p_stored, 16)
                        if table is not None:
                            sp.wait_ge(stored, 16 * NG)
                        if to_tables:
                            sp.wait_ge(p_stored, 16 * NG * len(sink))

                    @block.vector
                    def _(dve):
                        c = Count(dve, chain)

                        def group(g):
                            c.at(g, 2 * GT + 1)
                            for s in range(GT):
                                c.inc(v.bn_stats(st[:, s, :], row(X, g * GT + s)))
                            hold(dve, chain, c.base + c.n)
                            for s in range(GT):
                                c.inc(v.bn_aggr(mv[:, s, :], st[:, s, :]))
                            hold(dve, chain, c.base + c.n)
                            dve.sem_inc(stats, 1)
                            hold(dve, rooted, g + 1)
                            c.inc(v.reciprocal(rs[:, :], sd[:, :]))
                            hold(dve, chain, c.base + c.n)
                            if not zero(g):
                                hold(dve, xn_free, g)
                            for s in range(GT):
                                v.tensor_scalar(xn[:, s, :], row(X, g * GT + s), mv[:, s, 0:1], rs[:, s:s + 1],
                                                ALU.subtract, ALU.mult).then_inc(normed, 1)
                            if project:
                                if to_tables and not zero(g):
                                    hold(dve, pr_free, g)
                                for s in range(GT):
                                    hold(dve, projected, g * GT + s + 1)
                                    for a0, a1, spot in cuts:
                                        o = pr[:, s, a0:a1] if to_tables else row(sink, g * GT + s)[:, a0:a1]
                                        i0 = psP[:, s % 2, spot:spot + a1 - a0]
                                        ins = v.tensor_tensor(o, i0, bb[:, a0:a1], ALU.add) if bias is not None else v.tensor_copy(o, i0)
                                    ins.then_inc(evacuated, 1)
                        if project:
                            dve.wait_ge(w_in, n_w)
                        loop(dve, NG, group)

                    @block.scalar
                    def _(act):
                        with act.Fori(0, NG) as g:
                            hold(act, stats, g + 1)
                            a.activation(sd[:, :], mv[:, :, 1], ACT.Sqrt, bias=eps_col[:, :]).then_inc(rooted, 1)
                            if turn:
                                for s in range(GT):
                                    hold(act, turned, g * GT + s + 1)
                                    a.copy(xt[:, :, s, :], psT[:, s % 2, 0:D].rearrange("p (k c) -> p k c", k=2)).then_inc(columns, 1)
                            if rows_keep is not None:
                                hold(act, normed, (g + 1) * GT)
                                a.copy(rows_keep[:, bass.ds(g * GT, GT), :], xn[:, :, :]).then_inc(copied, 1)
                            if cols_keep is not None:
                                hold(act, columns, (g + 1) * GT)
                                a.copy(cols_keep[:, bass.ds(g, 1), :, :].rearrange("p a k c -> p (a k c)"),
                                       xt[:, :, :, :].rearrange("p k s c -> p (k s c)")).then_inc(copied, 1)

                    @block.tensor
                    def _(pe):
                        if project:
                            pe.wait_ge(w_in, n_w)

                        def group(g):
                                for s in range(GT):
                                    hold(pe, normed, g * GT + s + 1)
                                    if not zero(g) or s >= 2:
                                        hold(pe, columns, g * GT + max(s - 1, 0))
                                    nc.tensor.transpose(psT[:, s % 2, 0:P], xn[:, s, 0:P], ident[:, :])
                                    nc.tensor.transpose(psT[:, s % 2, P:D], xn[:, s, P:D], ident[:, :]).then_inc(turned, 1)
                                if project:
                                    for s in range(GT):
                                        hold(pe, columns, g * GT + s + 1)
                                        if not zero(g) or s >= 2:
                                            hold(pe, evacuated, g * GT + max(s - 1, 0))
                                        for a0, a1, spot in cuts:
                                            for k in range(2):
                                                ins = nc.tensor.matmul(psP[:, s % 2, spot:spot + a1 - a0], xt[:, k, s, :],
                                                                       wp[:, k, a0:a1], start=(k == 0), stop=(k == 1))
                                        ins.then_inc(projected, 1)
                        if turn:
                            loop(pe, NG, group)

                    @block.gpsimd
                    def _(pool):
                        with pool.Fori(0, NG) as g:
                            hold(pool, normed, (g + 1) * GT)
                            if turn:
                                hold(pool, columns, (g + 1) * GT)
                            if table is not None:
                                hold(pool, stored, 16 * (g + 1))
                            if n_keep:
                                hold(pool, copied, n_keep * (g + 1))
                            pool.sem_inc(xn_free, 1)
                            if scatter is not None:
                                nc.gpsimd.tensor_copy(spots[:, :], scatter[1][:, bass.ds(g * GT, GT)]).then_inc(spotted, 1)
                                hold(pool, spotted, g + 1)
                                hold(pool, evacuated, (g + 1) * GT)
                                for s in range(GT):
                                    pool.indirect_dma_start(out=scatter[0], out_offset=bass.IndirectOffsetOnAxis(ap=spots[:, s:s + 1], axis=0),
                                                            in_=pr[:, s, 0:D], in_offset=None).then_inc(scattered, 16)
                                hold(pool, scattered, 16 * GT * (g + 1))
                            if to_tables:
                                hold(pool, p_stored, 16 * len(sink) * (g + 1))
                                pool.sem_inc(pr_free, 1)

        def count_block(lo, hi, columns, J, counts):
            ctx, sb, ps, sem = phase()
            with ctx:
                onelo, onehi = sb("onelo", [P, 2, J, P], BF16), sb("onehi", [P, 2, J, NH], BF16)
                zerob = sb("zerob", [P, P], BF16)
                psC = ps("psC", [P, NH])
                built, used, counted, chain = sem("built"), sem("used"), sem("counted"), sem("chain")
                trips = columns // J // 2
                with nc.Block() as block:
                    @block.vector
                    def _(dve):
                        v.memset(zerob[:, :], 0.0).then_inc(chain, 1)
                        dve.wait_ge(chain, 1)

                        def body(i):
                            for s in range(2):
                                cols = bass.ds((i * 2 + s) * J, J)
                                if not zero(i):
                                    hold(dve, used, (i - 1) * 2 + s + 1)
                                v.tensor_tensor(onelo[:, s, :, :], iota_free[:, :].unsqueeze(1).broadcast_to([P, J, P]),
                                                lo[:, cols].unsqueeze(2).broadcast_to([P, J, P]), ALU.is_equal)
                                v.tensor_tensor(onehi[:, s, :, :], iota_free[:, 0:NH].unsqueeze(1).broadcast_to([P, J, NH]),
                                                hi[:, cols].unsqueeze(2).broadcast_to([P, J, NH]), ALU.is_equal).then_inc(built, 1)
                        loop(dve, trips, body)
                        dve.wait_ge(counted, 1)
                        v.tensor_copy(counts[:, :], psC[:, :]).then_inc(chain, 1)
                        dve.wait_ge(chain, 2)

                    @block.tensor
                    def _(pe):
                        pe.wait_ge(chain, 1)
                        nc.tensor.matmul(psC[:, :], zerob[:, :], zerob[:, 0:NH], start=True, stop=False)
                        with pe.Fori(0, trips) as i:
                            for s in range(2):
                                hold(pe, built, i * 2 + s + 1)
                                for j in range(J):
                                    ins = nc.tensor.matmul(psC[:, :], onelo[:, s, j, :], onehi[:, s, j, :], start=False, stop=False)
                                ins.then_inc(used, 1)
                        nc.tensor.matmul(psC[:, :], zerob[:, :], zerob[:, 0:NH], start=False, stop=True).then_inc(counted, 1)

        def prefix_block(counts, first, end, endrow, none_row, firstrow=None):
            ctx, sb, ps, sem = phase()
            with ctx:
                psI, psT = ps("psI", [P, 512]), ps("psTot", [P, 512])
                tot, scan, t1 = sb("tot", [P, NH]), sb("scan", [P, NH]), sb("t1", [P, NH])
                summed, chain = sem("summed"), sem("chain")
                with nc.Block() as block:
                    @block.tensor
                    def _(pe):
                        nc.tensor.matmul(psI[:, 0:NH], upper[:, :], counts[:, :], start=True, stop=True)
                        nc.tensor.matmul(psT[:, 0:NH], ones[:, :], counts[:, :], start=True, stop=True).then_inc(summed, 1)

                    @block.vector
                    def _(dve):
                        c = Count(dve, chain)
                        dve.wait_ge(summed, 1)
                        c.seq(v.tensor_copy(tot[:, :], psT[:, 0:NH]))
                        c.seq(v.tensor_tensor_scan(scan[:, :], ones[:, 0:NH], tot[:, :], 0.0, ALU.mult, ALU.add))
                        c.seq(v.tensor_tensor(scan[:, :], scan[:, :], tot[:, :], ALU.subtract))
                        c.seq(v.tensor_tensor(end[:, :], scan[:, :], psI[:, 0:NH], ALU.add))
                        c.seq(v.tensor_tensor(first[:, :], end[:, :], counts[:, :], ALU.subtract))
                        c.seq(v.tensor_scalar(t1[:, :], counts[:, :], 0.5, None, ALU.is_ge))
                        c.seq(v.scalar_tensor_tensor(scan[:, :], end[:, :], -1.0 - none_row, t1[:, :], ALU.add, ALU.mult))
                        c.seq(v.tensor_scalar(endrow[:, :], scan[:, 0:NT], float(none_row), None, ALU.add))
                        if firstrow is not None:
                            c.seq(v.tensor_scalar(tot[:, :], iota_free[:, 0:NH], float(P), float(none_row), ALU.mult, ALU.add))
                            c.seq(v.tensor_scalar(tot[:, :], tot[:, :], iota_part[:, 0:1], None, ALU.add))
                            c.seq(v.tensor_tensor(scan[:, :], first[:, :], tot[:, :], ALU.subtract))
                            c.seq(v.tensor_tensor(scan[:, :], scan[:, :], t1[:, :], ALU.mult))
                            c.seq(v.tensor_tensor(firstrow[:, :], scan[:, 0:NT], tot[:, 0:NT], ALU.add))

        def run_flags(dve, c, dstf, nextf, NJ, keep, pen, cont, tmp):
            c.seq(v.memset(keep[:, 0:1], 0.0))
            c.seq(v.tensor_tensor(keep[:, 1:NJ], dstf[:, 1:NJ], dstf[:, 0:NJ - 1], ALU.is_equal))
            c.seq(v.tensor_scalar(pen[:, :], keep[:, :], 1.0, BIG, ALU.subtract, ALU.mult))
            c.seq(v.tensor_tensor(tmp[:, 0:1], dstf[:, NJ - 1:NJ], nextf[:, :], ALU.is_equal))
            c.seq(v.scalar_tensor_tensor(cont[:, :], dstf[:, NJ - 1:NJ], 1.0, tmp[:, 0:1], ALU.add, ALU.mult))
            c.seq(v.tensor_scalar(cont[:, :], cont[:, :], 1.0, None, ALU.subtract))

        def graph_phase(lo, hi):
            ctx, sb, ps, sem = phase()
            with ctx:
                dstf, nexti, nextf = sb("dstf", [P, NJ1]), sb("nexti", [P, 1], I32), sb("nextf", [P, 1])
                loi, tmp = sb("loi", [P, NJ1], I32), sb("tmp", [P, 1])
                cleared, e_in, chain = sem("cleared"), sem("e_in"), sem("chain")
                with nc.Block() as block:
                    @block.sync
                    def _(sp):
                        sp.wait_ge(cleared, 1)
                        for tile, dr in ((src1, src), (dst1, dst)):
                            sp.dma_start(tile[0:FULL1, :], dr[0:FULL1 * NJ1].rearrange("(p j) -> p j", j=NJ1)).then_inc(e_in, 16)
                            sp.dma_start(tile[FULL1:FULL1 + 1, 0:REST1], dr[FULL1 * NJ1:E1].unsqueeze(0)).then_inc(e_in, 16)
                        sp.dma_start(nexti[0:FULL1, :], dst.rearrange("(e o) -> e o", o=1)[NJ1:(FULL1 * NJ1 + 1):NJ1, :], allow_slow_non_contiguous=True).then_inc(e_in, 16)

                    @block.vector
                    def _(dve):
                        c = Count(dve, chain)
                        c.inc(v.memset(src1[:, :], 0))
                        c.inc(v.memset(dst1[:, :], PAD_DST))
                        c.seq(v.memset(nexti[:, :], PAD_DST))
                        dve.sem_inc(cleared, 1)
                        dve.wait_ge(e_in, 16 * 5)
                        c.inc(v.tensor_copy(dstf[:, :], dst1[:, :]))
                        c.seq(v.tensor_copy(nextf[:, :], nexti[:, :]))
                        run_flags(dve, c, dstf, nextf, NJ1, keep1, pen1, cont1, tmp)
                        c.seq(v.tensor_single_scalar(loi[:, :], dst1[:, :], P - 1, ALU.bitwise_and))
                        c.seq(v.tensor_copy(lo[:, :], loi[:, :]))
                        c.seq(v.tensor_single_scalar(loi[:, :], dst1[:, :], 7, ALU.logical_shift_right))
                        c.seq(v.tensor_copy(hi[:, :], loi[:, :]))
                        c.seq(v.tensor_scalar(dstf[:, :], dstf[:, :], float(N - 1), None, ALU.min))
                        c.seq(v.tensor_copy(dst1[:, :], dstf[:, :]))

        def sort_phase(E, T, J, key_dram, payloads, keys_dram, table, endrow, none_row, firstrow=None):
            W = 1 + len(payloads)
            outer, osb, _, osem = phase()
            with outer:
                B = -(-T // P)
                TB = T // B
                assert TB * B == T
                full, rest = E // P, E % P
                key, pay = osb("key", [P, T]), osb("pay", [P, T, W])
                loi = osb("loi", [P, T], I32)
                lo, hi = osb("lo", [P, T + J]), osb("hi", [P, T + J])
                counts, first, end = osb("counts", [P, NH]), osb("first", [P, NH]), osb("end", [P, NH])

                def load_block():
                    ctx, sb, ps, sem = phase()
                    with ctx:
                        raw = [sb(f"raw{n}", [P, B, P], I32) for n in range(W)]
                        rawf = [sb(f"rawf{n}", [P, B, P]) for n in range(W)]
                        psT = ps("psT", [P, 2, 512])
                        cleared, r_in, floats, turned, copied, k_out = (sem(n) for n in ("cleared", "r_in", "floats", "turned", "copied", "k_out"))
                        n_in, drained = [0], sem("drained")
                        with nc.Block() as block:
                            @block.sync
                            def _(sp):
                                if full < T:
                                    sp.wait_ge(cleared, 1)
                                for n, dr in enumerate([key_dram] + payloads):
                                    for b in range(B):
                                        whole = min(TB, full - b * TB)
                                        o = raw[n] if dr.dtype == I32 else raw[n][:, :, :].bitcast(F32)
                                        sp.dma_start(o[0:whole, b, :], dr[b * TB * P:(b * TB + whole) * P].rearrange("(t e) -> t e", e=P)).then_inc(r_in, 16)
                                        n_in[0] += 16
                                    if rest:
                                        sp.dma_start(o[full % TB:full % TB + 1, full // TB, 0:rest], dr[full * P:E].unsqueeze(0)).then_inc(r_in, 16)
                                        n_in[0] += 16
                                sp.wait_ge(floats, 1)
                                sp.dma_start(keys_dram.rearrange("(b t e) -> t b e", t=TB, e=P), rawf[0][0:TB, :, :]).then_inc(k_out, 16)
                                sp.wait_ge(k_out, 16)

                            @block.vector
                            def _(dve):
                                c = Count(dve, copied)
                                if full < T:
                                    c.inc(v.memset(raw[0][:, :, :], PAD_DST))
                                    for n in range(1, W):
                                        c.inc(v.memset(raw[n][:, :, :], 0))
                                    c.wait()
                                    dve.sem_inc(cleared, 1)
                                dve.wait_ge(r_in, n_in[0])
                                for n, dr in enumerate([key_dram] + payloads):
                                    i0 = raw[n][0:TB, :, :] if dr.dtype == I32 else raw[n][:, :, :].bitcast(F32)[0:TB, :, :]
                                    c.inc(v.tensor_copy(rawf[n][0:TB, :, :], i0))
                                c.wait()
                                dve.sem_inc(floats, 1)
                                m = 0
                                for n, dr in enumerate([key_dram] + payloads):
                                    for b in range(B):
                                        m += 1
                                        dve.wait_ge(turned, m)
                                        o = pay[:, b * TB:(b + 1) * TB, n]
                                        if dr.dtype == I32:
                                            o = o.bitcast(I32)
                                        if n == 0:
                                            c.inc(v.tensor_copy(key[:, b * TB:(b + 1) * TB], psT[:, m % 2, 0:TB]))
                                        c.seq(v.tensor_copy(o, psT[:, m % 2, 0:TB]))
                                        dve.sem_inc(drained, 1)
                                keyi = pay[:, :, 0].bitcast(I32)
                                c.seq(v.tensor_single_scalar(loi[:, :], keyi, P - 1, ALU.bitwise_and))
                                c.inc(v.memset(lo[:, T:T + J], 0.0))
                                c.seq(v.tensor_copy(lo[:, 0:T], loi[:, :]))
                                c.seq(v.tensor_single_scalar(loi[:, :], keyi, 7, ALU.logical_shift_right))
                                c.inc(v.memset(hi[:, T:T + J], 0.0))
                                c.seq(v.tensor_copy(hi[:, 0:T], loi[:, :]))

                            @block.tensor
                            def _(pe):
                                pe.wait_ge(floats, 1)
                                m = 0
                                for n in range(W):
                                    for b in range(B):
                                        m += 1
                                        if m > 2:
                                            pe.wait_ge(drained, m - 2)
                                        nc.tensor.transpose(psT[:, m % 2, 0:TB], rawf[n][0:TB, b, :], ident[0:TB, 0:TB]).then_inc(turned, 1)

                def place_block():
                    ctx, sb, ps, sem = phase()
                    with ctx:
                        onelo, onehi = sb("onelo", [P, 2, J, P], BF16), sb("onehi", [P, 2, J, NH], BF16)
                        lowT = sb("lowT", [P, 2, J, P], BF16)
                        identb = sb("identb", [P, P], BF16)
                        keyS = sb("keyS", [P, 2, J])
                        kb = sb("kb", [P, 2, J, P])
                        grown, base, resets = sb("grown", [P, NH, J + 1]), sb("base", [P, NH, J + 1]), sb("resets", [P, NH, J + 1])
                        split = sb("split", [P, 2, J, 2, NH], BF16)
                        posA, posB = sb("posA", [P, 2, J]), sb("posB", [P, 2, J])
                        posS, payS = sb("posS", [P, 2, J], I32), sb("payS", [P, 2, J, W])
                        junk1, junk2 = sb("junk1", [P, J // 2, 2, NH]), sb("junk2", [P, J, P], BF16)
                        psH, psL = ps("psH", [P, 2, 512]), ps("psL", [P, 2, 512])
                        assert J * NH <= 512
                        psT = ps("psT", [P, 2, 1024], BF16)
                        kb_in = [sem("kb_in0"), sem("kb_in1")]
                        moved = [sem("moved0"), sem("moved1")]
                        built, turned, lows, splits, histed, looked, selected, placed, chain = (
                            sem(n) for n in ("built", "turned", "lows", "splits", "histed", "looked", "selected", "placed", "chain"))
                        QT = 4
                        quads = [(q, min(q + QT, J)) for q in range(0, J, QT)]
                        NQ = len(quads)
                        assert NQ % 2 == 0 and J % 2 == 0
                        trips = T // J // 2
                        with nc.Block() as block:
                            @block.sync
                            def _(sp):
                                def body(i):
                                    for s in range(2):
                                        if not zero(i):
                                            hold(sp, placed, 2 * i + s - 1)
                                        sp.dma_start(kb[:, s, :, :].rearrange("p j e -> p (j e)"),
                                                     keys_dram[bass.ds((2 * i + s) * J * P, J * P)].partition_broadcast(P)).then_inc(kb_in[s], 16)
                                loop(sp, trips, body)

                            @block.vector
                            def _(dve):
                                c = Count(dve, chain)
                                c.seq(v.tensor_copy(identb[:, :], ident[:, :]))

                                def build(m, s):
                                    cols = bass.ds(m * J, J)
                                    v.tensor_tensor(onelo[:, s, :, :], iota_free[:, :].unsqueeze(1).broadcast_to([P, J, P]),
                                                    lo[:, cols].unsqueeze(2).broadcast_to([P, J, P]), ALU.is_equal)
                                    v.tensor_tensor(onehi[:, s, :, :], iota_free[:, 0:NH].unsqueeze(1).broadcast_to([P, J, NH]),
                                                    hi[:, cols].unsqueeze(2).broadcast_to([P, J, NH]), ALU.is_equal).then_inc(built, 1)
                                c.inc(v.memset(resets[:, :, 1:J + 1], 1.0))
                                c.inc(v.memset(resets[:, :, 0:1], 0.0))
                                c.seq(v.tensor_copy(base[:, :, J], first[:, :]))
                                build(0, 0)

                                def body(i):
                                    c.at(i, 2 * 10)
                                    for s in range(2):
                                        m = 2 * i + s
                                        cols = bass.ds(m * J, J)
                                        if s or not zero(i):
                                            hold(dve, turned, m * NQ)
                                        build(m + 1, 1 - s)
                                        if not zero(i):
                                            hold(dve, moved[s], 16 * J * i)
                                        c.inc(v.tensor_copy(keyS[:, s, :], key[:, cols]))
                                        c.inc(v.tensor_copy(grown[:, :, 0], base[:, :, J]))
                                        hold(dve, histed, m + 1)
                                        c.inc(v.tensor_copy(grown[:, :, 1:J + 1], psH[:, s, 0:J * NH].rearrange("p (j h) -> p h j", h=NH)))
                                        hold(dve, chain, c.base + c.n)
                                        c.seq(v.tensor_tensor_scan(base[:, :, :].rearrange("p h j -> p (h j)"), resets[:, :, :].rearrange("p h j -> p (h j)"),
                                                                   grown[:, :, :].rearrange("p h j -> p (h j)"), 0.0, ALU.mult, ALU.add))
                                        before = base[:, :, 0:J].rearrange("p h j -> p j h")
                                        c.seq(v.tensor_copy(split[:, s, :, 0, :], before))
                                        v.tensor_tensor(split[:, s, :, 1, :], before, split[:, s, :, 0, :], ALU.subtract).then_inc(splits, 1)
                                        hold(dve, kb_in[s], 16 * (i + 1))
                                        for u in range(J):
                                            v.scalar_tensor_tensor(junk2[:, u, :], kb[:, s, u, :], keyS[:, s, u:u + 1], below[:, :],
                                                                   ALU.is_equal, ALU.mult, accum_out=posB[:, s, u:u + 1])
                                        hold(dve, looked, m + 1)
                                        for hf in range(2):
                                            js = slice(hf * (J // 2), (hf + 1) * (J // 2))
                                            ins = v.tensor_tensor(junk1[:, :, :, :], psL[:, hf, 0:J * NH].rearrange("p (u a h) -> p u a h", a=2, h=NH),
                                                                  onehi[:, s, js, :].unsqueeze(2).broadcast_to([P, J // 2, 2, NH]), ALU.mult)
                                            c.seq(ins)
                                            ins = v.tensor_reduce(posA[:, s, js], junk1[:, :, :, :].rearrange("p u a h -> p u (a h)"), AX, ALU.add)
                                            c.seq(ins)
                                        dve.sem_inc(selected, 1)
                                        c.seq(v.tensor_tensor(posA[:, s, :], posA[:, s, :], posB[:, s, :], ALU.add))
                                        v.tensor_copy(posS[:, s, :], posA[:, s, :])
                                        v.tensor_copy(payS[:, s, :, :], pay[:, cols, :]).then_inc(placed, 1)
                                        hold(dve, placed, m + 1)
                                loop(dve, trips, body)
                                c.end(trips)

                            @block.tensor
                            def _(pe):
                                pe.wait_ge(chain, 1)

                                def hist_and_turn(m, s, first_two):
                                    hold(pe, built, m + 1)
                                    for u in range(J):
                                        ins = nc.tensor.matmul(psH[:, s, u * NH:(u + 1) * NH], onelo[:, s, u, :], onehi[:, s, u, :], start=True, stop=True)
                                    ins.then_inc(histed, 1)
                                    for q, (a0, a1) in enumerate(quads):
                                        if q >= 2 or not first_two:
                                            hold(pe, lows, m * NQ + q - 1)
                                        for u in range(a0, a1):
                                            ins = nc.tensor.transpose(psT[:, q % 2, (u - a0) * P:(u - a0 + 1) * P], onelo[:, s, u, :], identb[:, :])
                                        ins.then_inc(turned, 1)
                                hist_and_turn(0, 0, True)

                                def body(i):
                                    for s in range(2):
                                        m = 2 * i + s
                                        if s or not zero(i):
                                            hold(pe, splits, m)
                                        hist_and_turn(m + 1, 1 - s, False)
                                        hold(pe, splits, m + 1)
                                        if s or not zero(i):
                                            hold(pe, selected, m)
                                        for u in range(J):
                                            hf, at = u // (J // 2), u % (J // 2)
                                            ins = nc.tensor.matmul(psL[:, hf, at * 2 * NH:(at + 1) * 2 * NH], lowT[:, s, u, :],
                                                                   split[:, s, u, :, :].rearrange("p a h -> p (a h)"), start=True, stop=True)
                                        ins.then_inc(looked, 1)
                                loop(pe, trips, body)

                            @block.scalar
                            def _(act):
                                def lower(m, s, q, a0, a1):
                                    hold(act, turned, m * NQ + q + 1)
                                    a.copy(lowT[:, s, a0:a1, :].rearrange("p u e -> p (u e)"), psT[:, q % 2, 0:(a1 - a0) * P]).then_inc(lows, 1)
                                for q, (a0, a1) in enumerate(quads):
                                    lower(0, 0, q, a0, a1)

                                def body(i):
                                    for s in range(2):
                                        m = 2 * i + s
                                        if s or not zero(i):
                                            hold(act, looked, m)
                                        for q, (a0, a1) in enumerate(quads):
                                            lower(m + 1, 1 - s, q, a0, a1)
                                loop(act, trips, body)

                            @block.gpsimd
                            def _(pool):
                                with pool.Fori(0, trips) as i:
                                    for s in range(2):
                                        hold(pool, placed, 2 * i + s + 1)
                                        for u in range(J):
                                            pool.indirect_dma_start(out=table, out_offset=bass.IndirectOffsetOnAxis(ap=posS[:, s, u:u + 1], axis=0),
                                                                    in_=payS[:, s, u, :].bitcast(I32), in_offset=None).then_inc(moved[s], 16)
                                for s in range(2):
                                    pool.wait_ge(moved[s], 16 * J * trips)
                load_block()
                count_block(lo, hi, T, J, counts)
                prefix_block(counts, first, end, endrow, none_row, firstrow)
                place_block()

        def reload_phase(table, NJ, fields, keep, pen, cont):
            ctx, sb, ps, sem = phase()
            with ctx:
                W = table.shape[1]
                rows_in = sb("rows_in", [P, NJ, W], I32)
                keyf, nexti, nextf, tmp = sb("keyf", [P, NJ]), sb("nexti", [P, 1], I32), sb("nextf", [P, 1]), sb("tmp", [P, 1])
                penx = pen if pen is not None else sb("penx", [P, NJ])
                r_in, cleared, chain = sem("r_in"), sem("cleared"), sem("chain")
                with nc.Block() as block:
                    @block.sync
                    def _(sp):
                        grid = table.rearrange("(p j) w -> p j w", j=NJ)
                        sp.dma_start(rows_in[:, :, :], grid).then_inc(r_in, 16)
                        sp.wait_ge(cleared, 1)
                        sp.dma_start(nexti[0:P - 1, :], grid[1:P, 0, 0:1], allow_slow_non_contiguous=True).then_inc(r_in, 16)

                    @block.vector
                    def _(dve):
                        c = Count(dve, chain)
                        c.seq(v.memset(nexti[:, :], -2))
                        dve.sem_inc(cleared, 1)
                        dve.wait_ge(r_in, 32)
                        c.inc(v.tensor_copy(keyf[:, :], rows_in[:, :, 0]))
                        c.inc(v.tensor_copy(nextf[:, :], nexti[:, :]))
                        for n, tile in fields:
                            i0 = rows_in[:, :, n] if tile.dtype == I32 else rows_in[:, :, n].bitcast(F32)
                            c.inc(v.tensor_copy(tile[:, :], i0))
                        c.wait()
                        run_flags(dve, c, keyf, nextf, NJ, keep, penx, cont, tmp)

        def gnn0_phase():
            ctx, sb, ps, sem = phase()
            with ctx:
                S = 4
                G = sb("G", [P, S, J1, D])
                wS, kS = sb("wS", [P, S, J1]), sb("kS", [P, S, J1])
                iS = sb("iS", [P, S, J1], I32)
                carry = sb("carry", [P, D])
                zrow = sb("zrow", [1, D])
                got, stored = [sem(f"got{s}") for s in range(S)], [sem(f"stored{s}") for s in range(S)]
                staged, cols, scaled, summed = sem("staged"), sem("cols"), sem("scaled"), sem("summed")
                chain, z_ready, z_stored = sem("chain"), sem("z_ready"), sem("z_stored")
                with nc.Block() as block:
                    @block.gpsimd
                    def _(pool):
                        def body(i):
                            for s in range(S):
                                if not zero(i):
                                    hold(pool, stored[s], 16 * i)
                                nc.gpsimd.tensor_copy(iS[:, s, :], nbr0[:, bass.ds((S * i + s) * J1, J1)]).then_inc(staged, 1)
                                hold(pool, staged, S * i + s + 1)
                                for j in range(J1):
                                    pool.indirect_dma_start(out=G[:, s, j, :], out_offset=None, in_=xn_tab,
                                                            in_offset=bass.IndirectOffsetOnAxis(ap=iS[:, s, j:j + 1], axis=0)).then_inc(got[s], 16)
                        loop(pool, NB1 // S, body)

                    @block.scalar
                    def _(act):
                        with act.Fori(0, NB1 // S) as i:
                            for s in range(S):
                                hold(act, cols, S * i + s + 1)
                                hold(act, got[s], 16 * J1 * (i + 1))
                                for j in range(J1):
                                    a.mul(G[:, s, j, :], G[:, s, j, :], wS[:, s, j:j + 1]).then_inc(scaled, 1)

                    @block.vector
                    def _(dve):
                        c = Count(dve, chain)
                        v.memset(zrow[:, :], 0.0).then_inc(z_ready, 1)
                        c.seq(v.memset(carry[:, :], 0.0))

                        def body(i):
                            c.at(i, S * (J1 + 1))
                            for s in range(S):
                                b = S * i + s
                                sl = bass.ds(b * J1, J1)
                                if not zero(i):
                                    hold(dve, scaled, (b - S + 1) * J1)
                                v.tensor_copy(wS[:, s, :], w0[:, sl])
                                v.tensor_copy(kS[:, s, :], keep0[:, sl]).then_inc(cols, 1)
                                hold(dve, cols, b + 1)
                                for j in range(J1):
                                    hold(dve, scaled, b * J1 + j + 1)
                                    prev = carry[:, :] if j == 0 else G[:, s, j - 1, :]
                                    c.seq(v.scalar_tensor_tensor(G[:, s, j, :], prev, kS[:, s, j:j + 1], G[:, s, j, :], ALU.mult, ALU.add))
                                c.seq(v.tensor_copy(carry[:, :], G[:, s, J1 - 1, :]))
                                dve.sem_inc(summed, 1)
                        loop(dve, NB1 // S, body)
                        c.end(NB1 // S)

                    @block.sync
                    def _(sp):
                        sp.wait_ge(z_ready, 1)
                        sp.dma_start(sum_tab[P * NJ1:P * NJ1 + 1, :], zrow[:, :]).then_inc(z_stored, 16)
                        tab = sum_tab[0:P * NJ1, :].rearrange("(p j) f -> p j f", j=NJ1)
                        with sp.Fori(0, NB1 // S) as i:
                            for s in range(S):
                                sp.wait_ge(summed, S * i + s + 1)
                                sp.dma_start(tab[:, bass.ds((S * i + s) * J1, J1), :], G[:, s, :, :]).then_inc(stored[s], 16)
                        sp.wait_ge(z_stored, 16)
                        for s in range(S):
                            sp.wait_ge(stored[s], 16 * (NB1 // S))
                gnn0_dense(carry)

        def gnn0_dense(tails):
            ctx, sb, ps, sem = phase()
            with ctx:
                own = sb("own", [P, NT, D])
                HW = NP // 8
                NXT, O1T = sb("NXT", [P, 2, NP]), sb("O1T", [P, 2, NP])
                H = [sb("H1", [P, 2, D]), sb("H2", [P, 2, D])]
                gam, bet = sb("gam", [P, 2]), sb("bet", [P, 2])
                cm, cmS, oh = sb("cm", [P, NT]), sb("cmS", [P, GT]), sb("oh", [P, GT, P])
                nx = sb("nx", [P, GT, D])
                mean, var, scl, bia, junk = (sb(n, [P, 2]) for n in ("mean", "var", "scl", "bia", "junk"))
                big = own
                psA, psT = ps("psA", [P, 2, 512]), ps("psT", [P, 2, 512])
                ps1 = ps("ps1", [P, 2, 512])
                h_in, own_in, chain, signed = sem("h_in"), sem("own_in"), sem("chain"), sem("signed")
                hots, tailed, added, turned, columns = sem("hots"), sem("tailed"), sem("added"), sem("turned"), sem("columns")
                mm1, ev1 = sem("mm1"), sem("ev1")
                a_stat, v_stat, tanhs, mm2, resid = sem("a_stat"), sem("v_stat"), sem("tanhs"), sem("mm2"), sem("resid")
                tt = sb("tt", [P, 2, GT * P])
                minus = {(1, 0), (2, 0), (3, 0), (2, 1), (3, 2), (1, 3)}
                with nc.Block() as block:
                    @block.sync
                    def _(sp):
                        for Ht, wd in zip(H, (g0_w1, g0_w2)):
                            for ra in range(4):
                                for cb in range(4):
                                    comp = ra ^ cb
                                    sp.dma_start(Ht[64 * (ra % 2):64 * (ra % 2) + 64, ra // 2, 64 * cb:64 * cb + 64],
                                                 wd[:, 64 * comp:64 * comp + 64]).then_inc(h_in, 16)
                        sp.dma_start(gam[:, :], g0_gamma.rearrange("(m p) -> p m", p=P), allow_slow_non_contiguous=True).then_inc(h_in, 16)
                        sp.dma_start(bet[:, :], g0_beta.rearrange("(m p) -> p m", p=P), allow_slow_non_contiguous=True).then_inc(h_in, 16)

                    @block.gpsimd
                    def _(pool):
                        for t in range(NT):
                            pool.indirect_dma_start(out=own[:, t, :], out_offset=None, in_=sum_tab[0:P * NJ1 + 1, :],
                                                    in_offset=bass.IndirectOffsetOnAxis(ap=end0[:, t:t + 1], axis=0)).then_inc(own_in, 16)

                    @block.vector
                    def _(dve):
                        c = Count(dve, chain)
                        c.seq(v.tensor_scalar(cm[:, :], iota_free[:, 0:NT], -float(P), cont0[:, :], ALU.mult, ALU.add))
                        dve.wait_ge(h_in, 16 * 34)
                        for Ht in H:
                            for ra, cb in sorted(minus):
                                blk = Ht[64 * (ra % 2):64 * (ra % 2) + 64, ra // 2, 64 * cb:64 * cb + 64]
                                c.seq(v.tensor_scalar(blk, blk, -1.0, None, ALU.mult))
                        dve.sem_inc(signed, 1)
                        dve.wait_ge(own_in, 16 * NT)

                        def body(g):
                            c.at(g, 1)
                            c.inc(v.tensor_copy(cmS[:, :], cm[:, bass.ds(g * GT, GT)]))
                            hold(dve, chain, c.base + c.n)
                            if not zero(g):
                                hold(dve, tailed, g * GT)
                                hold(dve, turned, g * GT)
                            for s in range(GT):
                                v.tensor_scalar(oh[:, s, :], iota_free[:, :], cmS[:, s:s + 1], None, ALU.is_equal).then_inc(hots, 1)
                            for s in range(GT):
                                hold(dve, tailed, g * GT + s + 1)
                                v.tensor_tensor(nx[:, s, :], psA[:, s % 2, 0:D], row(own, g * GT + s), ALU.add).then_inc(added, 1)
                        loop(dve, NG, body)
                        c.end(NG)
                        dve.wait_ge(ev1, 16)
                        for m in range(2):
                            c.inc(v.tensor_reduce(junk[:, m:m + 1], O1T[:, m, 0:N], AX, ALU.add))
                        c.wait()
                        c.seq(v.tensor_scalar(mean[:, :], junk[:, :], -1.0 / N, None, ALU.mult))
                        dve.sem_inc(v_stat, 1)
                        dve.wait_ge(a_stat, 3)
                        c.seq(v.reciprocal(scl[:, :], scl[:, :]))
                        c.seq(v.tensor_tensor(scl[:, :], scl[:, :], gam[:, :], ALU.mult))
                        c.seq(v.tensor_tensor(bia[:, :], mean[:, :], scl[:, :], ALU.mult))
                        c.seq(v.tensor_tensor(bia[:, :], bia[:, :], bet[:, :], ALU.add))
                        dve.sem_inc(v_stat, 1)
                        with dve.Fori(0, NG) as g:
                            for s in range(GT):
                                hold(dve, mm2, g * GT + s + 1)
                                v.tensor_tensor(row(X, g * GT + s), psA[:, s % 2, 0:D], row(X, g * GT + s), ALU.add).then_inc(resid, 1)

                    @block.tensor
                    def _(pe):
                        def sums(g):
                            for s in range(GT):
                                hold(pe, hots, g * GT + s + 1)
                                if not zero(g) or s >= 2:
                                    hold(pe, added, g * GT + max(s - 1, 0))
                                nc.tensor.matmul(psA[:, s % 2, 0:D], oh[:, s, :], tails[:, :], start=True, stop=True).then_inc(tailed, 1)
                            for s in range(GT):
                                hold(pe, added, g * GT + s + 1)
                                if not zero(g) or s >= 2:
                                    hold(pe, columns, g * GT + max(s - 1, 0))
                                nc.tensor.transpose(psT[:, s % 2, 0:P], nx[:, s, 0:P], ident[:, :])
                                nc.tensor.transpose(psT[:, s % 2, P:D], nx[:, s, P:D], ident[:, :]).then_inc(turned, 1)
                        loop(pe, NG, sums)
                        pe.wait_ge(columns, NT)
                        pe.wait_ge(signed, 1)

                        def dense(n):
                            for m in range(2):
                                if not zero(n):
                                    hold(pe, ev1, 2 * n + m - 1)
                                for k in range(2):
                                    ins = nc.tensor.matmul(ps1[:, m, 0:HW], H[0][:, k, m * P:(m + 1) * P], NXT[:, k, bass.ds(n * HW, HW)],
                                                           start=(k == 0), stop=(k == 1))
                                ins.then_inc(mm1, 1)
                        loop(pe, 8, dense)

                        def last(g):
                            hold(pe, tanhs, g + 1)
                            for s in range(GT):
                                if not zero(g) or s >= 2:
                                    hold(pe, resid, g * GT + max(s - 1, 0))
                                for k in range(2):
                                    ins = nc.tensor.matmul(psA[:, s % 2, 0:D], tt[:, k, s * P:(s + 1) * P], H[1][:, k, :], start=(k == 0), stop=(k == 1))
                                ins.then_inc(mm2, 1)
                        loop(pe, NG, last)

                    @block.scalar
                    def _(act):
                        with act.Fori(0, NG) as g:
                            for s in range(GT):
                                hold(act, turned, g * GT + s + 1)
                                a.copy(NXT[:, :, bass.ds((g * GT + s) * P, P)], psT[:, s % 2, 0:D].rearrange("p (k c) -> p k c", k=2)).then_inc(columns, 1)
                        with act.Fori(0, 8) as n:
                            for m in range(2):
                                hold(act, mm1, 2 * n + m + 1)
                                a.copy(O1T[:, m, bass.ds(n * HW, HW)], ps1[:, m, 0:HW]).then_inc(ev1, 1)
                        act.wait_ge(v_stat, 1)
                        flat = own[:, :, :].rearrange("p t d -> p (t d)")
                        for m in range(2):
                            a.activation(flat[:, m * N:(m + 1) * N], O1T[:, m, 0:N], ACT.Square, bias=mean[:, m:m + 1],
                                         accum_out=var[:, m:m + 1]).then_inc(a_stat, 1)
                        act.wait_ge(a_stat, 2)
                        a.activation(scl[:, :], var[:, :], ACT.Sqrt, bias=eps_col[:, :], scale=1.0 / N).then_inc(a_stat, 1)
                        act.wait_ge(v_stat, 2)

                        def body(g):
                            if not zero(g):
                                hold(act, mm2, g * GT)
                            for m in range(2):
                                ins = a.activation(tt[:, m, :], O1T[:, m, bass.ds(g * GT * P, GT * P)], ACT.Tanh,
                                                   bias=bia[:, m:m + 1], scale=scl[:, m:m + 1])
                            ins.then_inc(tanhs, 1)
                        loop(act, NG, body)

        def merge_phase(H, F, tails, cont, endrow, table, agg, self_score=None, self_rows=None, eps=None):
            W, C = 2 * H + F, F // H
            CW = 2 * H + F + 1
            ctx, sb, ps, sem = phase()
            with ctx:
                own, other = sb("own", [P, NT, W]), sb("other", [P, NT, CW])
                diag, eqm, tmp = sb("diag", [P, H + 1, P]), sb("eqm", [P, P]), sb("tmp", [P, P])
                penm, ref, lead, tw = sb("penm", [P, P]), sb("ref", [P, H]), sb("lead", [P, 1]), sb("tw", [P, H])
                tw_rows = sb("tw_rows", [P, CW])
                cm, cmS, oh = sb("cm", [P, NT]), sb("cmS", [P, GT]), sb("oh", [P, GT, P])
                top_, wts, den = sb("top_", [P, NT, H]), sb("wts", [P, 3, NT, H]), sb("den", [P, NT, H])
                zrow = sb("zrow", [1, W])
                HB = -(-(H + 1) // 4)
                psB, psA = ps("psB", [P, HB, 512]), ps("psA", [P, 2, 512])
                own_in, diags, spread, targ, texp, hots, tailed, taken, warg, wexp, chain = (
                    sem(n) for n in ("own_in", "diags", "spread", "targ", "texp", "hots", "tailed", "taken", "warg", "wexp", "chain"))
                z_ready, z_stored = sem("z_ready"), sem("z_stored")
                n_self = 1 if self_score is not None else 0
                with nc.Block() as block:
                    @block.sync
                    def _(sp):
                        sp.wait_ge(z_ready, 1)
                        sp.dma_start(table[table.shape[0] - 1:table.shape[0], :], zrow[:, :]).then_inc(z_stored, 16)

                    @block.gpsimd
                    def _(pool):
                        pool.wait_ge(z_stored, 16)
                        for t in range(NT):
                            pool.indirect_dma_start(out=own[:, t, :], out_offset=None, in_=table,
                                                    in_offset=bass.IndirectOffsetOnAxis(ap=endrow[:, t:t + 1], axis=0)).then_inc(own_in, 16)

                    @block.vector
                    def _(dve):
                        c = Count(dve, chain)
                        c.seq(v.memset(zrow[:, H:W], 0.0))
                        c.seq(v.memset(zrow[:, 0:H], -BIG))
                        dve.sem_inc(z_ready, 1)
                        for h in range(H):
                            c.inc(v.tensor_scalar(diag[:, h, :], ident[:, :], tails[:, h:h + 1], None, ALU.mult))
                        c.inc(v.tensor_scalar(diag[:, H, :], ident[:, :], cont[:, :], None, ALU.mult))
                        c.inc(v.tensor_scalar(cm[:, :], iota_free[:, 0:NT], -float(P), cont[:, :], ALU.mult, ALU.add))
                        c.wait()
                        dve.sem_inc(diags, 1)
                        dve.wait_ge(spread, 1)
                        bc = lambda h: psB[:, h // 4, (h % 4) * P:(h % 4 + 1) * P]
                        c.seq(v.tensor_scalar(eqm[:, :], bc(H), cont[:, :], None, ALU.is_equal))
                        c.seq(v.tensor_scalar(penm[:, :], eqm[:, :], 1.0, BIG, ALU.subtract, ALU.mult))
                        for h in range(H):
                            c.seq(v.tensor_tensor(tmp[:, :], bc(h), penm[:, :], ALU.add))
                            c.seq(v.tensor_reduce(ref[:, h:h + 1], tmp[:, :], AX, ALU.max))
                        c.seq(v.tensor_tensor(tmp[:, :], eqm[:, :], upper[:, :], ALU.mult))
                        c.seq(v.tensor_reduce(lead[:, :], tmp[:, :], AX, ALU.add))
                        c.seq(v.tensor_scalar(lead[:, :], lead[:, :], 1.5, None, ALU.is_lt))
                        c.seq(v.tensor_tensor(tw[:, :], tails[:, 0:H], ref[:, :], ALU.subtract))
                        dve.sem_inc(targ, 1)
                        dve.wait_ge(texp, 1)
                        c.inc(v.tensor_scalar(tw_rows[:, 0:H], ref[:, :], lead[:, :], None, ALU.mult))
                        c.inc(v.tensor_copy(tw_rows[:, CW - 1:CW], lead[:, :]))
                        c.inc(v.tensor_tensor(tw_rows[:, H:2 * H], tails[:, H:2 * H], tw[:, :], ALU.mult))
                        c.seq(v.tensor_tensor(tw_rows[:, 2 * H:W].rearrange("p (h c) -> p h c", c=C), tails[:, 2 * H:W].rearrange("p (h c) -> p h c", c=C),
                                              tw[:, :].unsqueeze(2).broadcast_to([P, H, C]), ALU.mult))

                        def body(g):
                            c.at(g, 1)
                            if not zero(g):
                                hold(dve, tailed, g * GT)
                            c.inc(v.tensor_copy(cmS[:, :], cm[:, bass.ds(g * GT, GT)]))
                            hold(dve, chain, c.base + c.n)
                            for s in range(GT):
                                v.tensor_scalar(oh[:, s, :], iota_free[:, :], cmS[:, s:s + 1], None, ALU.is_equal).then_inc(hots, 1)
                            for s in range(GT):
                                hold(dve, tailed, g * GT + s + 1)
                                v.tensor_copy(row(other, g * GT + s), psA[:, s % 2, 0:CW]).then_inc(taken, 1)
                        loop(dve, NG, body)
                        c.end(NG)
                        dve.wait_ge(taken, NT)
                        dve.wait_ge(own_in, 16 * NT)
                        om, oR = own[:, :, 0:H], other[:, :, 0:H]
                        has = other[:, :, CW - 1:CW]
                        c.seq(v.tensor_scalar(has, has, 1.0, BIG, ALU.subtract, ALU.mult))
                        c.seq(v.tensor_tensor(oR, oR, has.broadcast_to([P, NT, H]), ALU.add))
                        c.seq(v.tensor_tensor(top_[:, :, :], om, oR, ALU.max))
                        if n_self:
                            c.seq(v.tensor_tensor(top_[:, :, :], top_[:, :, :], self_score, ALU.max))
                            c.inc(v.tensor_tensor(wts[:, 2, :, :], self_score, top_[:, :, :], ALU.subtract))
                        c.inc(v.tensor_tensor(wts[:, 0, :, :], om, top_[:, :, :], ALU.subtract))
                        c.seq(v.tensor_tensor(wts[:, 1, :, :], oR, top_[:, :, :], ALU.subtract))
                        dve.sem_inc(warg, 1)
                        dve.wait_ge(wexp, 1)
                        wide = lambda n: wts[:, n, :, :].unsqueeze(3).broadcast_to([P, NT, H, C])
                        heads = lambda t, a0: t[:, :, a0:a0 + F].rearrange("p t (h c) -> p t h c", c=C)
                        c.inc(v.tensor_tensor(own[:, :, H:2 * H], own[:, :, H:2 * H], wts[:, 0, :, :], ALU.mult))
                        c.seq(v.tensor_tensor(other[:, :, H:2 * H], other[:, :, H:2 * H], wts[:, 1, :, :], ALU.mult))
                        c.seq(v.tensor_tensor(den[:, :, :], own[:, :, H:2 * H], other[:, :, H:2 * H], ALU.add))
                        for t in range(NT):
                            hs = lambda tile: tile[:, t, 2 * H:2 * H + F].rearrange("p (h c) -> p h c", c=C)
                            wv = lambda n: wts[:, n, t, :].unsqueeze(2).broadcast_to([P, H, C])
                            c.inc(v.tensor_tensor(hs(own), hs(own), wv(0), ALU.mult))
                            c.inc(v.tensor_tensor(hs(other), hs(other), wv(1), ALU.mult))
                        c.wait()
                        c.seq(v.tensor_tensor(agg[:, :, :], own[:, :, 2 * H:W], other[:, :, 2 * H:W], ALU.add))
                        if n_self:
                            c.seq(v.tensor_tensor(den[:, :, :], den[:, :, :], wts[:, 2, :, :], ALU.add))
                            for t in range(NT):
                                c.inc(v.tensor_tensor(own[:, t, 2 * H:W].rearrange("p (h c) -> p h c", c=C), self_rows[:, t, 0:F].rearrange("p (h c) -> p h c", c=C),
                                                      wts[:, 2, t, :].unsqueeze(2).broadcast_to([P, H, C]), ALU.mult))
                            c.wait()
                            c.seq(v.tensor_tensor(agg[:, :, :], agg[:, :, :], own[:, :, 2 * H:W], ALU.add))
                        c.seq(v.tensor_scalar(den[:, :, :], den[:, :, :], eps or 0.0, 1e-30, ALU.add, ALU.max))
                        c.seq(v.reciprocal(den[:, :, :], den[:, :, :]))
                        for t in range(NT):
                            c.inc(v.tensor_tensor(agg[:, t, :].rearrange("p (h c) -> p h c", c=C), agg[:, t, :].rearrange("p (h c) -> p h c", c=C),
                                                  den[:, t, :].unsqueeze(2).broadcast_to([P, H, C]), ALU.mult))
                        c.wait()

                    @block.tensor
                    def _(pe):
                        pe.wait_ge(diags, 1)
                        for b in range(HB):
                            w = min(4, H + 1 - 4 * b)
                            ins = nc.tensor.matmul(psB[:, b, 0:w * P], ones[:, :], diag[:, 4 * b:4 * b + w, :].rearrange("p h c -> p (h c)"), start=True, stop=True)
                        ins.then_inc(spread, 1)

                        def body(g):
                            for s in range(GT):
                                hold(pe, hots, g * GT + s + 1)
                                if not zero(g) or s >= 2:
                                    hold(pe, taken, g * GT + max(s - 1, 0))
                                nc.tensor.matmul(psA[:, s % 2, 0:CW], oh[:, s, :], tw_rows[:, :], start=True, stop=True).then_inc(tailed, 1)
                        loop(pe, NG, body)

                    @block.scalar
                    def _(act):
                        act.wait_ge(targ, 1)
                        a.activation(tw[:, :], tw[:, :], ACT.Exp).then_inc(texp, 1)
                        act.wait_ge(warg, 1)
                        n = 2 + n_self
                        a.activation(wts[:, 0:n, :, :].rearrange("p n t h -> p (n t h)"), wts[:, 0:n, :, :].rearrange("p n t h -> p (n t h)"), ACT.Exp).then_inc(wexp, 1)

        E0, FF0 = f0_w1.shape[0], f0_w1.shape[2]
        FC0 = FF0 // P
        HN = GT * P // 2
        STEPS = E0 * NG
        EXP_AT = STEPS - 3
        ye_tab = [dram(f"ye_tab{e}", [NP, D]) for e in range(E0)]

        def gat_phase(HG, self_score, XNT, b1T, tails, lo, hi, counts):
            H, F, W = 4, 16, 24
            ctx, sb, ps, sem = phase()
            with ctx:
                att = sb("att", [P, 2, F])
                prod = sb("prod", [P, NT, F])
                zeros = sb("zeros", [P, NJ2 * H])
                b1r, psB = sb("b1r", [E0 * FC0, P]), ps("psB", [P, 512])
                b1_in, b1_turned, b1_out = sem("b1_in"), sem("b1_turned"), sem("b1_out")
                att_in, chain, cleared, blank, stored, moved = (sem(n) for n in ("att_in", "chain", "cleared", "blank", "stored", "moved"))
                with nc.Block() as block:
                    @block.sync
                    def _(sp):
                        for n, dr in enumerate((f0_att_src, f0_att_dst)):
                            sp.dma_start(att[:, n, :], dr.rearrange("h e -> (h e)").partition_broadcast(P)).then_inc(att_in, 16)
                        sp.dma_start(b1r[:, :], f0_b1.rearrange("e (c p) -> (e c) p", p=P)).then_inc(b1_in, 16)
                        sp.wait_ge(cleared, 1)
                        sp.dma_start(adst_tab[0:E2, :].rearrange("(p j) w -> p (j w)", j=NJ2), zeros[:, :]).then_inc(blank, 16)
                        sp.wait_ge(chain, 6)
                        sp.dma_start(table_rows(h_tab), HG[:, :, :]).then_inc(stored, 16)
                        sp.wait_ge(stored, 16)

                    @block.vector
                    def _(dve):
                        c = Count(dve, chain)
                        v.memset(zeros[:, :], 0.0).then_inc(cleared, 1)
                        dve.wait_ge(att_in, 32)
                        for n in range(2):
                            c.seq(v.tensor_tensor(prod[:, :, :], HG[:, :, 0:F], att[:, n, :].unsqueeze(1).broadcast_to([P, NT, F]), ALU.mult))
                            c.seq(v.tensor_reduce(HG[:, :, F + H * n:F + H * (n + 1)], prod[:, :, :].rearrange("p t (h c) -> p t h c", h=H), AX, ALU.add))
                        c.seq(v.tensor_tensor(self_score[:, :, :], HG[:, :, F:F + H], HG[:, :, F + H:F + 2 * H], ALU.add))
                        c.seq(v.scalar_tensor_tensor(self_score[:, :, :], self_score[:, :, :], 0.2, self_score[:, :, :], ALU.mult, ALU.max))

                    @block.tensor
                    def _(pe):
                        pe.wait_ge(b1_in, 16)
                        nc.tensor.transpose(psB[:, 0:E0 * FC0], b1r[:, :], ident[0:E0 * FC0, 0:E0 * FC0]).then_inc(b1_turned, 1)

                    @block.scalar
                    def _(act):
                        act.wait_ge(b1_turned, 1)
                        a.copy(b1T[:, :], psB[:, 0:E0 * FC0]).then_inc(b1_out, 1)

                    @block.gpsimd
                    def _(pool):
                        pool.wait_ge(blank, 16)
                        pool.wait_ge(chain, 4)
                        for t in range(NT):
                            pool.indirect_dma_start(out=adst_tab, out_offset=bass.IndirectOffsetOnAxis(ap=first2[:, t:t + 1], axis=0),
                                                    in_=HG[:, t, F + H:W], in_offset=None).then_inc(moved, 16)
                        pool.wait_ge(moved, 16 * NT)
            ctx, sb, ps, sem = phase()
            with ctx:
                hs, hd, adst = sb("hs", [P, 2, J2, W]), sb("hd", [P, W]), sb("adst", [P, NJ2, H])
                iS = sb("iS", [P, 2, J2], I32)
                feat, score = sb("feat", [P, F, NJ2]), sb("score", [P, H, NJ2])
                M, AE = sb("M", [P, H, NJ2 + 1]), sb("AE", [P, 2, H, NJ2])
                ST = sb("ST", [P, NJ2, W])
                got = [sem("got0"), sem("got1")]
                first_in, adst_in = sem("first_in"), sem("adst_in")
                W1s, W2s = sb("W1s", [P, 2, 2, FF0]), sb("W2s", [P, 2, FC0, D])
                hT, Ye = sb("hT", [P, 2, FC0, GT * P]), sb("Ye", [P, 2, GT, D])
                psH = [ps("psH0", [P, 2, 512]), ps("psH1", [P, 2, 512])]
                psY = ps("psY", [P, 3, 512])
                w_in, y_stored = [sem("w_in0"), sem("w_in1")], [sem("y_stored0"), sem("y_stored1")]
                hidden, acted, rows_out, rows_read = (sem(n) for n in ("hidden", "acted", "rows_out", "rows_read"))
                onelo, onehi = sb("onelo", [P, 2, J1, P], BF16), sb("onehi", [P, 2, J1, NH], BF16)
                zerob, psC = sb("zerob", [P, P], BF16), ps("psC", [P, NH])
                z_ready, built, used, counted = sem("z_ready"), sem("built"), sem("used"), sem("counted")
                CB = 4
                assert CB * (NB2 // 2 - 1) == NB1
                staged, spread, args, exps, states, stored, chain = (sem(n) for n in ("staged", "spread", "args", "exps", "states", "stored", "chain"))
                with nc.Block() as block:
                    @block.gpsimd
                    def _(pool):
                        pool.indirect_dma_start(out=hd[:, :], out_offset=None, in_=h_tab,
                                                in_offset=bass.IndirectOffsetOnAxis(ap=dst2[:, 0:1], axis=0)).then_inc(first_in, 16)

                        def body(i):
                            for s in range(2):
                                if not zero(i):
                                    hold(pool, spread, 2 * i + s - 1)
                                cols = bass.ds((2 * i + s) * J2, J2)
                                nc.gpsimd.tensor_copy(iS[:, s, :], src2[:, cols]).then_inc(staged, 1)
                                hold(pool, staged, 2 * i + s + 1)
                                for j in range(J2):
                                    pool.indirect_dma_start(out=hs[:, s, j, :], out_offset=None, in_=h_tab,
                                                            in_offset=bass.IndirectOffsetOnAxis(ap=iS[:, s, j:j + 1], axis=0)).then_inc(got[s], 16)
                        loop(pool, NB2 // 2, body)

                    @block.vector
                    def _(dve):
                        c = Count(dve, chain)
                        dve.wait_ge(first_in, 16)
                        dve.wait_ge(adst_in, 16)
                        c.seq(v.tensor_copy(adst[:, 0, :], hd[:, F + H:W]))
                        for h in range(H):
                            c.inc(v.tensor_tensor_scan(score[:, h, :], keep2[:, :], adst[:, :, h], 0.0, ALU.mult, ALU.add))
                        c.wait()
                        v.memset(zerob[:, :], 0.0).then_inc(z_ready, 1)

                        def body(i):
                            for s in range(2):
                                cols = bass.ds((2 * i + s) * J2, J2)
                                hold(dve, got[s], 16 * J2 * (i + 1))
                                v.tensor_copy(feat[:, :, cols], hs[:, s, :, 0:F].rearrange("p j f -> p f j"))
                                v.tensor_tensor(score[:, :, cols], hs[:, s, :, F:F + H].rearrange("p j f -> p f j"),
                                                score[:, :, cols], ALU.add).then_inc(spread, 1)
                            for q in range(0 if zero(i) else CB):
                                b = CB * i + q - CB
                                cols = bass.ds(b * J1, J1)
                                hold(dve, used, b + 1)
                                v.tensor_tensor(onelo[:, q % 2, :, :], iota_free[:, :].unsqueeze(1).broadcast_to([P, J1, P]),
                                                lo[:, cols].unsqueeze(2).broadcast_to([P, J1, P]), ALU.is_equal)
                                v.tensor_tensor(onehi[:, q % 2, :, :], iota_free[:, 0:NH].unsqueeze(1).broadcast_to([P, J1, NH]),
                                                hi[:, cols].unsqueeze(2).broadcast_to([P, J1, NH]), ALU.is_equal).then_inc(built, 1)
                        loop(dve, NB2 // 2, body)
                        dve.wait_ge(spread, NB2)
                        c.seq(v.scalar_tensor_tensor(score[:, :, :], score[:, :, :], 0.2, score[:, :, :], ALU.mult, ALU.max))
                        c.seq(v.memset(M[:, :, 0:1], -BIG))
                        for h in range(H):
                            c.inc(v.tensor_tensor_scan(M[:, h, 1:NJ2 + 1], pen2[:, :], score[:, h, :], -BIG, ALU.add, ALU.max))
                        c.wait()
                        c.inc(v.tensor_tensor(AE[:, 0, :, :], M[:, :, 0:NJ2], pen2[:, :].unsqueeze(1).broadcast_to([P, H, NJ2]), ALU.add))
                        c.seq(v.tensor_tensor(AE[:, 1, :, :], score[:, :, :], M[:, :, 1:NJ2 + 1], ALU.subtract))
                        c.seq(v.tensor_tensor(AE[:, 0, :, :], AE[:, 0, :, :], M[:, :, 1:NJ2 + 1], ALU.subtract))
                        dve.sem_inc(args, 1)
                        c.inc(v.tensor_copy(ST[:, :, 0:H], M[:, :, 1:NJ2 + 1].rearrange("p h j -> p j h")))
                        dve.wait_ge(exps, 1)
                        for h in range(H):
                            c.inc(v.tensor_tensor(feat[:, 4 * h:4 * h + 4, :], feat[:, 4 * h:4 * h + 4, :],
                                                  AE[:, 1, h, :].unsqueeze(1).broadcast_to([P, 4, NJ2]), ALU.mult))
                            c.inc(v.tensor_tensor_scan(ST[:, :, H + h], AE[:, 0, h, :], AE[:, 1, h, :], 0.0, ALU.mult, ALU.add))
                        c.wait()
                        for f in range(F):
                            c.inc(v.tensor_tensor_scan(ST[:, :, 2 * H + f], AE[:, 0, f // 4, :], feat[:, f, :], 0.0, ALU.mult, ALU.add))
                        c.wait()
                        c.seq(v.tensor_copy(tails[:, :], ST[:, NJ2 - 1, :]))
                        dve.sem_inc(states, 1)
                        dve.wait_ge(counted, 1)
                        c.seq(v.tensor_copy(counts[:, :], psC[:, :]))

                    @block.tensor
                    def _(pe):
                        def up(n):
                            e, g = n // NG, n % NG
                            if g == 0:
                                pe.wait_ge(w_in[e % 2], 32 * (e // 2 + 1))
                            for f in range(FC0):
                                if n or f >= 2:
                                    pe.wait_ge(acted, n * FC0 + f - 1)
                                for hf in range(2):
                                    for k in range(2):
                                        ins = nc.tensor.matmul(psH[f % 2][:, hf, 0:HN], W1s[:, e % 2, k, f * P:(f + 1) * P],
                                                               XNT[:, g, k, hf * HN:(hf + 1) * HN], start=(k == 0), stop=(k == 1))
                                ins.then_inc(hidden, 1)

                        def down(n):
                            e = n // NG
                            pe.wait_ge(acted, (n + 1) * FC0)
                            for t in range(GT):
                                if n or t >= 3:
                                    pe.wait_ge(rows_read, n * GT + t - 2)
                                for f in range(FC0):
                                    ins = nc.tensor.matmul(psY[:, (n * GT + t) % 3, 0:D], hT[:, n % 2, f, t * P:(t + 1) * P], W2s[:, e % 2, f, :],
                                                           start=(f == 0), stop=(f == FC0 - 1))
                                ins.then_inc(rows_out, 1)
                        def count(b):
                            pe.wait_ge(built, b + 1)
                            for j in range(J1):
                                ins = nc.tensor.matmul(psC[:, :], onelo[:, b % 2, j, :], onehi[:, b % 2, j, :], start=False, stop=False)
                            ins.then_inc(used, 1)
                        pe.sem_inc(used, 2)
                        pe.wait_ge(z_ready, 1)
                        nc.tensor.matmul(psC[:, :], zerob[:, :], zerob[:, 0:NH], start=True, stop=False)
                        up(0)
                        b = 0
                        for n in range(STEPS):
                            if n + 1 < STEPS:
                                up(n + 1)
                            if n >= 3 and b < NB1:
                                count(b)
                                count(b + 1)
                                b += 2
                            down(n)
                        assert b == NB1
                        nc.tensor.matmul(psC[:, :], zerob[:, :], zerob[:, 0:NH], start=False, stop=True).then_inc(counted, 1)

                    @block.scalar
                    def _(act):
                        def gelu(n):
                            if n >= 2:
                                act.wait_ge(rows_out, (n - 1) * GT)
                            for f in range(FC0):
                                act.wait_ge(hidden, n * FC0 + f + 1)
                                a.activation(hT[:, n % 2, f, :].rearrange("p (a c) -> p a c", a=2), psH[f % 2][:, :, 0:HN], ACT.Gelu,
                                             bias=b1T[:, n // NG * FC0 + f:n // NG * FC0 + f + 1]).then_inc(acted, 1)
                        gelu(0)
                        for n in range(STEPS):
                            if n + 1 < STEPS:
                                gelu(n + 1)
                            if n >= 2:
                                act.wait_ge(y_stored[n % 2], 16 * (n // 2))
                            for t in range(GT):
                                act.wait_ge(rows_out, n * GT + t + 1)
                                a.copy(Ye[:, n % 2, t, :], psY[:, (n * GT + t) % 3, 0:D]).then_inc(rows_read, 1)
                            if n == EXP_AT:
                                act.wait_ge(args, 1)
                                flat = AE[:, :, :, :].rearrange("p n h j -> p (n h j)")
                                a.activation(flat, flat, ACT.Exp).then_inc(exps, 1)

                    @block.sync
                    def _(sp):
                        sp.dma_start(adst[:, :, :], adst_tab[0:E2, :].rearrange("(p j) w -> p j w", j=NJ2)).then_inc(adst_in, 16)

                        def load(e):
                            sp.dma_start(W1s[:, e % 2, :, :], f0_w1[e].rearrange("(k p) f -> p k f", p=P)).then_inc(w_in[e % 2], 16)
                            sp.dma_start(W2s[:, e % 2, :, :], f0_w2[e].rearrange("(c p) d -> p c d", p=P)).then_inc(w_in[e % 2], 16)
                        load(0)
                        load(1)
                        for n in range(STEPS):
                            e, g = n // NG, n % NG
                            sp.wait_ge(rows_read, (n + 1) * GT)
                            sp.dma_start(table_rows(ye_tab[e])[:, g * GT:(g + 1) * GT, :], Ye[:, n % 2, :, :]).then_inc(y_stored[n % 2], 16)
                            if g == NG - 1 and e + 2 < E0:
                                load(e + 2)
                        sp.wait_ge(states, 1)
                        sp.dma_start(gat_tab[0:E2, :].rearrange("(p j) w -> p j w", j=NJ2), ST[:, :, :]).then_inc(stored, 16)
                        sp.wait_ge(stored, 16)
                        for s in range(2):
                            sp.wait_ge(y_stored[s], 16 * (STEPS // 2))

        def add_experts_phase(G):
            ctx, sb, ps, sem = phase()
            with ctx:
                Y = sb("Y", [P, E0, NT, D])
                got, chain = [sem(f"got{g}") for g in range(NG)], sem("chain")
                with nc.Block() as block:
                    load_biases, lay_gates, add_biases = second_biases(block, sb, ps, sem, E0, G, f0_b2, X)

                    @block.sync
                    def _(sp):
                        load_biases(sp)
                        for g in range(NG):
                            for e in range(E0):
                                sp.dma_start(Y[:, e, g * GT:(g + 1) * GT, :], table_rows(ye_tab[e])[:, g * GT:(g + 1) * GT, :]).then_inc(got[g], 16)

                    @block.vector
                    def _(dve):
                        c = Count(dve, chain)
                        lay_gates(dve, 0)
                        for g in range(NG):
                            add_biases(dve, g)
                            if g + 1 < NG:
                                lay_gates(dve, g + 1)
                            dve.wait_ge(got[g], 16 * E0)
                            for e in range(E0):
                                for t in range(g * GT, (g + 1) * GT):
                                    c.inc(v.scalar_tensor_tensor(X[:, t, :], Y[:, e, t, :], G[:, e, t:t + 1], X[:, t, :], ALU.mult, ALU.add))
                                c.wait()

        def router_phase(agg, SC):
            F = 16
            ctx, sb, ps, sem = phase()
            with ctx:
                prm = sb("prm", [P, 3, F])
                mu, var, sq = sb("mu", [P, NT]), sb("var", [P, NT]), sb("sq", [P, NT, F])
                prm_in, vars_, rooted, chain = sem("prm_in"), sem("vars"), sem("rooted"), sem("chain")
                with nc.Block() as block:
                    @block.sync
                    def _(sp):
                        for n, dr in enumerate((f0_bgat, f0_lng, f0_lnb)):
                            sp.dma_start(prm[:, n, :], dr.partition_broadcast(P)).then_inc(prm_in, 16)

                    @block.vector
                    def _(dve):
                        c = Count(dve, chain)
                        A = agg[:, :, :]
                        par = lambda n: prm[:, n, :].unsqueeze(1).broadcast_to([P, NT, F])
                        tok = lambda t: t[:, :].unsqueeze(2).broadcast_to([P, NT, F])
                        dve.wait_ge(prm_in, 48)
                        c.seq(v.tensor_tensor(A, A, par(0), ALU.add))
                        c.seq(v.tensor_reduce(mu[:, :], A, AX, ALU.add))
                        c.seq(v.tensor_scalar(mu[:, :], mu[:, :], 1.0 / F, None, ALU.mult))
                        c.seq(v.tensor_tensor(A, A, tok(mu), ALU.subtract))
                        c.seq(v.tensor_tensor(sq[:, :, :], A, A, ALU.mult))
                        c.seq(v.tensor_reduce(var[:, :], sq[:, :, :], AX, ALU.add))
                        dve.sem_inc(vars_, 1)
                        dve.wait_ge(rooted, 1)
                        c.seq(v.reciprocal(var[:, :], var[:, :]))
                        c.seq(v.tensor_tensor(A, A, tok(var), ALU.mult))
                        c.seq(v.tensor_tensor(A, A, par(1), ALU.mult))
                        c.seq(v.tensor_tensor(A, A, par(2), ALU.add))
                        c.seq(v.tensor_reduce(SC[:, :, :], A.rearrange("p t (h e) -> p t e h", h=4), AX, ALU.add))
                        c.seq(v.tensor_scalar(SC[:, :, :], SC[:, :, :], 0.25, None, ALU.mult))

                    @block.scalar
                    def _(act):
                        act.wait_ge(vars_, 1)
                        a.activation(var[:, :], var[:, :], ACT.Sqrt, bias=eps_col[:, :], scale=1.0 / F).then_inc(rooted, 1)

        def gate_phase(SC, E, G, chosen=None, weight=None):
            ctx, sb, ps, sem = phase()
            with ctx:
                t1, mask = sb("t1", [P, NT, E]), [sb("mask0", [P, NT, E]), sb("mask1", [P, NT, E])]
                m, first = sb("m", [P, 2, NT]), sb("first", [P, NT])
                e2, w = sb("e2", [P, NT]), weight if weight is not None else sb("w", [P, 2, NT])
                arg, exped, chain = sem("arg"), sem("exped"), sem("chain")
                with nc.Block() as block:
                    @block.vector
                    def _(dve):
                        c = Count(dve, chain)
                        over = lambda t: t.unsqueeze(2).broadcast_to([P, NT, E])
                        numbers = iota_free[:, 0:E].unsqueeze(1).broadcast_to([P, NT, E])
                        for n in range(2):
                            c.seq(v.tensor_reduce(m[:, n, :], SC[:, :, :], AX, ALU.max))
                            c.seq(v.tensor_tensor(t1[:, :, :], SC[:, :, :], over(m[:, n, :]), ALU.is_equal))
                            c.seq(v.scalar_tensor_tensor(t1[:, :, :], t1[:, :, :], -float(P), numbers, ALU.mult, ALU.add))
                            c.seq(v.tensor_reduce(first[:, :], t1[:, :, :], AX, ALU.min))
                            c.seq(v.tensor_tensor(mask[n][:, :, :], t1[:, :, :], over(first[:, :]), ALU.is_equal))
                            if n == 0:
                                c.seq(v.scalar_tensor_tensor(SC[:, :, :], mask[n][:, :, :], -BIG, SC[:, :, :], ALU.mult, ALU.add))
                        c.seq(v.tensor_tensor(e2[:, :], m[:, 1, :], m[:, 0, :], ALU.subtract))
                        dve.sem_inc(arg, 1)
                        if chosen is not None:
                            for n in range(2):
                                c.inc(v.tensor_copy(chosen[:, n, :, :], mask[n][:, :, :]))
                        dve.wait_ge(exped, 1)
                        c.seq(v.tensor_scalar(w[:, 0, :], e2[:, :], 1.0, None, ALU.add))
                        c.seq(v.reciprocal(w[:, 0, :], w[:, 0, :]))
                        c.seq(v.tensor_tensor(w[:, 1, :], w[:, 0, :], e2[:, :], ALU.mult))
                        for n in range(2):
                            c.seq(v.tensor_tensor(mask[n][:, :, :], mask[n][:, :, :], over(w[:, n, :]), ALU.mult))
                        c.seq(v.tensor_tensor(G[:, :, :].rearrange("p e t -> p t e"), mask[0][:, :, :], mask[1][:, :, :], ALU.add))

                    @block.scalar
                    def _(act):
                        act.wait_ge(arg, 1)
                        a.activation(e2[:, :], e2[:, :], ACT.Exp).then_inc(exped, 1)

        def second_biases(block, sb, ps, sem, E, G, b2, acc, act_last=None):
            b2s, gS, gT = sb("b2s", [E, D]), sb("gS", [P, GT, E]), sb("gT", [E, GT, P])
            psG, psA = ps("psG", [P, 2, 512]), ps("psA", [P, 2, 512])
            b2_in, gs, turned, gts, biased, added = (sem(n) for n in ("b2_in", "gs", "turned", "gts", "biased", "added"))

            @block.tensor
            def _(pe):
                pe.wait_ge(b2_in, 16)

                def body(g):
                    for s in range(GT):
                        hold(pe, gs, g + 1)
                        if not zero(g) or s >= 2:
                            hold(pe, gts, g * GT + max(s - 1, 0))
                        nc.tensor.transpose(psG[0:E, s % 2, 0:P], gS[:, s, :], ident[:, :]).then_inc(turned, 1)
                    for s in range(GT):
                        hold(pe, gts, g * GT + s + 1)
                        if not zero(g) or s >= 2:
                            hold(pe, added, g * GT + max(s - 1, 0))
                        nc.tensor.matmul(psA[:, s % 2, 0:D], gT[:, s, :], b2s[:, :], start=True, stop=True).then_inc(biased, 1)
                loop(pe, NG, body)

            @block.scalar
            def _(act):
                def body(g):
                    for s in range(GT):
                        hold(act, turned, g * GT + s + 1)
                        if not zero(g):
                            hold(act, biased, g * GT)
                        a.copy(gT[:, s, :], psG[0:E, s % 2, 0:P]).then_inc(gts, 1)
                loop(act, NG, body)
                if act_last is not None:
                    act_last(act)

            def load(sp):
                sp.dma_start(b2s[:, :], b2).then_inc(b2_in, 16)

            def lay_gates(dve, g):
                if g:
                    dve.wait_ge(turned, g * GT)
                v.tensor_copy(gS[:, :, :], G[:, :, g * GT:(g + 1) * GT].rearrange("p e t -> p t e")).then_inc(gs, 1)

            def add_biases(dve, g):
                for t in range(g * GT, (g + 1) * GT):
                    dve.wait_ge(biased, t + 1)
                    v.tensor_tensor(acc[:, t, :], psA[:, t % GT % 2, 0:D], acc[:, t, :], ALU.add).then_inc(added, 1)
                dve.wait_ge(added, (g + 1) * GT)
            return load, lay_gates, add_biases

        E3, FF3 = f1_w1.shape[0], f1_w1.shape[2]
        FC3 = FF3 // P
        MAX_BLOCKS = (2 * N + E3 * (P - 1)) // P
        SLOTS = 4
        assert MAX_BLOCKS % SLOTS == 0
        disp_tab = sum_tab
        y_tab = dram("y_tab", [MAX_BLOCKS * P, D])

        def load_experts_phase(W1r, W2r):
            ctx, sb, ps, sem = phase()
            with ctx:
                with nc.Block() as block:
                    @block.scalar
                    def _(act):
                        for k in range(2):
                            act.dma_start(W1r[:, k, :, :], f1_w1[:, k * P:(k + 1) * P, :].rearrange("e p f -> p e f")).then_inc(weights_in, 16)
                        for f in range(FC3):
                            act.dma_start(W2r[:, f, :, :], f1_w2[:, f * P:(f + 1) * P, :].rearrange("e p d -> p e d")).then_inc(weights_in, 16)

        def dispatch_phase(chosen, XNR, pos_out, block_expert, b1T):
            E = E3
            ctx, sb, ps, sem = phase()
            with ctx:
                both, tot, cum, S = (sb(n, [P, E, NT]) for n in ("both", "tot", "cum", "S"))
                psI, psTot = ps("psI", [P, 512]), ps("psTot", [P, 512])
                valid, pad_row, k128 = sb("valid", [P, 1]), sb("pad_row", [P, 2]), sb("k128", [P, NT])
                cnt, blocks, last, off = (sb(n, [P, E]) for n in ("cnt", "blocks", "last", "off"))
                pf, pos, pick = sb("pf", [P, 2, NT]), sb("pos", [P, 2, NT], I32), sb("pick", [P, NT, E])
                passed, bf = sb("passed", [P, MAX_BLOCKS + 2, E]), sb("bf", [P, MAX_BLOCKS + 2])
                chain, marked, summed, placed, moved = (sem(n) for n in ("chain", "marked", "summed", "placed", "moved"))
                flat = lambda t: t.rearrange("p e t -> p (e t)")
                over_t = lambda t: t.unsqueeze(2).broadcast_to([P, E, NT])
                b1r, psB = sb("b1r", [E * FC3, P]), ps("psB", [P, 512])
                b1_in, b1_turned, b1_out = sem("b1_in"), sem("b1_turned"), sem("b1_out")
                with nc.Block() as block:
                    @block.sync
                    def _(sp):
                        sp.dma_start(b1r[:, :], f1_b1.rearrange("e (c p) -> (e c) p", p=P)).then_inc(b1_in, 16)

                    @block.scalar
                    def _(act):
                        act.wait_ge(b1_turned, 1)
                        a.copy(b1T[:, :], psB[:, 0:E * FC3]).then_inc(b1_out, 1)

                    @block.tensor
                    def _(pe):
                        pe.wait_ge(marked, 1)
                        nc.tensor.matmul(psI[:, 0:E * NT], upper[:, :], flat(both[:, :, :]), start=True, stop=True)
                        nc.tensor.matmul(psTot[:, 0:E * NT], ones[:, :], flat(both[:, :, :]), start=True, stop=True).then_inc(summed, 1)
                        pe.wait_ge(b1_in, 16)
                        nc.tensor.transpose(psB[:, 0:E * FC3], b1r[:, :], ident[0:E * FC3, 0:E * FC3]).then_inc(b1_turned, 1)

                    @block.vector
                    def _(dve):
                        c = Count(dve, chain)
                        c.seq(v.tensor_scalar(valid[:, :], iota_part[:, :], float(TAIL_ROWS), None, ALU.is_lt))
                        for n in range(2):
                            c.inc(v.tensor_scalar(chosen[:, n, NT - 1, :], chosen[:, n, NT - 1, :], valid[:, 0:1], None, ALU.mult))
                        for n in range(2):
                            c.inc(v.tensor_scalar(pad_row[:, n:n + 1], iota_part[:, :], float((MAX_BLOCKS + n) * P + 1), None, ALU.add))
                        c.inc(v.tensor_scalar(k128[:, :], iota_free[:, 0:NT], float(P), None, ALU.mult))
                        c.wait()
                        c.inc(v.tensor_scalar(valid[:, :], valid[:, :], 0.5, None, ALU.is_lt))
                        c.seq(v.tensor_tensor(both[:, :, :].rearrange("p e t -> p t e"), chosen[:, 0, :, :], chosen[:, 1, :, :], ALU.add))
                        dve.sem_inc(marked, 1)
                        c.inc(v.tensor_scalar(pad_row[:, :], pad_row[:, :], valid[:, 0:1], None, ALU.mult))
                        dve.wait_ge(summed, 1)
                        c.seq(v.tensor_copy(flat(tot[:, :, :]), psTot[:, 0:E * NT]))
                        c.inc(v.tensor_tensor_scan(flat(cum[:, :, :]), flat(tot[:, :, :]), flat(tot[:, :, :]), 0.0, ALU.add, ALU.max))
                        c.seq(v.tensor_reduce(cnt[:, :], tot[:, :, :], AX, ALU.add))
                        c.seq(v.tensor_tensor(S[:, :, :], over_t(cnt[:, :]), k128[:, :].unsqueeze(1).broadcast_to([P, E, NT]), ALU.is_gt))
                        c.seq(v.tensor_reduce(blocks[:, :], S[:, :, :], AX, ALU.add))
                        c.seq(v.tensor_tensor_scan(last[:, :], blocks[:, :], blocks[:, :], 0.0, ALU.add, ALU.max))
                        c.seq(v.tensor_tensor(off[:, :], last[:, :], blocks[:, :], ALU.subtract))
                        c.seq(v.scalar_tensor_tensor(off[:, :], off[:, :], float(P), cnt[:, :], ALU.mult, ALU.add))
                        c.seq(v.tensor_tensor(off[:, :], off[:, :], cum[:, :, NT - 1], ALU.subtract))
                        c.inc(v.tensor_tensor(tot[:, :, :], cum[:, :, :], tot[:, :, :], ALU.subtract))
                        c.seq(v.tensor_tensor(S[:, :, :], over_t(off[:, :]), psI[:, 0:E * NT].rearrange("p (e t) -> p e t", t=NT), ALU.add))
                        c.seq(v.tensor_tensor(S[:, :, :], S[:, :, :], tot[:, :, :], ALU.add))
                        for n in range(2):
                            c.seq(v.tensor_tensor(pick[:, :, :], S[:, :, :].rearrange("p e t -> p t e"), chosen[:, n, :, :], ALU.mult))
                            c.seq(v.tensor_reduce(pf[:, n, :], pick[:, :, :], AX, ALU.add))
                            c.seq(v.tensor_tensor(pf[:, n, NT - 1:NT], pf[:, n, NT - 1:NT], pad_row[:, n:n + 1], ALU.add))
                        c.seq(v.tensor_scalar(pf[:, :, :], pf[:, :, :], -1.0, 0.0, ALU.add, ALU.max))
                        c.seq(v.tensor_copy(pos[:, :, :], pf[:, :, :]))
                        dve.sem_inc(placed, 1)
                        c.seq(v.tensor_scalar(pf[:, :, :], pf[:, :, :], float(MAX_BLOCKS * P - 1), None, ALU.min))
                        c.inc(v.tensor_copy(pos_out[:, :, :], pf[:, :, :]))
                        KB = MAX_BLOCKS + 2
                        c.seq(v.tensor_tensor(passed[:, :, :], iota_free[:, 0:KB].unsqueeze(2).broadcast_to([P, KB, E]),
                                              last[:, :].unsqueeze(1).broadcast_to([P, KB, E]), ALU.is_ge))
                        c.seq(v.tensor_reduce(bf[:, :], passed[:, :, :], AX, ALU.add))
                        c.seq(v.tensor_scalar(bf[:, :], bf[:, :], float(E - 1), None, ALU.min))
                        c.seq(v.tensor_copy(block_expert[:, :], bf[:, :]))

                    @block.gpsimd
                    def _(pool):
                        pool.wait_ge(placed, 1)
                        for t in range(NT):
                            for n in range(2):
                                pool.indirect_dma_start(out=disp_tab, out_offset=bass.IndirectOffsetOnAxis(ap=pos[:, n, t:t + 1], axis=0),
                                                        in_=XNR[:, t, :], in_offset=None).then_inc(moved, 16)
                        pool.wait_ge(moved, 16 * 2 * NT)

        def sparse_experts_phase(block_expert, W1r, W2r, b1T):
            KB, S = MAX_BLOCKS, SLOTS
            PASSES = KB // S
            ctx, sb, ps, sem = phase()
            with ctx:
                xb, xT, w1c = sb("xb", [P, S, D]), sb("xT", [P, 2, 2, P]), sb("w1c", [P, 2, 2, FF3])
                hT, yb = sb("hT", [P, 2, FC3, P]), sb("yb", [P, S, D])
                psX, psH, psY = ps("psX", [P, 2, 512]), ps("psH", [P, 2, 512]), ps("psY", [P, 2, 512])
                bet, beta_in, shifted = sb("bet", [P, D]), sem("beta_in"), sem("shifted")
                x_in, y_out = [sem(f"x_in{s}") for s in range(S)], [sem(f"y_out{s}") for s in range(S)]
                turned, columns, w1_copied, hidden, acted, rows_out, rows_read = (
                    sem(n) for n in ("turned", "columns", "w1_copied", "hidden", "acted", "rows_out", "rows_read"))
                disp_rows = disp_tab[0:(KB + S) * P, :].rearrange("(k p) d -> p k d", p=P)
                y_rows = table_rows(y_tab)

                def after(eng, sem_, value):
                    if not isinstance(value, int) or value > 0:
                        hold(eng, sem_, value)

                with nc.Block() as block:
                    @block.gpsimd
                    def _(pool):
                        pool.wait_ge(beta_in, 16)
                        nc.gpsimd.tensor_tensor(X[:, :, :], X[:, :, :], bet[:, :].unsqueeze(1).broadcast_to([P, NT, D]), ALU.add).then_inc(shifted, 1)

                    @block.sync
                    def _(sp):
                        sp.dma_start(bet[:, :], f1_beta.partition_broadcast(P)).then_inc(beta_in, 16)
                        def load(k, s):
                            sp.dma_start(xb[:, s, :], disp_rows[:, bass.ds(k, 1), :].rearrange("p a d -> p (a d)")).then_inc(x_in[s], 16)
                        for s in range(S):
                            load(s, s)
                        with sp.Fori(0, PASSES) as i:
                            for s in range(S):
                                sp.wait_ge(turned, S * i + s + 1)
                                load(S * i + s + S, s)
                                sp.wait_ge(rows_read, S * i + s + 1)
                                sp.dma_start(y_rows[:, bass.ds(S * i + s, 1), :].rearrange("p a d -> p (a d)"), yb[:, s, :]).then_inc(y_out[s], 16)
                        for s in range(S):
                            sp.wait_ge(y_out[s], 16 * PASSES)
                            sp.wait_ge(x_in[s], 16 * (PASSES + 1))

                    @block.tensor
                    def _(pe):
                        def turn(k, s, i):
                            hold(pe, x_in[s], 16 * (i + 1))
                            after(pe, columns, k - 1)
                            nc.tensor.transpose(psX[:, s % 2, 0:P], xb[:, s, 0:P], ident[:, :])
                            nc.tensor.transpose(psX[:, s % 2, P:D], xb[:, s, P:D], ident[:, :]).then_inc(turned, 1)

                        def up(k, s):
                            hold(pe, columns, k + 1)
                            hold(pe, w1_copied, k + 1)
                            after(pe, acted, k - 1)
                            for f in range(FC3):
                                for c in range(2):
                                    ins = nc.tensor.matmul(psH[:, s % 2, f * P:(f + 1) * P], w1c[:, s % 2, c, f * P:(f + 1) * P],
                                                           xT[:, s % 2, c, :], start=(c == 0), stop=(c == 1))
                            ins.then_inc(hidden, 1)

                        def down(k, s):
                            e = pe.value_load(block_expert[0:1, bass.ds(k, 1)], min_val=0, max_val=E3 - 1)
                            hold(pe, acted, k + 1)
                            after(pe, rows_read, k - 1)
                            for f in range(FC3):
                                ins = nc.tensor.matmul(psY[:, s % 2, 0:D], hT[:, s % 2, f, :], W2r[:, f, bass.ds(e, 1), :].rearrange("p a d -> p (a d)"),
                                                       start=(f == 0), stop=(f == FC3 - 1))
                            ins.then_inc(rows_out, 1)
                        turn(0, 0, 0)
                        turn(1, 1, 0)
                        pe.wait_ge(weights_in, 16 * (2 + FC3))
                        up(0, 0)

                        def body(i):
                            for s in range(S):
                                k = S * i + s
                                up(k + 1, (s + 1) % S)
                                turn(k + 2, (s + 2) % S, i if s + 2 < S else i + 1)
                                down(k, s)
                        loop(pe, PASSES, body)

                    @block.scalar
                    def _(act):
                        def relu(k, s):
                            e = act.value_load(block_expert[0:1, bass.ds(k, 1)], min_val=0, max_val=E3 - 1)
                            hold(act, hidden, k + 1)
                            after(act, rows_out, k - 1)
                            for f in range(FC3):
                                ins = a.activation(hT[:, s % 2, f, :], psH[:, s % 2, f * P:(f + 1) * P], ACT.Relu, bias=b1T[:, bass.ds(e * FC3 + f, 1)])
                            ins.then_inc(acted, 1)
                        relu(0, 0)

                        def body(i):
                            for s in range(S):
                                relu(S * i + s + 1, (s + 1) % S)
                        loop(act, PASSES, body)

                    @block.vector
                    def _(dve):
                        def first_weights(k, s):
                            e = dve.value_load(block_expert[0:1, bass.ds(k, 1)], min_val=0, max_val=E3 - 1)
                            after(dve, hidden, k - 1)
                            v.tensor_copy(w1c[:, s % 2, :, :], W1r[:, :, bass.ds(e, 1), :].rearrange("p c a f -> p c (a f)")).then_inc(w1_copied, 1)

                        def spread(k, s):
                            hold(dve, turned, k + 1)
                            after(dve, hidden, k - 1)
                            v.tensor_copy(xT[:, s % 2, :, :].rearrange("p c t -> p (c t)"), psX[:, s % 2, 0:D]).then_inc(columns, 1)
                        dve.wait_ge(weights_in, 16 * (2 + FC3))
                        for k in range(2):
                            spread(k, k)
                            first_weights(k, k)

                        def body(i):
                            for s in range(S):
                                k = S * i + s
                                first_weights(k + 2, (s + 2) % S)
                                spread(k + 2, (s + 2) % S)
                                hold(dve, rows_out, k + 1)
                                if not zero(i):
                                    hold(dve, y_out[s], 16 * i)
                                v.tensor_copy(yb[:, s, :], psY[:, s % 2, 0:D]).then_inc(rows_read, 1)
                        loop(dve, PASSES, body)

        def combine_phase(pos, weight, G, Y):
            ctx, sb, ps, sem = phase()
            with ctx:
                chosen_y = sb("chosen_y", [P, 2, NT, D])
                st, mv, sd, rs = sb("st", [P, NT, 6]), sb("mv", [P, NT, 2]), sb("sd", [P, NT]), sb("rs", [P, NT])
                gam = sb("gam", [P, D])
                rows_in, p_in, stats, rooted, summed, out_stored, chain = (
                    sem(n) for n in ("rows_in", "p_in", "stats", "rooted", "summed", "out_stored", "chain"))
                got = [sem(f"got{g}") for g in range(NG)]

                def roots(act):
                    act.wait_ge(stats, 1)
                    a.activation(sd[:, :], mv[:, :, 1], ACT.Sqrt, bias=eps_col[:, :]).then_inc(rooted, 1)

                with nc.Block() as block:
                    load_biases, lay_gates, add_biases = second_biases(block, sb, ps, sem, E3, G, f1_b2, Y, roots)

                    @block.sync
                    def _(sp):
                        load_biases(sp)
                        sp.dma_start(Y[:, :, :], table_rows(xn_tab)).then_inc(rows_in, 16)
                        sp.dma_start(gam[:, :], f1_gamma.partition_broadcast(P)).then_inc(p_in, 16)
                        for g in range(NG):
                            sp.wait_ge(summed, g + 1)
                            t0, t1 = g * GT, min((g + 1) * GT, NT - 1)
                            sp.dma_start(table_rows(out[t0 * P:t1 * P, :]), X[:, t0:t1, :]).then_inc(out_stored, 16)
                        sp.dma_start(out[(NT - 1) * P:N, :], X[0:TAIL_ROWS, NT - 1, :]).then_inc(out_stored, 16)
                        sp.wait_ge(out_stored, 16 * (NG + 1))

                    @block.gpsimd
                    def _(pool):
                        for t in range(NT):
                            for n in range(2):
                                pool.indirect_dma_start(out=chosen_y[:, n, t, :], out_offset=None, in_=y_tab,
                                                        in_offset=bass.IndirectOffsetOnAxis(ap=pos[:, n, t:t + 1], axis=0)).then_inc(got[t // GT], 16)

                    @block.vector
                    def _(dve):
                        c = Count(dve, chain)
                        dve.wait_ge(rows_in, 16)
                        lay_gates(dve, 0)
                        for g in range(NG):
                            add_biases(dve, g)
                            if g + 1 < NG:
                                lay_gates(dve, g + 1)
                            dve.wait_ge(got[g], 16 * 2 * GT)
                            tiles = range(g * GT, (g + 1) * GT)
                            for n in range(2):
                                for t in tiles:
                                    c.inc(v.scalar_tensor_tensor(Y[:, t, :], chosen_y[:, n, t, :], weight[:, n, t:t + 1], Y[:, t, :], ALU.mult, ALU.add))
                                c.wait()
                            for t in tiles:
                                c.inc(v.bn_stats(st[:, t, :], Y[:, t, :]))
                            c.wait()
                            for t in tiles:
                                c.inc(v.bn_aggr(mv[:, t, :], st[:, t, :]))
                        c.wait()
                        dve.sem_inc(stats, 1)
                        dve.wait_ge(p_in, 16)
                        dve.wait_ge(rooted, 1)
                        c.seq(v.reciprocal(rs[:, :], sd[:, :]))
                        for g in range(NG):
                            tiles = slice(g * GT, (g + 1) * GT)
                            for t in range(g * GT, (g + 1) * GT):
                                c.inc(v.tensor_scalar(Y[:, t, :], Y[:, t, :], mv[:, t, 0:1], rs[:, t:t + 1], ALU.subtract, ALU.mult))
                            c.wait()
                            c.seq(v.tensor_tensor(Y[:, tiles, :], Y[:, tiles, :], gam[:, :].unsqueeze(1).broadcast_to([P, GT, D]), ALU.mult))
                            c.seq(v.tensor_tensor(X[:, tiles, :], X[:, tiles, :], Y[:, tiles, :], ALU.add))
                            dve.sem_inc(summed, 1)

        def attention_phase(tails):
            H, DH = 8, 32
            W = 2 * H + D
            SCALE = DH ** -0.5
            ctx, sb, ps, sem = phase()
            with ctx:
                Q, KV = sb("Q", [P, 2, J1, D]), sb("KV", [P, 2, J1, 2 * D])
                ST, q0 = sb("ST", [P, 2, J1, W]), sb("q0", [P, D])
                S, pen, M = sb("S", [P, 2, H, J1 + 1]), sb("pen", [P, 2, H, J1 + 1]), sb("M", [P, 2, H, J1 + 1])
                AE, L = sb("AE", [P, 2, 2, H, J1 + 1]), sb("L", [P, 2, H, J1 + 1])
                VT, decay = sb("VT", [P, H, DH, J1 + 1]), sb("decay", [P, H, DH, J1 + 1])
                same = sb("same", [P, 2, J1])
                new, newS = sb("new", [P, NJ1]), sb("newS", [P, 2, J1])
                iS = sb("iS", [P, 2, J1], I32)
                got, stored, q_in = ([sem(f"{n}{s}") for s in range(2)] for n in ("got", "stored", "q_in"))
                first_in, flagged, staged, masked, filled, q_free, args, exps, chain = (
                    sem(n) for n in ("first_in", "flagged", "staged", "masked", "filled", "q_free", "args", "exps", "chain"))
                weighed, carried = sem("weighed"), sem("carried")
                decays, summed, states, sums_out = sem("decays"), sem("summed"), sem("states"), sem("sums_out")
                PASSES = NB1 // 2

                def passes(eng, body):
                    body(0, False)
                    with eng.Fori(1, PASSES - 1) as i:
                        body(i, False)
                    body(PASSES - 1, True)

                with nc.Block() as block:
                    @block.gpsimd
                    def _(pool):
                        pool.indirect_dma_start(out=q0[:, :], out_offset=None, in_=q_tab,
                                                in_offset=bass.IndirectOffsetOnAxis(ap=dst1[:, 0:1], axis=0)).then_inc(first_in, 16)
                        pool.wait_ge(flagged, 1)

                        def gather(b, s):
                            cols = bass.ds(b * J1, J1)
                            nc.gpsimd.tensor_copy(newS[:, s, :], new[:, cols])
                            nc.gpsimd.tensor_copy(same[:, s, :], keep1[:, cols])
                            nc.gpsimd.tensor_copy(iS[:, s, :], src1[:, cols]).then_inc(staged, 1)
                            hold(pool, staged, b + 1)
                            for j in range(J1):
                                pool.indirect_dma_start(out=KV[:, s, j, :], out_offset=None, in_=kv_tab,
                                                        in_offset=bass.IndirectOffsetOnAxis(ap=iS[:, s, j:j + 1], axis=0)).then_inc(got[s], 16)
                        gather(0, 0)

                        def body(i, last):
                            for s in range(2):
                                b = 2 * i + s
                                if s or not zero(i):
                                    hold(pool, weighed, b)
                                    hold(pool, filled, b)
                                if not (last and s == 1):
                                    gather(b + 1, 1 - s)
                                hold(pool, got[s], 16 * J1 * (i + 1))
                                hold(pool, exps, b + 1)
                                if s or not zero(i):
                                    hold(pool, sums_out, b)
                                    hold(pool, carried, b)
                                nc.gpsimd.tensor_tensor(VT[:, :, :, 1:J1 + 1].rearrange("p h c j -> p j h c"),
                                                        KV[:, s, :, D:2 * D].rearrange("p j (h c) -> p j h c", c=DH),
                                                        AE[:, s, 1, :, 1:J1 + 1].rearrange("p h j -> p j h").unsqueeze(3).broadcast_to([P, J1, H, DH]),
                                                        ALU.mult).then_inc(weighed, 1)
                        passes(pool, body)

                    @block.vector
                    def _(dve):
                        c = Count(dve, chain)
                        for s in range(2):
                            c.inc(v.memset(pen[:, s, :, 0:1], -BIG))
                            c.inc(v.memset(AE[:, s, 0, :, 0:1], 0.0))
                        c.inc(v.memset(M[:, 1, :, :], -BIG))
                        c.inc(v.memset(L[:, 1, :, :], 0.0))
                        c.inc(v.memset(VT[:, :, :, 0], 0.0))
                        c.inc(v.memset(decay[:, :, :, 0], 0.0))
                        c.seq(v.memset(keep1[:, 0:1], 1.0))
                        c.seq(v.tensor_scalar(new[:, :], keep1[:, :], -SCALE, SCALE, ALU.mult, ALU.add))
                        dve.wait_ge(first_in, 16)
                        c.seq(v.tensor_scalar(q0[:, :], q0[:, :], SCALE, None, ALU.mult))
                        dve.sem_inc(flagged, 1)
                        flat = lambda t: t.rearrange("p h j -> p (h j)")
                        whole = lambda t: t.rearrange("p h c j -> p (h c j)")

                        def fill(b, s):
                            hold(dve, masked, b + 1)
                            for j in range(J1):
                                prev = q0[:, :] if j == 0 else Q[:, s, j - 1, :]
                                c.seq(v.scalar_tensor_tensor(Q[:, s, j, :], prev, same[:, s, j:j + 1], Q[:, s, j, :], ALU.mult, ALU.add))
                            c.seq(v.tensor_copy(q0[:, :], Q[:, s, J1 - 1, :]))
                            dve.sem_inc(filled, 1)
                        fill(0, 0)

                        def body(i, last):
                            c.at(i, 2 * (15 + J1))
                            for s in range(2):
                                b, o = 2 * i + s, 1 - s
                                cols = bass.ds(b * J1, J1)
                                c.inc(v.tensor_copy(pen[:, s, :, 1:J1 + 1], pen1[:, cols].unsqueeze(1).broadcast_to([P, H, J1])))
                                c.inc(v.tensor_copy(S[:, s, :, 0], M[:, o, :, J1]))
                                hold(dve, got[s], 16 * J1 * (i + 1))
                                c.seq(v.tensor_tensor(KV[:, s, :, 0:D], Q[:, s, :, :], KV[:, s, :, 0:D], ALU.mult))
                                dve.sem_inc(q_free, 1)
                                c.seq(v.tensor_reduce(S[:, s, :, 1:J1 + 1].rearrange("p h j -> p j h"),
                                                      KV[:, s, :, 0:D].rearrange("p j (h c) -> p j h c", c=DH), AX, ALU.add))
                                c.seq(v.tensor_tensor_scan(flat(M[:, s, :, :]), flat(pen[:, s, :, :]), flat(S[:, s, :, :]), -BIG, ALU.add, ALU.max))
                                c.inc(v.tensor_tensor(AE[:, s, 0, :, 1:J1 + 1], M[:, s, :, 0:J1], pen[:, s, :, 1:J1 + 1], ALU.add))
                                c.seq(v.tensor_tensor(AE[:, s, 1, :, 1:J1 + 1], S[:, s, :, 1:J1 + 1], M[:, s, :, 1:J1 + 1], ALU.subtract))
                                c.seq(v.tensor_tensor(AE[:, s, 0, :, 1:J1 + 1], AE[:, s, 0, :, 1:J1 + 1], M[:, s, :, 1:J1 + 1], ALU.subtract))
                                dve.sem_inc(args, 1)
                                if not zero(i):
                                    hold(dve, stored[s], 16 * i)
                                c.inc(v.tensor_copy(ST[:, s, :, 0:H], M[:, s, :, 1:J1 + 1].rearrange("p h j -> p j h")))
                                c.inc(v.tensor_copy(AE[:, s, 1, :, 0], L[:, o, :, J1]))
                                if not (last and s == 1):
                                    fill(b + 1, o)
                                else:
                                    c.wait()
                                hold(dve, exps, b + 1)
                                c.seq(v.tensor_tensor_scan(flat(L[:, s, :, :]), flat(AE[:, s, 0, :, :]), flat(AE[:, s, 1, :, :]), 0.0, ALU.mult, ALU.add))
                                c.seq(v.tensor_copy(ST[:, s, :, H:2 * H], L[:, s, :, 1:J1 + 1].rearrange("p h j -> p j h")))
                                dve.sem_inc(states, 1)
                                hold(dve, decays, b + 1)
                                hold(dve, weighed, b + 1)
                                c.seq(v.tensor_tensor_scan(whole(VT[:, :, :, :]), whole(decay[:, :, :, :]), whole(VT[:, :, :, :]), 0.0, ALU.mult, ALU.add))
                                dve.sem_inc(summed, 1)
                                c.seq(v.tensor_copy(VT[:, :, :, 0], VT[:, :, :, J1]))
                                dve.sem_inc(carried, 1)
                        passes(dve, body)
                        c.inc(v.tensor_copy(tails[:, 0:2 * H], ST[:, 1, J1 - 1, 0:2 * H]))
                        c.seq(v.tensor_copy(tails[:, 2 * H:W].rearrange("p (h c) -> p h c", c=DH), VT[:, :, :, J1]))

                    @block.scalar
                    def _(act):
                        def mask(b, s, i):
                            hold(act, staged, b + 1)
                            hold(act, q_in[s], 16 * (i + 1))
                            for j in range(J1):
                                ins = a.mul(Q[:, s, j, :], Q[:, s, j, :], newS[:, s, j:j + 1])
                            ins.then_inc(masked, 1)
                        mask(0, 0, 0)

                        def body(i, last):
                            for s in range(2):
                                b = 2 * i + s
                                if not (last and s == 1):
                                    mask(b + 1, 1 - s, i + s)
                                hold(act, args, b + 1)
                                e = AE[:, s, :, :, 1:J1 + 1].rearrange("p n h j -> p (n h) j")
                                a.activation(e, e, ACT.Exp).then_inc(exps, 1)
                                hold(act, exps, b + 1)
                                if s or not zero(i):
                                    hold(act, summed, b)
                                a.copy(decay[:, :, :, 1:J1 + 1], AE[:, s, 0, :, 1:J1 + 1].unsqueeze(2).broadcast_to([P, H, DH, J1])).then_inc(decays, 1)
                                if not zero(i):
                                    hold(act, stored[s], 16 * i)
                                hold(act, summed, b + 1)
                                a.copy(ST[:, s, :, 2 * H:W].rearrange("p j (h c) -> p h c j", c=DH), VT[:, :, :, 1:J1 + 1]).then_inc(sums_out, 1)
                        passes(act, body)

                    @block.sync
                    def _(sp):
                        tab = att_tab[0:P * NJ1, :].rearrange("(p j) w -> p j w", j=NJ1)
                        q_runs = sum_tab[0:P * NJ1, :].rearrange("(p j) f -> p j f", j=NJ1)

                        def store(b, s):
                            hold(sp, states, b + 1)
                            hold(sp, sums_out, b + 1)
                            sp.dma_start(tab[:, bass.ds(b * J1, J1), :], ST[:, s, :, :]).then_inc(stored[s], 16)

                        def load(b, s):
                            sp.dma_start(Q[:, s, :, :], q_runs[:, bass.ds(b * J1, J1), :]).then_inc(q_in[s], 16)
                        load(0, 0)
                        load(1, 1)

                        def body(i, last):
                            for s in range(2):
                                b = 2 * i + s
                                if not last:
                                    hold(sp, q_free, b + 1)
                                    load(b + 2, s)
                                store(b, s)
                        passes(sp, body)
                        for s in range(2):
                            sp.wait_ge(stored[s], 16 * PASSES)

        def out_phase(agg):
            H, DH = 8, 32
            ctx, sb, ps, sem = phase()
            with ctx:
                XNR = sb("XNR", [P, NT, D])
                wo, bo = sb("wo", [P, 2, D]), sb("bo", [P, D])
                u, ut = sb("u", [P, GT, D]), sb("ut", [P, 2, GT, P])
                psT, psO = ps("psT", [P, 2, 512]), ps("psO", [P, 2, 512])
                w_in, summed, turned, columns, done, added, chain = (sem(n) for n in ("w_in", "summed", "turned", "columns", "done", "added", "chain"))
                with nc.Block() as block:
                    @block.sync
                    def _(sp):
                        sp.dma_start(wo[:, :, :], g1_wout.rearrange("(k p) n -> p k n", p=P)).then_inc(w_in, 16)
                        sp.dma_start(bo[:, :], g1_bout.partition_broadcast(P)).then_inc(w_in, 16)
                        sp.dma_start(XNR[:, :, :], table_rows(xn_tab)).then_inc(w_in, 16)

                    @block.vector
                    def _(dve):
                        dve.wait_ge(w_in, 48)

                        def body(g):
                            if not zero(g):
                                hold(dve, turned, g * GT)
                            for s in range(GT):
                                t = g * GT + s
                                v.tensor_tensor(u[:, s, :].rearrange("p (c h) -> p c h", h=H), row(agg, t).rearrange("p (h c) -> p c h", h=H),
                                                row(XNR, t).rearrange("p (c h) -> p c h", h=H), ALU.add).then_inc(summed, 1)
                            for s in range(GT):
                                t = g * GT + s
                                v.tensor_tensor(row(X, t), row(X, t), bo[:, :], ALU.add).then_inc(chain, 1)
                            for s in range(GT):
                                t = g * GT + s
                                hold(dve, done, t + 1)
                                hold(dve, chain, t + 1)
                                v.tensor_tensor(row(X, t), row(X, t), psO[:, s % 2, 0:D], ALU.add).then_inc(added, 1)
                        loop(dve, NG, body)

                    @block.tensor
                    def _(pe):
                        pe.wait_ge(w_in, 48)

                        def body(g):
                            for s in range(GT):
                                hold(pe, summed, g * GT + s + 1)
                                if not zero(g) or s >= 2:
                                    hold(pe, columns, g * GT + max(s - 1, 0))
                                nc.tensor.transpose(psT[:, s % 2, 0:P], u[:, s, 0:P], ident[:, :])
                                nc.tensor.transpose(psT[:, s % 2, P:D], u[:, s, P:D], ident[:, :]).then_inc(turned, 1)
                            for s in range(GT):
                                hold(pe, columns, g * GT + s + 1)
                                if not zero(g) or s >= 2:
                                    hold(pe, added, g * GT + max(s - 1, 0))
                                for k in range(2):
                                    ins = nc.tensor.matmul(psO[:, s % 2, 0:D], ut[:, k, s, :], wo[:, k, :], start=(k == 0), stop=(k == 1))
                                ins.then_inc(done, 1)
                        loop(pe, NG, body)

                    @block.scalar
                    def _(act):
                        def body(g):
                            for s in range(GT):
                                hold(act, turned, g * GT + s + 1)
                                if not zero(g):
                                    hold(act, done, g * GT)
                                a.copy(ut[:, :, s, :], psT[:, s % 2, 0:D].rearrange("p (k c) -> p k c", k=2)).then_inc(columns, 1)
                        loop(act, NG, body)

        start_phase()
        g_ctx = ExitStack()
        with g_ctx:
            nbr0 = keep_sb(g_ctx, "nbr0", [P, NJ1], I32)
            keep0 = keep_sb(g_ctx, "keep0", [P, NJ1])
            cont0 = keep_sb(g_ctx, "cont0", [P, 1])
            end0 = keep_sb(g_ctx, "end0", [P, NT], I32)
            w0 = keep_sb(g_ctx, "w0", [P, NJ1])
            sort_phase(E1, NJ1, J1, src, [dst, edge_weight], key_tab[0], by_src_tab, end0, P * NJ1)
            reload_phase(by_src_tab, NJ1, [(1, nbr0), (2, w0)], keep0, None, cont0)
            norm_phase(table=xn_tab)
            gnn0_phase()
        e1_ctx = ExitStack()
        with e1_ctx:
            src1 = keep_sb(e1_ctx, "src1", [P, NJ1], I32)
            dst1 = keep_sb(e1_ctx, "dst1", [P, NJ1], I32)
            keep1 = keep_sb(e1_ctx, "keep1", [P, NJ1])
            pen1 = keep_sb(e1_ctx, "pen1", [P, NJ1])
            cont1 = keep_sb(e1_ctx, "cont1", [P, 1])
            end1 = keep_sb(e1_ctx, "end1", [P, NT], I32)
            first1 = keep_sb(e1_ctx, "first1", [P, NT], I32)
            counts1 = keep_sb(e1_ctx, "counts1", [P, NH])
            f_ctx = ExitStack()
            with f_ctx:
                G0 = keep_sb(f_ctx, "G0", [P, E0, NT])
                src2 = keep_sb(f_ctx, "src2", [P, NJ2], I32)
                dst2 = keep_sb(f_ctx, "dst2", [P, NJ2], I32)
                keep2 = keep_sb(f_ctx, "keep2", [P, NJ2])
                pen2 = keep_sb(f_ctx, "pen2", [P, NJ2])
                cont2 = keep_sb(f_ctx, "cont2", [P, 1])
                end2 = keep_sb(f_ctx, "end2", [P, NT], I32)
                first2 = keep_sb(f_ctx, "first2", [P, NT], I32)
                r_ctx = ExitStack()
                sort_phase(E2, NJ2, J2, f0_edges[1, :], [f0_edges[0, :]], key_tab[1], by_dst_tab, end2, E2, first2)
                reload_phase(by_dst_tab, NJ2, [(0, dst2), (1, src2)], keep2, pen2, cont2)
                with r_ctx:
                    XNT0 = keep_sb(r_ctx, "XNT0", [P, NG, 2, GT * P])
                    b1T0 = keep_sb(r_ctx, "b1T0", [P, E0 * FC0])
                    tails0 = keep_sb(r_ctx, "tails0", [P, 24])
                    HG = keep_sb(r_ctx, "HG", [P, NT, 24])
                    agg0 = keep_sb(r_ctx, "agg0", [P, NT, 16])
                    self_score = keep_sb(r_ctx, "self_score", [P, NT, 4])
                    SC0 = keep_sb(r_ctx, "SC0", [P, NT, 4])
                    lo1, hi1 = keep_sb(r_ctx, "lo1", [P, NJ1]), keep_sb(r_ctx, "hi1", [P, NJ1])
                    graph_phase(lo1, hi1)
                    norm_phase(cols_keep=XNT0, project=(f0_wgat, 16, None, HG))
                    gat_phase(HG, self_score, XNT0, b1T0, tails0, lo1, hi1, counts1)
                    merge_phase(4, 16, tails0[:, :], cont2, end2, gat_tab, agg0, self_score[:, :, :], HG, 1e-16)
                    router_phase(agg0, SC0)
                    gate_phase(SC0, E0, G0)
                add_experts_phase(G0)
            x_ctx = ExitStack()
            with x_ctx:
                first_edge, end_edge = keep_sb(x_ctx, "first_edge", [P, NH]), keep_sb(x_ctx, "end_edge", [P, NH])
                prefix_block(counts1, first_edge, end_edge, end1, P * NJ1, first1)
                tails = keep_sb(x_ctx, "att_tails", [P, 16 + D])
                norm_phase(table=xn_tab, project=(g1_wqkv, 3 * D, g1_bqkv, [(q_tab, 0, D), (kv_tab, D, 2 * D)]),
                           scatter=(sum_tab, first1))
                attention_phase(tails)
                agg1 = keep_sb(x_ctx, "agg1", [P, NT, D])
                merge_phase(8, D, tails[:, :], cont1, end1, att_tab, agg1)
                out_phase(agg1)
        e_ctx = ExitStack()
        with e_ctx:
            G1 = keep_sb(e_ctx, "G1", [P, E3, NT])
            weight1 = keep_sb(e_ctx, "weight1", [P, 2, NT])
            pos1 = keep_sb(e_ctx, "pos1", [P, 2, NT], I32)
            block_expert = keep_sb(e_ctx, "block_expert", [P, MAX_BLOCKS + 2], I32)
            b1T1 = keep_sb(e_ctx, "b1T1", [P, E3 * FC3])
            w_ctx = ExitStack()
            with w_ctx:
                W1r = keep_sb(w_ctx, "W1r", [P, 2, E3, FF3])
                W2r = keep_sb(w_ctx, "W2r", [P, FC3, E3, D])
                r_ctx = ExitStack()
                with r_ctx:
                    XNR = keep_sb(r_ctx, "XNR1", [P, NT, D])
                    SC1 = keep_sb(r_ctx, "SC1", [P, NT, E3])
                    chosen = keep_sb(r_ctx, "chosen", [P, 2, NT, E3])
                    norm_phase(table=xn_tab, rows_keep=XNR, project=(f1_gw, E3, f1_gb, SC1))
                    load_experts_phase(W1r, W2r)
                    gate_phase(SC1, E3, G1, chosen, weight1)
                    dispatch_phase(chosen, XNR, pos1, block_expert, b1T1)
                sparse_experts_phase(block_expert, W1r, W2r, b1T1)
            ACC = keep_sb(e_ctx, "ACC", [P, NT, D])
            combine_phase(pos1, weight1, G1, ACC)


_INS = ['x', 'src', 'dst', 'edge_weight', 'L0_gnn_weight1', 'L0_gnn_weight2', 'L0_gnn_gamma', 'L0_gnn_beta',
        'L0_ffn_W_gat', 'L0_ffn_att_src', 'L0_ffn_att_dst', 'L0_ffn_b_gat', 'L0_ffn_ln_gamma', 'L0_ffn_ln_beta',
        'L0_ffn_W1', 'L0_ffn_b1', 'L0_ffn_W2', 'L0_ffn_b2', 'L0_ffn_edge_index', 'L1_gnn_W_qkv', 'L1_gnn_b_qkv',
        'L1_gnn_W_out', 'L1_gnn_b_out', 'L1_ffn_gate_w', 'L1_ffn_gate_b', 'L1_ffn_w1', 'L1_ffn_b1', 'L1_ffn_w2',
        'L1_ffn_b2', 'L1_ffn_gamma', 'L1_ffn_beta']


def kernel(**inputs):
    import numpy as _np
    import concourse.bacc as _bacc
    from concourse import mybir as _mybir
    from concourse.bass_utils import run_bass_kernel_spmd as _run

    nc = _bacc.Bacc("TRN2", target_bir_lowering=False, num_devices=1)
    arrays, args = {}, []
    for name in _INS:
        arr = _np.ascontiguousarray(inputs[name])
        arrays[f"in_{name}_dram"] = arr
        args.append(nc.dram_tensor(f"in_{name}_dram", arr.shape, _mybir.dt.from_np(arr.dtype), kind="ExternalInput").ap())
    out = nc.dram_tensor("out_0_dram", (N, D), F32, kind="ExternalOutput").ap()
    bass_gnn_moe_kernel(nc, *args, out)
    r = _run(nc, [arrays], core_ids=[0])
    return r.results[0]["out_0_dram"]
```
